# Optimizing a Trainium2 kernel written in Bass

```python
import numpy as np
import jax
import jax.numpy as jnp

def _softmax(x, axis=-1):
    return jax.nn.softmax(x, axis=axis)

def _gelu(x):
    return jax.nn.gelu(x, approximate=True)

def _silu(x):
    return jax.nn.silu(x)

def _sigmoid(x):
    return jax.nn.sigmoid(x)

def _layernorm(x, axis=-1, eps=1e-05):
    m = jnp.mean(x, axis=axis, keepdims=True)
    v = jnp.var(x, axis=axis, keepdims=True)
    return (x - m) / jnp.sqrt(v + eps)

def _scatter_add(tgt, idx, src, axis=0):
    return tgt.at[idx].add(src)

def _segment_sum(src, seg, n):
    return jax.ops.segment_sum(src, seg, n)
kernel_name = 'mk_vit_tower_d1_tok_img512_r4_b1c55b'

def setup_inputs(seed: int=0):
    np.random.seed(seed)
    _w = jnp.asarray

    def _rec_inputs():
        import jax
        import jax.numpy as jnp
        _rk = jax.random.key(seed)
        x = -0.000147625 + 0.999875 * jax.random.normal(jax.random.fold_in(_rk, 1), (64, 3, 224, 224), jnp.float32)
        return x
    x = _rec_inputs()

    def _L0_tok_setup():
        import jax, jax.numpy as jnp
        import numpy as np
        N_PATCHES = 8
        PATCH = 28
        C = 3
        IN_D = C * PATCH * PATCH
        HID = 128
        SEQ = N_PATCHES * N_PATCHES + 1

        def _positional_embedding(seq_len, dim):
            i = np.arange(seq_len)[:, None].astype(np.float32)
            j = np.arange(dim)[None, :].astype(np.float32)
            ang = i / np.power(100000.0, j / dim)
            pe = np.where(j % 2 == 0, np.sin(ang), np.cos(ang))
            return jnp.asarray(pe, dtype=jnp.float32)
        key = jax.random.key(seed)
        k1, k2, k3, k4 = jax.random.split(key, 4)
        B = 64
        X = jax.random.normal(k1, (B, C, 224, 224), dtype=jnp.float32)
        bound = 1.0 / np.sqrt(IN_D)
        W = jax.random.uniform(k2, (HID, IN_D), minval=-bound, maxval=bound, dtype=jnp.float32)
        b = jax.random.uniform(k3, (HID,), minval=-bound, maxval=bound, dtype=jnp.float32)
        class_token = jax.random.uniform(k4, (1, HID), dtype=jnp.float32)
        pos_embed = _positional_embedding(SEQ, HID)
        return {'X': X, 'W': W, 'b': b, 'class_token': class_token, 'pos_embed': pos_embed}
    _L0_tok_all = _L0_tok_setup()
    _L0_tok_in = {k: v for k, v in _L0_tok_all.items() if k in ('W', 'b', 'class_token', 'pos_embed')}
    del _L0_tok_all

    def _L0_attn_setup():
        import jax, jax.numpy as jnp
        import numpy as np
        H, DH, M, DIN = (8, 64, 32, 128)
        INNER = H * DH
        key = jax.random.key(seed)
        ks = jax.random.split(key, 12)
        s = 0.02
        B, N = (4, 4096)
        return {'x': jax.random.normal(ks[0], (B, N, DIN), jnp.float32), 'Wx': jax.random.normal(ks[1], (INNER, DIN), jnp.float32) * s, 'bx': jnp.zeros((INNER,), jnp.float32), 'Wfx': jax.random.normal(ks[2], (INNER, DIN), jnp.float32) * s, 'bfx': jnp.zeros((INNER,), jnp.float32), 'Wslice': jax.random.normal(ks[3], (M, DH), jnp.float32) * s, 'bslice': jnp.zeros((M,), jnp.float32), 'Wq': jax.random.normal(ks[4], (DH, DH), jnp.float32) * s, 'Wk': jax.random.normal(ks[5], (DH, DH), jnp.float32) * s, 'Wv': jax.random.normal(ks[6], (DH, DH), jnp.float32) * s, 'Wout': jax.random.normal(ks[7], (DIN, INNER), jnp.float32) * s, 'bout': jnp.zeros((DIN,), jnp.float32), 'temperature': jnp.full((1, H, 1, 1), 0.5, jnp.float32)}
    _L0_attn_all = _L0_attn_setup()
    _L0_attn_in = {k: v for k, v in _L0_attn_all.items() if k in ('Wx', 'bx', 'Wfx', 'bfx', 'Wslice', 'bslice', 'Wq', 'Wk', 'Wv', 'Wout', 'bout', 'temperature')}
    del _L0_attn_all

    def _L0_ffn_setup():
        import jax, jax.numpy as jnp
        import numpy as np
        D, NH, HID, E = (128, 8, 512, 8)
        EPS = 1e-05

        def _layernorm(x, g, b):
            mu = jnp.mean(x, axis=-1, keepdims=True)
            var = jnp.mean(jnp.square(x - mu), axis=-1, keepdims=True)
            return (x - mu) * jax.lax.rsqrt(var + EPS) * g + b
        key = jax.random.key(seed)
        ks = jax.random.split(key, 20)
        s = 0.02
        inp = {'x': jax.random.normal(ks[0], (4, 256, D), jnp.float32), 'Wq': jax.random.normal(ks[1], (D, D), jnp.float32) * s, 'bq': jnp.zeros((D,), jnp.float32), 'Wk': jax.random.normal(ks[2], (D, D), jnp.float32) * s, 'bk': jnp.zeros((D,), jnp.float32), 'Wv': jax.random.normal(ks[3], (D, D), jnp.float32) * s, 'bv': jnp.zeros((D,), jnp.float32), 'Wo': jax.random.normal(ks[4], (D, D), jnp.float32) * s, 'bo': jnp.zeros((D,), jnp.float32), 'g1': jnp.ones((D,), jnp.float32), 'beta1': jnp.zeros((D,), jnp.float32), 'g2': jnp.ones((D,), jnp.float32), 'beta2': jnp.zeros((D,), jnp.float32), 'Wg': jax.random.normal(ks[5], (D, E), jnp.float32) * s, 'bg': jnp.zeros((E,), jnp.float32), 'W1': jax.random.normal(ks[6], (E, D, HID), jnp.float32) * s, 'b1': jnp.zeros((E, HID), jnp.float32), 'W2': jax.random.normal(ks[7], (E, HID, D), jnp.float32) * s, 'b2': jnp.zeros((E, D), jnp.float32)}
        return inp
    _L0_ffn_all = _L0_ffn_setup()
    _L0_ffn_in = {k: v for k, v in _L0_ffn_all.items() if k in ('Wq', 'bq', 'Wk', 'bk', 'Wv', 'bv', 'Wo', 'bo', 'g1', 'beta1', 'g2', 'beta2', 'Wg', 'bg', 'W1', 'b1', 'W2', 'b2')}
    del _L0_ffn_all
    return {'x': x, 'L0_tok_W': _L0_tok_in['W'], 'L0_tok_b': _L0_tok_in['b'], 'L0_tok_class_token': _L0_tok_in['class_token'], 'L0_tok_pos_embed': _L0_tok_in['pos_embed'], 'L0_attn_Wx': _L0_attn_in['Wx'], 'L0_attn_bx': _L0_attn_in['bx'], 'L0_attn_Wfx': _L0_attn_in['Wfx'], 'L0_attn_bfx': _L0_attn_in['bfx'], 'L0_attn_Wslice': _L0_attn_in['Wslice'], 'L0_attn_bslice': _L0_attn_in['bslice'], 'L0_attn_Wq': _L0_attn_in['Wq'], 'L0_attn_Wk': _L0_attn_in['Wk'], 'L0_attn_Wv': _L0_attn_in['Wv'], 'L0_attn_Wout': _L0_attn_in['Wout'], 'L0_attn_bout': _L0_attn_in['bout'], 'L0_attn_temperature': _L0_attn_in['temperature'], 'L0_ffn_Wq': _L0_ffn_in['Wq'], 'L0_ffn_bq': _L0_ffn_in['bq'], 'L0_ffn_Wk': _L0_ffn_in['Wk'], 'L0_ffn_bk': _L0_ffn_in['bk'], 'L0_ffn_Wv': _L0_ffn_in['Wv'], 'L0_ffn_bv': _L0_ffn_in['bv'], 'L0_ffn_Wo': _L0_ffn_in['Wo'], 'L0_ffn_bo': _L0_ffn_in['bo'], 'L0_ffn_g1': _L0_ffn_in['g1'], 'L0_ffn_beta1': _L0_ffn_in['beta1'], 'L0_ffn_g2': _L0_ffn_in['g2'], 'L0_ffn_beta2': _L0_ffn_in['beta2'], 'L0_ffn_Wg': _L0_ffn_in['Wg'], 'L0_ffn_bg': _L0_ffn_in['bg'], 'L0_ffn_W1': _L0_ffn_in['W1'], 'L0_ffn_b1': _L0_ffn_in['b1'], 'L0_ffn_W2': _L0_ffn_in['W2'], 'L0_ffn_b2': _L0_ffn_in['b2']}

def reference(x, L0_tok_W, L0_tok_b, L0_tok_class_token, L0_tok_pos_embed, L0_attn_Wx, L0_attn_bx, L0_attn_Wfx, L0_attn_bfx, L0_attn_Wslice, L0_attn_bslice, L0_attn_Wq, L0_attn_Wk, L0_attn_Wv, L0_attn_Wout, L0_attn_bout, L0_attn_temperature, L0_ffn_Wq, L0_ffn_bq, L0_ffn_Wk, L0_ffn_bk, L0_ffn_Wv, L0_ffn_bv, L0_ffn_Wo, L0_ffn_bo, L0_ffn_g1, L0_ffn_beta1, L0_ffn_g2, L0_ffn_beta2, L0_ffn_Wg, L0_ffn_bg, L0_ffn_W1, L0_ffn_b1, L0_ffn_W2, L0_ffn_b2):
    import jax
    import jax.numpy as jnp

    def _L0_tok_ref(X, W, b, class_token, pos_embed):
        import jax, jax.numpy as jnp
        import numpy as np
        N_PATCHES = 8
        PATCH = 28
        C = 3
        IN_D = C * PATCH * PATCH
        HID = 128
        SEQ = N_PATCHES * N_PATCHES + 1

        def _positional_embedding(seq_len, dim):
            i = np.arange(seq_len)[:, None].astype(np.float32)
            j = np.arange(dim)[None, :].astype(np.float32)
            ang = i / np.power(100000.0, j / dim)
            pe = np.where(j % 2 == 0, np.sin(ang), np.cos(ang))
            return jnp.asarray(pe, dtype=jnp.float32)
        B = X.shape[0]
        patches = X.reshape(B, C, N_PATCHES, PATCH, N_PATCHES, PATCH)
        patches = patches.transpose(0, 2, 4, 1, 3, 5).reshape(B, N_PATCHES * N_PATCHES, IN_D)
        tokens = jnp.einsum('bpi,hi->bph', patches, W) + b
        cls = jnp.broadcast_to(class_token[None, :, :], (B, 1, HID))
        tokens = jnp.concatenate([cls, tokens], axis=1)
        return tokens * pos_embed[None, :, :]

    def _L0_attn_ref(x, Wx, bx, Wfx, bfx, Wslice, bslice, Wq, Wk, Wv, Wout, bout, temperature):
        import jax, jax.numpy as jnp
        import numpy as np
        H, DH, M, DIN = (8, 64, 32, 128)
        INNER = H * DH
        B, N, D = x.shape
        scale = DH ** (-0.5)
        x_mid = (x @ Wx.T + bx).reshape(B, N, H, DH).transpose(0, 2, 1, 3)
        fx_mid = (x @ Wfx.T + bfx).reshape(B, N, H, DH).transpose(0, 2, 1, 3)
        slice_logits = (x_mid @ Wslice.T + bslice) / temperature
        slice_weights = jax.nn.softmax(slice_logits, axis=-1)
        slice_norm = slice_weights.sum(axis=2)
        slice_token = jnp.einsum('bhnd,bhnm->bhmd', fx_mid, slice_weights)
        slice_token = slice_token / (slice_norm[:, :, :, None] + 1e-05)
        q = slice_token @ Wq.T
        k = slice_token @ Wk.T
        v = slice_token @ Wv.T
        attn = jax.nn.softmax(jnp.einsum('bhmd,bhkd->bhmk', q, k) * scale, axis=-1)
        out_slice = jnp.einsum('bhmk,bhkd->bhmd', attn, v)
        out_x = jnp.einsum('bhmd,bhnm->bhnd', out_slice, slice_weights)
        out_x = out_x.transpose(0, 2, 1, 3).reshape(B, N, INNER)
        return out_x @ Wout.T + bout

    def _L0_ffn_ref(x, Wq, bq, Wk, bk, Wv, bv, Wo, bo, g1, beta1, g2, beta2, Wg, bg, W1, b1, W2, b2):
        import jax, jax.numpy as jnp
        import numpy as np
        D, NH, HID, E = (128, 8, 512, 8)
        EPS = 1e-05

        def _layernorm(x, g, b):
            mu = jnp.mean(x, axis=-1, keepdims=True)
            var = jnp.mean(jnp.square(x - mu), axis=-1, keepdims=True)
            return (x - mu) * jax.lax.rsqrt(var + EPS) * g + b
        B, S, _ = x.shape
        dh = D // NH
        q = (x @ Wq + bq).reshape(B, S, NH, dh)
        k = (x @ Wk + bk).reshape(B, S, NH, dh)
        v = (x @ Wv + bv).reshape(B, S, NH, dh)
        scores = jnp.einsum('bqhd,bkhd->bhqk', q, k) / jnp.sqrt(jnp.float32(dh)).astype(x.dtype)
        attn = jax.nn.softmax(scores, axis=-1)
        ctx = jnp.einsum('bhqk,bkhd->bqhd', attn, v).reshape(B, S, D)
        sa = ctx @ Wo + bo
        x = _layernorm(x + sa, g1, beta1)
        t = x.reshape(-1, D)
        logits = t @ Wg + bg
        idx = jnp.argmax(logits, axis=-1)
        h = jax.nn.gelu(jnp.einsum('td,edh->teh', t, W1) + b1, approximate=False)
        y = jnp.einsum('teh,ehd->ted', h, W2) + b2
        onehot = jax.nn.one_hot(idx, E, dtype=t.dtype)
        moe = jnp.einsum('ted,te->td', y, onehot).reshape(B, S, D)
        return _layernorm(x + moe, g2, beta2)
    h = _L0_tok_ref(x, L0_tok_W, L0_tok_b, L0_tok_class_token, L0_tok_pos_embed)
    h = h + _L0_attn_ref(_layernorm(h, axis=-1), L0_attn_Wx, L0_attn_bx, L0_attn_Wfx, L0_attn_bfx, L0_attn_Wslice, L0_attn_bslice, L0_attn_Wq, L0_attn_Wk, L0_attn_Wv, L0_attn_Wout, L0_attn_bout, L0_attn_temperature)
    h = h + _L0_ffn_ref(_layernorm(h, axis=-1), L0_ffn_Wq, L0_ffn_bq, L0_ffn_Wk, L0_ffn_bk, L0_ffn_Wv, L0_ffn_bv, L0_ffn_Wo, L0_ffn_bo, L0_ffn_g1, L0_ffn_beta1, L0_ffn_g2, L0_ffn_beta2, L0_ffn_Wg, L0_ffn_bg, L0_ffn_W1, L0_ffn_b1, L0_ffn_W2, L0_ffn_b2)
    return h

_drawn_inputs = setup_inputs


def setup_inputs(seed=0):
    import zlib

    import numpy as np

    out = dict(_drawn_inputs(seed))
    spreads = {'L0_attn_bx': (0.0, 0.8),
     'L0_attn_bfx': (0.0, 0.358),
     'L0_attn_bslice': (0.0, 0.8),
     'L0_attn_bout': (0.0, 0.1),
     'L0_attn_temperature': (0.5, 0.6),
     'L0_ffn_bq': (0.0, 0.8),
     'L0_ffn_bk': (0.0, 0.8),
     'L0_ffn_bv': (0.0, 0.346),
     'L0_ffn_bo': (0.0, 0.1),
     'L0_ffn_g1': (1.0, 0.2),
     'L0_ffn_beta1': (0.0, 0.1),
     'L0_ffn_g2': (1.0, 0.2),
     'L0_ffn_beta2': (0.0, 0.1),
     'L0_ffn_bg': (0.0, 0.1),
     'L0_ffn_b1': (0.0, 0.487),
     'L0_ffn_b2': (0.0, 0.1)}
    factors = {'L0_attn_Wx': 8.0,
     'L0_attn_Wfx': 6.978,
     'L0_attn_Wslice': 8.0,
     'L0_attn_Wq': 8.0,
     'L0_attn_Wk': 8.0,
     'L0_ffn_Wq': 8.0,
     'L0_ffn_Wk': 8.0,
     'L0_ffn_Wv': 3.801}
    for name, (base, spread) in spreads.items():
        noise = np.random.default_rng([zlib.crc32(name.encode()), seed]).standard_normal(out[name].shape)
        drawn = base * np.exp(spread * noise) if base else spread * noise
        out[name] = jnp.asarray(drawn.astype(out[name].dtype))
    for name, factor in factors.items():
        out[name] = (out[name] * factor).astype(out[name].dtype)
    return out
```

```python
import concourse.bass as bass
from concourse import mybir
from contextlib import ExitStack


def vit_tower_kernel(nc, x, tok_w, tok_b, tok_cls, tok_pos,
                     wx, bx, wfx, bfx, wslice, bslice, wq, wk, wv, wout, bout, temp,
                     f_wq, f_bq, f_wk, f_bk, f_wv, f_bv, f_wo, f_bo, g1, beta1, g2, beta2,
                     wg, bg, w1, b1, w2, b2, out):
    fp32 = mybir.dt.float32
    int32 = mybir.dt.int32
    uint32 = mybir.dt.uint32
    ALU = mybir.AluOpType
    ACT = mybir.ActivationFunctionType
    AX = mybir.AxisListType.X

    B, C, IMG, _ = x.shape
    D = tok_w.shape[0]
    S = tok_pos.shape[0]
    NP = 8
    PS = IMG // NP
    NPP = NP * NP
    GI = 4
    G = B // GI
    R = GI * S
    H, M = temp.shape[1], wslice.shape[0]
    DH = wslice.shape[1]
    HH = H // 4
    Q = GI * HH
    DH2 = D // H
    E, _, HID = w1.shape
    HC = HID // D
    TAIL = PS // (C + 1)
    STEPS = PS - TAIL
    assert C == 3 and STEPS == C * TAIL and 4 * M == 128 and D == 128
    T128 = 128
    NT = (B * S) // T128 + E
    EPS = 1e-5
    UNITS = 2 * GI
    UH = H // 2
    UW = UH * S
    VW = DH2 + 1
    T_SLOT = [2, 2, 2, 3, 3, 3, 3, 3]
    assert sum(T_SLOT) == STEPS and G % 2 == 0 and G >= 10
    LOOP0 = 8
    LAST = G + 6

    ctx = ExitStack()
    with ctx:
        def sb(name, shape, dt=fp32):
            return ctx.enter_context(nc.sbuf_tensor(name, shape, dt))

        def ps(name, cols=512):
            return ctx.enter_context(nc.psum_tensor(name, [128, cols], fp32))

        def sem(name):
            return ctx.enter_context(nc.semaphore(name))

        xs_dram = nc.dram_tensor("x_sorted", (NT * T128, D), fp32, kind="Internal").ap()
        zs_dram = nc.dram_tensor("z_sorted", (NT * T128, D), fp32, kind="Internal").ap()
        h_dram = nc.dram_tensor("h_rows", (B, S, D), fp32, kind="Internal").ap()

        XCOLS = GI * NP * IMG
        arena = sb("arena", [128, 2 * XCOLS])
        xbuf = [arena[:, p * XCOLS:(p + 1) * XCOLS] for p in range(2)]
        w1_sb = arena[:, 0:E * HID].rearrange("p (e n) -> p e n", e=E)
        w2_sb = arena[:, E * HID:2 * E * HID].rearrange("p (e c n) -> p e c n", e=E, c=HC)
        b1_bc = arena[:, 2 * E * HID:3 * E * HID].rearrange("p (e n) -> p e n", e=E)
        b2_bc = arena[:, 3 * E * HID:3 * E * HID + E * D].rearrange("p (e n) -> p e n", e=E)
        o = [XCOLS]

        def setup_buf(cols, parts=128):
            o[0] += cols
            assert o[0] <= 2 * XCOLS
            return arena[0:parts, o[0] - cols:o[0]]

        t_all = sb("t_all", [S, B, D])
        hT_all = sb("hT_all", [D, G, R])

        ident = sb("ident", [128, 128])
        ones = sb("ones", [S, 128])
        triu = sb("triu", [S, S])
        head_mask = sb("head_mask", [128, H])
        mhalf = sb("mhalf", [128, GI])
        w_tok = sb("w_tok", [128, STEPS, D])
        b_tok = sb("b_tok", [D, 1])
        posT = sb("posT", [D, S])
        w_log = sb("w_log", [D, H * M])
        w_stp = sb("w_stp", [D, H, 2 * DH])
        wvT = sb("wvT", [DH, DH])
        woutT = sb("woutT", [128, 4, D])
        bout_col = sb("bout_col", [D, 1])
        wq_aug = sb("wq_aug", [D, D])
        wk_aug = sb("wk_aug", [D, D])
        wv_aug = sb("wv_aug", [D, D])
        wo_sb = sb("wo_sb", [D, D])
        wg_sb = sb("wg_sb", [D, E])
        bo_bc = sb("bo_bc", [S, D])
        g1_bc = sb("g1_bc", [S, D])
        beta1_bc = sb("beta1_bc", [S, D])
        g2_bc = sb("g2_bc", [128, D])
        beta2_bc = sb("beta2_bc", [128, D])
        bg_bc = sb("bg_bc", [S, E])

        hT = sb("hT", [D, GI, S])
        xn = sb("xn", [S, GI, D])
        xnT = sb("xnT", [D, R])
        w = sb("w", [S, GI, H * M])
        mx1 = sb("mx1", [S, GI * H])
        wT = sb("wT", [128, 2, Q, S])
        gn = sb("gn", [128, Q, 128])
        gnT = gn[:, :, :].rearrange("p (b hh) (hl m) -> p b hh hl m", b=GI, hl=4)
        stT = gn[0:DH, :, :].rearrange("p q n -> p (q n)")
        pT = sb("pT", [DH, GI * H * M])
        rn = sb("rn", [128, Q])
        sc = sb("sc", [128, Q, M])
        smx = sb("smx", [128, Q])
        v_sb = sb("v_sb", [128, Q, DH])
        bd = sb("bd", [128, Q, 128])
        osb = sb("osb", [128, Q, 4 * DH])
        oxT = sb("oxT", [128, 4, R])
        oT = sb("oT", [D, R])
        h2 = sb("h2", [S, 2, GI, D])
        xa = sb("xa", [S, GI, D])
        xaT = sb("xaT", [D, R])
        qT = sb("qT", [D, 2, R])
        kT = sb("kT", [D, 2, R])
        va = sb("va", [S, 2, GI, H * VW])
        km = sb("km", [D, 2, UH, S])
        e2 = sb("e2", [S, 2, UW])
        eT = sb("eT", [S, 2, UW])
        mx2 = sb("mx2", [S, 2, UH])
        cx = sb("cx", [S, GI, D])
        cxT = sb("cxT", [D, R])
        xr = sb("xr", [S, GI, D])
        ts = sb("ts", [S, GI, D])
        tT = sb("tT", [D, R])
        pause = sb("pause", [128, 1])
        gl_all = sb("gl_all", [S, B, E])
        lnb = {n: (sb(f"st_{n}", [128, GI, 6]), sb(f"mv_{n}", [128, GI, 2]),
                   sb(f"ve_{n}", [128, GI]), sb(f"rs_{n}", [128, GI])) for n in ("a1", "f1", "f3")}

        ps_t = ps("ps_t")
        ps_a1 = ps("ps_a1")
        ps_a2 = ps("ps_a2", 1024)
        ps_a3 = ps("ps_a3")
        ps_f = ps("ps_f")
        ps_s = ps("ps_s")
        ps_e = ps("ps_e")

        s_ld = [sem(f"weights_loaded{k}") for k in range(8)]
        s_x = [sem(f"pixels_loaded{p}") for p in range(2)]
        s_hst = [sem(f"h_rows_stored{p}") for p in range(2)]
        s_zero = sem("sorted_rows_zeroed")
        s_moew = sem("expert_weights_loaded")
        s_dve0 = sem("setup_dve")
        s_pool0 = sem("setup_pool")
        s_pe0 = sem("setup_pe")
        s_act0 = sem("setup_act")
        s_xz = sem("pixel_buffer_zeroed")
        s_tail = sem("pixel_tail_copied")
        s_tok = sem("patch_products")
        s_hT = sem("tokens_transposed")
        s_hTc = sem("tokens_transposed_kept")
        s_hps = sem("tokens_in_psum")
        s_a1c = sem("a1_norm_chain")
        s_a1r = sem("a1_rstd")
        s_xn = sem("a1_normed")
        s_xnTp = sem("a1_normed_T_psum")
        s_xnT = sem("a1_normed_T")
        s_lg = sem("slice_logits")
        s_mx1 = sem("slice_max")
        s_sub1 = sem("slice_logits_less_max")
        s_exp1 = sem("slice_exp")
        s_wc = sem("slice_weight_chain")
        s_w = sem("slice_weights")
        s_wTp = sem("slice_weights_T_psum")
        s_wT = sem("slice_weights_T")
        s_gp = sem("slice_sums_psum")
        s_gc = sem("slice_sum_chain")
        s_gn = sem("slice_means")
        s_gTp = sem("slice_means_T_psum")
        s_gT = sem("slice_means_T")
        s_stp = sem("slice_tokens_psum")
        s_stT = sem("slice_tokens_T")
        s_pT = sem("slice_queries_T")
        s_scp = sem("slice_scores_psum")
        s_sc = sem("slice_scores")
        s_vp = sem("slice_values_psum")
        s_v = sem("slice_values")
        s_ac = sem("slice_attention_chain")
        s_asub = sem("slice_scores_less_max")
        s_aexp = sem("slice_scores_exp")
        s_bd = sem("slice_attention_T")
        s_osp = sem("slice_outputs_psum")
        s_osb = sem("slice_outputs")
        s_oxp = sem("token_outputs_psum")
        s_ox = sem("token_outputs")
        s_oTp = sem("output_product_psum")
        s_oT = sem("output_product_T")
        s_oTr = sem("output_with_residual")
        s_hp2 = sem("h_in_psum")
        s_h2 = sem("h_rows")
        s_f1c = sem("f1_norm_chain")
        s_f1r = sem("f1_rstd")
        s_x2 = sem("f1_normed_rows")
        s_xa = sem("f1_normed_aug")
        s_xaTp = sem("f1_normed_T_psum")
        s_xaT = sem("f1_normed_T")
        s_qp = sem("q_psum")
        s_q = sem("q_ready")
        s_kp = sem("k_psum")
        s_k = sem("k_ready")
        s_vp2 = sem("v_psum")
        s_v2 = sem("v_ready")
        s_km = sem("k_masked")
        s_s2p = sem("scores_psum")
        s_s2m = sem("scores_max")
        s_s2 = sem("scores_less_max")
        s_e2 = sem("scores_exp")
        s_eTp = sem("exp_T_psum")
        s_eT = sem("exp_T")
        s_cp = sem("context_psum")
        s_cr = sem("context_sum_recip")
        s_cx = sem("context")
        s_cTp = sem("context_T_psum")
        s_cT = sem("context_T")
        s_xr = sem("f3_residual_and_bias")
        s_saP = sem("attention_out_psum")
        s_r3 = sem("f3_sum")
        s_f3c = sem("f3_norm_chain")
        s_f3r = sem("f3_rstd")
        s_tn = sem("f3_normed")
        s_tg = sem("f3_scaled")
        s_t = sem("t_rows")
        s_tk = sem("t_rows_kept")
        s_tTp = sem("t_T_psum")
        s_tT = sem("t_T")
        s_gtp = sem("gate_psum")
        s_gt = sem("gate_logits")

        eqv = w[:, 0:2, :].rearrange("p a n -> p (a n)").rearrange("p (b e) -> p b e", e=E)
        oh = w[:, 2:4, :].rearrange("p a n -> p (a n)").rearrange("p (e b) -> p e b", e=E)
        tot = gn[0:S, 0:4, :].rearrange("p q n -> p (q n)")
        cum = gn[0:S, 4:8, :].rearrange("p q n -> p (q n)")
        zrow = e2[:, :, 0:256].rearrange("p a n -> p a n")
        pos_f = mx1
        NTH = -(-(B * S) // T128)
        rt = sb("rt", [S, 12, E])
        cmp_nt = bd[0:S, :, 0:NTH]
        cmp_te = oxT[0:1, 0:2, 0:NT * E // 2].rearrange("p a n -> p a n")
        mxg = sb("mxg", [S, 2, B])
        pos_i = sb("pos_i", [S, B], int32)
        thr = sb("thr", [S, NTH])
        tix = sb("tix", [1, NT])
        tef = sb("tef", [1, NT])
        te_i = sb("te_i", [1, NT], int32)
        wsc = sb("wsc", [S, E])
        zeros = sb("zeros", [S, B * E])
        xt = osb[:, 0, :].rearrange("p (a n) -> p a n", a=2)
        xtT = osb[:, 1, :].rearrange("p (a n) -> p a n", a=2)
        xb = osb[:, 2, :].rearrange("p (a n) -> p a n", a=2)
        hb = gn[:, :, :].rearrange("p (a q) n -> p a (q n)", a=2)
        hbT = bd[:, :, :].rearrange("p (a q) n -> p a q n", a=2)
        st_m, mv_m, ve_m, rs_m = (sb("st_m", [128, 6]), sb("mv_m", [128, 2]), sb("ve_m", [128, 1]), sb("rs_m", [128, 1]))
        CI = 8
        zg = t_all[:, 0:2 * CI, :].rearrange("p (a b) n -> p a b n", a=2)
        hz = t_all[:, 2 * CI:4 * CI, :].rearrange("p (a b) n -> p a b n", a=2)

        s_iota = sem("routing_constants")
        s_rc = sem("routing_chain")
        s_rp = sem("routing_prefix_psum")
        s_pos = sem("positions_ready")
        s_te = sem("tile_experts_ready")
        s_scat = sem("rows_scattered")
        s_xt = [sem(f"tile_rows_loaded{p}") for p in range(2)]
        s_xtP = sem("tile_T_psum")
        s_xtT = sem("tile_T")
        s_w1 = sem("hidden_psum")
        s_xb = sem("tile_rows_and_bias")
        s_hb = sem("hidden_and_bias")
        s_gl = sem("hidden_gelu")
        s_hTP = sem("hidden_T_psum")
        s_hbT = sem("hidden_T")
        s_w2 = sem("expert_out_psum")
        s_rz = sem("expert_sum")
        s_mc = sem("tile_norm_chain")
        s_mr = sem("tile_rstd")
        s_mn = sem("tile_normed")
        s_mg = sem("tile_scaled")
        s_z = sem("tile_done")
        s_zst = [sem(f"tile_stored{p}") for p in range(2)]
        s_gath = [sem(f"rows_gathered{p}") for p in range(2)]
        s_hl = [sem(f"h_loaded{p}") for p in range(2)]
        s_fin = sem("last_sum")
        s_out = [sem(f"out_stored{p}") for p in range(2)]

        def tile_bodies(eng, body):
            for k in range(2):
                body(k, k // 2, k % 2)
            with eng.Fori(1, NT // 2, 1) as j:
                for p in range(2):
                    body(j * 2 + p, j, p)
            body(NT, NT // 2, 0)

        def m1(k):
            return k < NT if isinstance(k, int) else True

        def m2(k):
            return k >= 1 if isinstance(k, int) else True

        block = ctx.enter_context(nc.Block())

        def upto(eng, s, per, g, k=None):
            n = g * per + (per if k is None else k)
            if isinstance(g, int) and n <= 0:
                return
            eng.wait_ge(s, n)

        def bodies(eng, body):
            for i in range(LOOP0):
                body(i, i // 2, i % 2)
            with eng.Fori(LOOP0 // 2, G // 2, 1) as j:
                for p in range(2):
                    body(j * 2 + p, j, p)
            for i in range(G, LAST):
                body(i, i // 2, i % 2)

        def on(i, lag):
            return 0 <= i - lag < G if isinstance(i, int) else True

        DVE0 = {}
        n = 0
        for name in ("zeros", "gaps", "aug1", "aug2", "aug3", "pad_zero", "wpad", "wx1", "wx2", "wfx1", "wfx2", "wslT", "wvT", "idA",
                     "pos", "cls", "itemp", "wlog", "wstp", "wout", "negk", "wqa", "wqs", "wka", "wva"):
            n += 1
            DVE0[name] = n
        PE0 = {name: k + 1 for k, name in enumerate(("wslT", "wvT", "A", "pos", "wlog", "wstp", "wout"))}
        TB = (STEPS + 3) // 4

        wtok_nat = setup_buf(C * PS * PS)
        assert C * PS * PS == tok_w.shape[1]
        wpad = setup_buf(STEPS * 128)
        wx_nat = setup_buf(H * D, DH).rearrange("p (h n) -> p h n", h=H)
        wfx_nat = t_all[0:DH, 0:H, :]
        wout_nat = hT_all[:, 0:2, 0:256].rearrange("p a n -> p a n")
        wq_nat = t_all[0:DH, H, 0:DH]
        wk_nat = t_all[0:DH, H, DH:2 * DH]
        wv_nat = t_all[0:DH, H + 1, 0:DH]
        wsl_nat = t_all[0:M, H + 2, 0:DH]
        wslT = t_all[0:DH, H + 3, 0:M]
        idA = t_all[0:DH, H + 4, :]
        pos_nat = t_all[0:S, H + 5, :]
        bsl_row = t_all[0:1, H + 6:H + 8, :]
        e_last = t_all[0:1, H + 8, :]
        bx_nat = t_all[0:DH, H + 9, 0:H]
        bfx_nat = t_all[0:DH, H + 9, H:2 * H]
        temp_bc = hT_all[:, 3, 0:H]
        itemp = hT_all[:, 3, H:2 * H]
        cls_col = hT_all[:, 3, 2 * H:2 * H + 1]
        neg_keep = hT_all[:, 3, 2 * H + 1:2 * H + 2]
        lastq = hT_all[:, 4, 0:D]
        lastk = hT_all[:, 5, 0:D]
        lastv = hT_all[:, 6, 0:D]
        natq = hT_all[:, 7, 0:D]
        natk = hT_all[:, 8, 0:D]
        natv = hT_all[:, 9, 0:D]
        zero_tile = osb[:, 0, 0:128]

        def row(a, n=128):
            return a.rearrange("(o n) -> o n", o=1).broadcast_to([n, a.shape[0]])

        def load_pixels(eng, g, half, p):
            if not isinstance(g, int) or g >= 2:
                upto(eng, s_tok, 1, g - 2)
            for b in range(GI):
                for c in range(C):
                    src = x[bass.ds(g * GI + b, 1), c, :, :].rearrange("o h w -> (o h) w") if not isinstance(g, int) \
                        else x[g * GI + b, c, :, :]
                    dst = xbuf[p][32 * c:32 * c + PS, b * NP * IMG:(b + 1) * NP * IMG].rearrange("p (a w) -> p a w", a=NP)
                    eng.dma_start(dst, src.rearrange("(a y) w -> y a w", y=PS)).then_inc(s_x[p], 16)

        def sp_tail(sp):
            sp.wait_ge(s_scat, 16 * B)

            def load(k, p):
                upto(sp, s_xtP, 1, k - 2)
                upto(sp, s_xb, 1, k - 2)
                src = xs_dram[bass.ds(k * T128, T128), :] if not isinstance(k, int) else xs_dram[k * T128:(k + 1) * T128, :]
                sp.dma_start(xt[:, p, :], src).then_inc(s_xt[p], 16)

            load(0, 0)

            def body(k, j, p):
                if m1(k) and (not isinstance(k, int) or k + 1 < NT):
                    load(k + 1, 1 - p)
                if m2(k):
                    t = k - 1
                    upto(sp, s_z, 1, t)
                    dst = zs_dram[bass.ds(t * T128, T128), :] if not isinstance(k, int) else zs_dram[t * T128:(t + 1) * T128, :]
                    sp.dma_start(dst, xb[:, 1 - p, :]).then_inc(s_zst[1 - p], 16)

            for k in range(2):
                body(k, k // 2, k % 2)
            with sp.Fori(1, NT // 2 - 1, 1) as j:
                for p in range(2):
                    body(j * 2 + p, j, p)
            for k in range(NT - 2, NT + 1):
                body(k, k // 2, k % 2)
            NCH = B // CI
            for c in range(2):
                sp.dma_start(hz[:, c, :, :], h_dram[c * CI:(c + 1) * CI, :, :].rearrange("b s d -> s b d")).then_inc(s_hl[c], 16)
            for c in range(NCH):
                p = c % 2
                sp.wait_ge(s_fin, c + 1)
                sp.dma_start(out[c * CI:(c + 1) * CI, :, :].rearrange("b s d -> s b d"), zg[:, p, :, :]).then_inc(s_out[p], 16)
                if c + 2 < NCH:
                    sp.dma_start(hz[:, p, :, :], h_dram[(c + 2) * CI:(c + 3) * CI, :, :].rearrange("b s d -> s b d"))\
                      .then_inc(s_hl[p], 16)
            for p in range(2):
                sp.wait_ge(s_out[p], 16 * (NCH // 2))

        def pool_tail(pool):
            nc.gpsimd.iota(thr[:, :], [[T128, NTH]], base=0, channel_multiplier=0, allow_small_or_imprecise_dtypes=True).then_inc(s_iota, 1)
            nc.gpsimd.iota(tix[:, :], [[1, NT]], base=0, channel_multiplier=0, allow_small_or_imprecise_dtypes=True).then_inc(s_iota, 1)
            nc.gpsimd.iota(wsc[:, :], [[-1, E]], base=E, channel_multiplier=0, allow_small_or_imprecise_dtypes=True).then_inc(s_iota, 1)
            pool.wait_ge(s_pos, 1)
            pool.wait_ge(s_zero, 16)
            upto(pool, s_tk, 1, G - 1)
            for b in range(B):
                pool.indirect_dma_start(xs_dram, bass.IndirectOffsetOnAxis(ap=pos_i[:, b:b + 1], axis=0),
                                        t_all[:, b, :], None).then_inc(s_scat, 16)
            g2v, beta2v = g2_bc[:, :], beta2_bc[:, :]

            def body(k, j, p):
                if not m2(k):
                    return
                t = k - 1
                upto(pool, s_mc, 3, t)
                nc.gpsimd.tensor_tensor(rs_m[:, :], ve_m[:, :], mhalf[:, 0:1], ALU.pow).then_inc(s_mr, 1)
                upto(pool, s_mn, 1, t)
                nc.gpsimd.tensor_tensor(xb[:, 1 - p, :], xb[:, 1 - p, :], g2v, ALU.mult).then_inc(s_mg, 1)
                upto(pool, s_mg, 1, t)
                nc.gpsimd.tensor_tensor(xb[:, 1 - p, :], xb[:, 1 - p, :], beta2v, ALU.add).then_inc(s_z, 1)

            tile_bodies(pool, body)
            for p in range(2):
                pool.wait_ge(s_zst[p], 16 * (NT // 2))
            for c in range(B // CI):
                p = c % 2
                if c >= 2:
                    pool.wait_ge(s_out[p], 16 * (c // 2))
                for b in range(CI):
                    img = c * CI + b
                    pool.indirect_dma_start(zg[:, p, b, :], None, zs_dram,
                                            bass.IndirectOffsetOnAxis(ap=pos_i[:, img:img + 1], axis=0)).then_inc(s_gath[p], 16)

        def pe_tail(pe):
            pe.wait_ge(s_rc, RC["oh"])
            upto(pe, s_gt, 1, G - 1)
            ohf = oh.rearrange("p e b -> p (e b)")
            nc.tensor.matmul(ps_f[0:S, :], triu[:, :], ohf, start=True, stop=True)
            nc.tensor.matmul(ps_s[0:S, :], ones[:, 0:S], ohf, start=True, stop=True).then_inc(s_rp, 1)
            pe.wait_ge(s_moew, 64)
            pe.wait_ge(s_te, 1)
            pe.wait_ge(s_pos, 1)

            def body(k, j, p):
                def expert(t):
                    src = te_i[0:1, bass.ds(t, 1)] if not isinstance(t, int) else te_i[0:1, t:t + 1]
                    return pe.value_load(src, min_val=0, max_val=E - 1)
                e1 = expert(k) if m1(k) else None
                e2_ = expert(k - 1) if m2(k) else None
                if m1(k):
                    pe.wait_ge(s_xt[p], ((k // 2 if isinstance(k, int) else j) + 1) * 16)
                    upto(pe, s_xtT, 1, k - 1)
                    nc.tensor.transpose(ps_s[:, 0:D], xt[:, p, :], ident[:, :]).then_inc(s_xtP, 1)
                if m2(k):
                    upto(pe, s_gl, 1, k - 1)
                    upto(pe, s_hbT, 1, k - 2)
                    for c in range(HC):
                        mm = nc.tensor.transpose(ps_a1[:, c * 128:(c + 1) * 128], hb[:, 1 - p, c * 128:(c + 1) * 128], ident[:, :])
                    mm.then_inc(s_hTP, 1)
                if m1(k):
                    upto(pe, s_xtT, 1, k)
                    upto(pe, s_hb, 1, k - 2)
                    nc.tensor.matmul(ps_a2[:, p * 512:(p + 1) * 512], xtT[:, p, :],
                                     w1_sb[:, bass.ds(e1, 1), :].rearrange("p o n -> p (o n)"),
                                     start=True, stop=True).then_inc(s_w1, 1)
                if m2(k):
                    upto(pe, s_hbT, 1, k - 1)
                    upto(pe, s_rz, 1, k - 2)
                    for c in range(HC):
                        mm = nc.tensor.matmul(ps_a3[:, 0:D], hbT[:, 1 - p, c, :],
                                              w2_sb[:, bass.ds(e2_, 1), c, :].rearrange("p o n -> p (o n)"),
                                              start=(c == 0), stop=(c == HC - 1))
                    mm.then_inc(s_w2, 1)

            tile_bodies(pe, body)

        def act_tail(act):
            act.preload_act_table(ACT.Gelu)

            def body(k, j, p):
                if m1(k):
                    upto(act, s_xtP, 1, k)
                    upto(act, s_w1, 1, k - 2)
                    nc.scalar.activation(xtT[:, p, :], ps_s[:, 0:D], ACT.Copy).then_inc(s_xtT, 1)
                if m2(k):
                    upto(act, s_hTP, 1, k - 1)
                    upto(act, s_w2, 1, k - 3)
                    nc.scalar.activation(hbT[:, 1 - p, :, :].rearrange("p c n -> p (c n)"), ps_a1[:, :], ACT.Copy).then_inc(s_hbT, 1)
                if m1(k):
                    upto(act, s_hb, 1, k)
                    nc.scalar.activation(hb[:, p, :], hb[:, p, :], ACT.Gelu).then_inc(s_gl, 1)

            tile_bodies(act, body)

        RC = {name: k + 1 for k, name in enumerate((
            "max", "eq", "eqw", "first", "oh", "tot", "cum", "excl", "cnt", "cmp", "nt", "ntc", "base", "base2", "base3",
            "pos", "pos2", "pos3", "posf", "posi", "tecmp", "te", "temin"))}

        def dve_tail(dve):
            v = nc.vector
            upto(dve, s_gt, 1, G - 1)
            dve.wait_ge(s_iota, 3)
            done = [0]

            def step(ins, name):
                done[0] += 1
                assert RC[name] == done[0], name
                ins.then_inc(s_rc, 1)
                dve.wait_ge(s_rc, done[0])

            v.memset(zeros[:, :], 0.0)
            step(v.tensor_reduce(mxg[:, 0, :], gl_all[:, :, :], AX, ALU.max), "max")
            step(v.tensor_tensor(eqv, gl_all[:, :, :], mxg[:, 0, :].unsqueeze(2).broadcast_to([S, B, E]), ALU.is_equal), "eq")
            step(v.tensor_tensor(eqv, eqv, wsc[:, :].unsqueeze(1).broadcast_to([S, B, E]), ALU.mult), "eqw")
            step(v.tensor_reduce(mxg[:, 1, :], eqv, AX, ALU.max), "first")
            step(v.tensor_tensor(oh.rearrange("p e b -> p b e"), eqv, mxg[:, 1, :].unsqueeze(2).broadcast_to([S, B, E]),
                                 ALU.is_equal), "oh")
            dve.wait_ge(s_rp, 1)
            tot3, cum3 = (a.rearrange("p (e b) -> p e b", e=E) for a in (tot, cum))
            step(v.tensor_copy(tot, ps_s[0:S, :]), "tot")
            step(v.tensor_tensor_scan(cum, tot, zeros[:, :], 0.0, ALU.add, ALU.add), "cum")
            step(v.tensor_tensor(tot, cum, tot, ALU.subtract), "excl")
            cnt, nt, ntc, base = rt[:, 0, :], rt[:, 1, :], rt[:, 2, :], rt[:, 3, :]
            step(v.tensor_tensor(cnt.unsqueeze(2), cum3[:, :, B - 1:B], tot3[:, :, 0:1], ALU.subtract), "cnt")
            step(v.tensor_tensor(cmp_nt, cnt.unsqueeze(2).broadcast_to([S, E, NTH]),
                                 thr[:, :].unsqueeze(1).broadcast_to([S, E, NTH]), ALU.is_gt), "cmp")
            step(v.tensor_reduce(nt, cmp_nt, AX, ALU.add), "nt")
            step(v.tensor_tensor_scan(ntc, nt, zeros[:, 0:E], 0.0, ALU.add, ALU.add), "ntc")
            step(v.tensor_tensor(base, ntc, nt, ALU.subtract), "base")
            step(v.tensor_scalar(base, base, float(T128), -1.0, ALU.mult, ALU.add), "base2")
            step(v.tensor_tensor(base.unsqueeze(2), base.unsqueeze(2), tot3[:, :, 0:1], ALU.subtract), "base3")
            step(v.tensor_tensor(tot, tot, ps_f[0:S, :], ALU.add), "pos")
            step(v.tensor_tensor(tot3, tot3, base.unsqueeze(2).broadcast_to([S, E, B]), ALU.add), "pos2")
            step(v.tensor_tensor(tot3, tot3, oh, ALU.mult), "pos3")
            step(v.tensor_reduce(mxg[:, 0, :], tot3.rearrange("p e b -> p b e"), AX, ALU.add), "posf")
            ins = v.tensor_copy(pos_i[:, :], mxg[:, 0, :])
            step(ins, "posi")
            v.nop().then_inc(s_pos, 1)
            cte = cmp_te.rearrange("p a n -> p a n")
            half = NT // 2
            for a in range(2):
                last = v.tensor_tensor(cte[:, a, :].rearrange("p (t e) -> p t e", e=E),
                                       ntc[0:1, :].unsqueeze(1).broadcast_to([1, half, E]),
                                       tix[:, a * half:(a + 1) * half].unsqueeze(2).broadcast_to([1, half, E]), ALU.is_le)
            step(last, "tecmp")
            for a in range(2):
                last = v.tensor_reduce(tef[:, a * half:(a + 1) * half], cte[:, a, :].rearrange("p (t e) -> p t e", e=E), AX, ALU.add)
            step(last, "te")
            step(v.tensor_scalar(te_i[:, :], tef[:, :], float(E - 1), None, ALU.min), "temin")
            v.nop().then_inc(s_te, 1)
            dve.wait_ge(s_moew, 64)

            def body(k, j, p):
                t = k - 1
                if m1(k):
                    src = te_i[0:1, bass.ds(k, 1)] if not isinstance(k, int) else te_i[0:1, k:k + 1]
                    e = dve.value_load(src, min_val=0, max_val=E - 1)
                    dve.wait_ge(s_xt[p], ((k // 2 if isinstance(k, int) else j) + 1) * 16)
                    if not isinstance(k, int) or k >= 2:
                        dve.wait_ge(s_zst[p], (k // 2 if isinstance(k, int) else j) * 16)
                    v.tensor_tensor(xb[:, p, :], xt[:, p, :], b2_bc[:, bass.ds(e, 1), :].rearrange("p o n -> p (o n)"),
                                    ALU.add).then_inc(s_xb, 1)
                if m2(k):
                    upto(dve, s_w2, 1, t)
                    v.tensor_tensor(xb[:, 1 - p, :], xb[:, 1 - p, :], ps_a3[:, 0:D], ALU.add).then_inc(s_rz, 1)
                    upto(dve, s_rz, 1, t)
                    v.bn_stats(st_m[:, :], xb[:, 1 - p, :]).then_inc(s_mc, 1)
                    upto(dve, s_mc, 3, t, 1)
                    v.memset(pause[:, :], 0.0)
                    v.bn_aggr(mv_m[:, :], st_m[:, :]).then_inc(s_mc, 1)
                    upto(dve, s_mc, 3, t, 2)
                    v.tensor_scalar(ve_m[:, :], mv_m[:, 1:2], EPS, None, ALU.add).then_inc(s_mc, 1)
                if m1(k):
                    upto(dve, s_w1, 1, k)
                    upto(dve, s_hTP, 1, k - 2)
                    v.tensor_tensor(hb[:, p, :], ps_a2[:, p * 512:(p + 1) * 512],
                                    b1_bc[:, bass.ds(e, 1), :].rearrange("p o n -> p (o n)"), ALU.add).then_inc(s_hb, 1)
                if m2(k):
                    upto(dve, s_mr, 1, t)
                    v.tensor_scalar(xb[:, 1 - p, :], xb[:, 1 - p, :], mv_m[:, 0:1], rs_m[:, :], ALU.subtract, ALU.mult)\
                        .then_inc(s_mn, 1)

            tile_bodies(dve, body)
            for c in range(B // CI):
                p = c % 2
                dve.wait_ge(s_gath[p], 16 * CI * (c // 2 + 1))
                dve.wait_ge(s_hl[p], 16 * (c // 2 + 1))
                v.tensor_tensor(zg[:, p, :, :], zg[:, p, :, :], hz[:, p, :, :], ALU.add).then_inc(s_fin, 1)

        @block.sync
        def _(sp):
            sp.dma_start(wtok_nat, tok_w).then_inc(s_ld[0], 16)
            sp.dma_start(pos_nat, tok_pos).then_inc(s_ld[1], 16)
            sp.dma_start(cls_col, tok_cls.rearrange("o n -> n o")).then_inc(s_ld[1], 16)
            sp.dma_start(b_tok[:, :], tok_b.rearrange("(n o) -> n o", o=1)).then_inc(s_ld[1], 16)
            sp.wait_ge(s_xz, 1)
            load_pixels(sp, 0, 0, 0)
            sp.dma_start(wx_nat, wx.rearrange("(h d) c -> d h c", d=DH)).then_inc(s_ld[2], 16)
            sp.dma_start(wfx_nat, wfx.rearrange("(h d) c -> d h c", d=DH)).then_inc(s_ld[2], 16)
            sp.dma_start(bx_nat, bx.rearrange("(h d) -> d h", d=DH), allow_slow_non_contiguous=True).then_inc(s_ld[2], 16)
            sp.dma_start(bfx_nat, bfx.rearrange("(h d) -> d h", d=DH), allow_slow_non_contiguous=True).then_inc(s_ld[2], 16)
            sp.dma_start(wq_nat, wq).then_inc(s_ld[3], 16)
            sp.dma_start(wk_nat, wk).then_inc(s_ld[3], 16)
            sp.dma_start(wv_nat, wv).then_inc(s_ld[3], 16)
            sp.dma_start(wsl_nat, wslice).then_inc(s_ld[3], 16)
            sp.dma_start(bsl_row.rearrange("p a (h m) -> p (a h) m", m=M),
                         bslice.rearrange("(o n) -> o n", o=1).unsqueeze(1).broadcast_to([1, H, M]))\
              .then_inc(s_ld[3], 16)
            sp.dma_start(wout_nat, wout.rearrange("p (a n) -> p a n", a=2)).then_inc(s_ld[4], 16)
            sp.dma_start(bout_col[:, :], bout.rearrange("(n o) -> n o", o=1)).then_inc(s_ld[4], 16)
            sp.dma_start(temp_bc, row(temp.rearrange("a h b c -> (a h b c)"))).then_inc(s_ld[4], 16)
            for nat, last, wd, bd_ in ((natq, lastq, f_wq, f_bq), (natk, lastk, f_wk, f_bk), (natv, lastv, f_wv, f_bv)):
                sp.dma_start(nat[0:D - 1, :], wd[0:D - 1, :]).then_inc(s_ld[5], 16)
                sp.dma_start(nat[D - 1:D, :], row(bd_, 1)).then_inc(s_ld[5], 16)
                sp.dma_start(last, wd[D - 1:D, :].broadcast_to([D, D])).then_inc(s_ld[5], 16)
            sp.dma_start(wo_sb[:, :], f_wo).then_inc(s_ld[6], 16)
            sp.dma_start(wg_sb[:, :], wg).then_inc(s_ld[6], 16)
            sp.dma_start(bo_bc[:, :], row(f_bo, S)).then_inc(s_ld[7], 16)
            sp.dma_start(g1_bc[:, :], row(g1, S)).then_inc(s_ld[7], 16)
            sp.dma_start(beta1_bc[:, :], row(beta1, S)).then_inc(s_ld[7], 16)
            sp.dma_start(bg_bc[:, :], row(bg, S)).then_inc(s_ld[7], 16)
            sp.dma_start(g2_bc[:, :], row(g2)).then_inc(s_ld[7], 16)
            sp.dma_start(beta2_bc[:, :], row(beta2)).then_inc(s_ld[7], 16)
            sp.wait_ge(s_dve0, DVE0["zeros"])
            sp.dma_start(xs_dram.rearrange("(k p) d -> p k d", p=T128),
                         zero_tile.unsqueeze(1).broadcast_to([128, NT, D])).then_inc(s_zero, 16)
            sp.wait_ge(s_xz, 2)
            load_pixels(sp, 1, 0, 1)

            def body(i, j, p):
                if on(i, 0) and (not isinstance(i, int) or i + 2 < G):
                    load_pixels(sp, i + 2, j + 1, p)
                if on(i, 3):
                    g = i - 3
                    upto(sp, s_h2, 1, g)
                    dst = h_dram[bass.ds(g * GI, GI), :, :] if not isinstance(g, int) \
                        else h_dram[g * GI:(g + 1) * GI, :, :]
                    sp.dma_start(dst.rearrange("b s d -> s b d"), h2[:, 1 - p, :, :]).then_inc(s_hst[1 - p], 16)

            for i in range(LOOP0):
                body(i, i // 2, i % 2)
            with sp.Fori(LOOP0 // 2, G // 2 - 1, 1) as j:
                for p in range(2):
                    body(j * 2 + p, j, p)
            for i in range(G - 2, LAST):
                body(i, i // 2, i % 2)
            upto(sp, s_tok, 1, G - 1)
            sp.dma_start(w1_sb, w1.rearrange("e c n -> c e n")).then_inc(s_moew, 16)
            sp.dma_start(w2_sb, w2.rearrange("e (c p) n -> p e c n", p=D)).then_inc(s_moew, 16)
            sp.dma_start(b1_bc, b1.rearrange("(o e) n -> o e n", o=1).broadcast_to([128, E, HID])).then_inc(s_moew, 16)
            sp.dma_start(b2_bc, b2.rearrange("(o e) n -> o e n", o=1).broadcast_to([128, E, D])).then_inc(s_moew, 16)
            sp.wait_ge(s_zero, 16)
            sp.wait_ge(s_moew, 64)
            for p in range(2):
                sp.wait_ge(s_hst[p], 16 * (G // 2))
            sp_tail(sp)

        @block.gpsimd
        def _(pool):
            nc.gpsimd.memset(ident[:, :], 0.0).then_inc(s_pool0, 1)
            pool.wait_ge(s_pool0, 1)
            nc.gpsimd.affine_select(out=ident[:, :], in_=ident[:, :], compare_op=ALU.not_equal, fill=1.0,
                                    base=0, pattern=[[-1, 128]], channel_multiplier=1).then_inc(s_pool0, 1)
            nc.gpsimd.memset(mhalf[:, :], -0.5).then_inc(s_pool0, 1)
            nc.gpsimd.memset(ones[:, :], 1.0).then_inc(s_pool0, 1)
            pool.wait_ge(s_pool0, 4)
            nc.gpsimd.affine_select(out=triu[:, :], in_=ones[0:S, 0:S], compare_op=ALU.is_ge, fill=0.0,
                                    base=0, pattern=[[1, S]], channel_multiplier=-1).then_inc(s_pool0, 1)
            nc.gpsimd.memset(head_mask[:, :], 1.0).then_inc(s_pool0, 1)
            pool.wait_ge(s_pool0, 6)
            nc.gpsimd.affine_select(out=head_mask[:, :], in_=head_mask[:, :], compare_op=ALU.is_ge, fill=0.0,
                                    base=0, pattern=[[-DH2, H]], channel_multiplier=1).then_inc(s_pool0, 1)
            pool.wait_ge(s_pool0, 7)
            nc.gpsimd.affine_select(out=head_mask[:, :], in_=head_mask[:, :], compare_op=ALU.is_ge, fill=0.0,
                                    base=DH2 - 1, pattern=[[DH2, H]], channel_multiplier=-1).then_inc(s_pool0, 1)
            pool.wait_ge(s_pool0, 8)
            pool.wait_ge(s_ld[7], 96)

            def rstd(name, s_chain, s_r, g):
                _, _, ve, rs = lnb[name]
                upto(pool, s_chain, 3, g)
                nc.gpsimd.tensor_tensor(rs[0:S, :], ve[0:S, :], mhalf[0:S, :], ALU.pow).then_inc(s_r, 1)

            def masked_k(g, u, p):
                b, hf = u // 2, u % 2
                upto(pool, s_s2p, UNITS, g, u - 1)
                kv = kT[:, p, b * S:(b + 1) * S].unsqueeze(1).broadcast_to([D, UH, S])
                mv = head_mask[:, hf * UH:(hf + 1) * UH].unsqueeze(2).broadcast_to([D, UH, S])
                nc.gpsimd.tensor_tensor(km[:, u % 2, :, :], kv, mv, ALU.mult).then_inc(s_km, 1)

            def body(i, j, p):
                if on(i, 5):
                    upto(pool, s_k, 1, i - 5)
                    masked_k(i - 5, 0, 1 - p)
                    masked_k(i - 5, 1, 1 - p)
                if on(i, 6):
                    g = i - 6
                    upto(pool, s_x2, 1, g)
                    upto(pool, s_t, 1, g - 1)
                    src = t_all[:, bass.ds(g * GI, GI), :] if not isinstance(g, int) else t_all[:, g * GI:(g + 1) * GI, :]
                    nc.gpsimd.tensor_tensor(xr[:, :, :], src, bo_bc[:, :].unsqueeze(1).broadcast_to([S, GI, D]),
                                            ALU.add).then_inc(s_xr, 1)
                if on(i, 4):
                    rstd("f1", s_f1c, s_f1r, i - 4)
                if on(i, 1):
                    rstd("a1", s_a1c, s_a1r, i - 1)
                if on(i, 5):
                    masked_k(i - 5, 2, 1 - p)
                if on(i, 6):
                    g = i - 6
                    rstd("f3", s_f3c, s_f3r, g)
                if on(i, 5):
                    masked_k(i - 5, 3, 1 - p)
                if on(i, 6):
                    g = i - 6
                    upto(pool, s_tn, 1, g)
                    nc.gpsimd.tensor_tensor(xr[:, :, :], xr[:, :, :], g1_bc[:, :].unsqueeze(1).broadcast_to([S, GI, D]),
                                            ALU.mult).then_inc(s_tg, 1)
                    upto(pool, s_tg, 1, g)
                    upto(pool, s_tTp, 1, g - 1)
                    upto(pool, s_tk, 1, g - 1)
                    nc.gpsimd.tensor_tensor(ts[:, :, :], xr[:, :, :], beta1_bc[:, :].unsqueeze(1).broadcast_to([S, GI, D]),
                                            ALU.add).then_inc(s_t, 1)
                if on(i, 5):
                    for u in range(4, UNITS):
                        masked_k(i - 5, u, 1 - p)

            bodies(pool, body)
            pool_tail(pool)

        @block.tensor
        def _(pe):
            pe.wait_ge(s_pool0, 8)
            pe.wait_ge(s_dve0, DVE0["wpad"])
            wp = wpad.rearrange("p (s n) -> p s n", s=STEPS)
            for k in range(TB):
                if k >= 2:
                    pe.wait_ge(s_act0, k - 1)
                for q in range(4 * k, min(4 * k + 4, STEPS)):
                    last = nc.tensor.transpose(ps_a2[:, (q % 8) * 128:(q % 8) * 128 + 128], wp[:, q, :], ident[:, :])
                last.then_inc(s_pe0, 1)
            pe.wait_ge(s_ld[3], 80)
            nc.tensor.transpose(ps_a1[0:DH, 0:M], wsl_nat, ident[0:M, 0:M]).then_inc(s_pe0, 1)
            nc.tensor.transpose(ps_a1[0:DH, 64:64 + DH], wv_nat, ident[0:DH, 0:DH]).then_inc(s_pe0, 1)
            nc.tensor.matmul(ps_a1[0:DH, 128:128 + DH], wq_nat, wk_nat, start=True, stop=True).then_inc(s_pe0, 1)
            pe.wait_ge(s_ld[1], 48)
            nc.tensor.transpose(ps_a1[:, 192:192 + S], pos_nat, ident[0:S, 0:S]).then_inc(s_pe0, 1)
            pe.wait_ge(s_dve0, DVE0["wslT"])
            nc.tensor.matmul(ps_f[:, 0:H * M], e_last, bsl_row.rearrange("p a n -> p (a n)"), start=True, stop=False)
            for h in range(H):
                last = nc.tensor.matmul(ps_f[:, h * M:(h + 1) * M], wx_nat[:, h, :], wslT, start=False, stop=(h == H - 1))
            last.then_inc(s_pe0, 1)
            pe.wait_ge(s_act0, TB)
            pe.wait_ge(s_dve0, DVE0["idA"])
            for h in range(H):
                last = nc.tensor.matmul(ps_a2[:, h * 128:(h + 1) * 128], wfx_nat[:, h, :], idA, start=True, stop=True)
            last.then_inc(s_pe0, 1)
            pe.wait_ge(s_ld[4], 48)
            wo4 = wout_nat.rearrange("p a (c n) -> p a c n", c=2)
            for k in range(4):
                last = nc.tensor.transpose(ps_a3[:, k * 128:(k + 1) * 128], wo4[:, k // 2, k % 2, :], ident[:, :])
            last.then_inc(s_pe0, 1)
            pe.wait_ge(s_dve0, DVE0["wva"])
            pe.wait_ge(s_ld[6], 32)

            def patch_products(i, p, slot):
                g = i
                if slot == 0:
                    upto(pe, s_hT, 1, g - 1)
                v = xbuf[p].rearrange("p (a n) -> p a n", n=PS)
                s0 = sum(T_SLOT[:slot])
                for s in range(s0, s0 + T_SLOT[slot]):
                    if s % TAIL == 0:
                        upto(pe, s_tail, C, g, s // TAIL + 1)
                    mm = nc.tensor.matmul(ps_t[:, 0:GI * NPP], w_tok[:, s, :], v[:, :, s],
                                          start=(s == 0), stop=(s == STEPS - 1))
                if slot == 7:
                    mm.then_inc(s_tok, 1)

            def scores(g, u, pq):
                b = u // 2
                upto(pe, s_km, UNITS, g, u + 1)
                if u == 0:
                    upto(pe, s_q, 1, g)
                upto(pe, s_s2, UNITS, g, u)
                nc.tensor.matmul(ps_s[0:S, 0:UW], qT[:, pq, b * S:(b + 1) * S],
                                 km[:, u % 2, :, :].rearrange("p h s -> p (h s)"), start=True, stop=True)\
                    .then_inc(s_s2p, 1)

            def exp_transposes(g, u):
                upto(pe, s_e2, UNITS, g, u + 1)
                upto(pe, s_eT, UNITS, g, u)
                for h in range(UH):
                    mm = nc.tensor.transpose(ps_e[0:S, h * S:(h + 1) * S], e2[:, u % 2, h * S:(h + 1) * S], ident[0:S, 0:S])
                mm.then_inc(s_eTp, 1)

            def contexts(g, u, pq):
                b, hf = u // 2, u % 2
                upto(pe, s_eT, UNITS, g, u + 1)
                if u == 0:
                    upto(pe, s_v2, 1, g)
                upto(pe, s_cx, UNITS, g, u - 1)
                c0 = 300 + (u % 2) * UH * VW
                for h in range(UH):
                    hd = hf * UH + h
                    mm = nc.tensor.matmul(ps_e[0:S, c0 + h * VW:c0 + (h + 1) * VW], eT[:, u % 2, h * S:(h + 1) * S],
                                          va[:, pq, b, hd * VW:(hd + 1) * VW], start=True, stop=True)
                mm.then_inc(s_cp, 1)

            def token_outputs(g, jc, pw):
                hh, jj = jc // 2, jc % 2
                if jc == 0:
                    upto(pe, s_osb, 2, g)
                    upto(pe, s_wT, 1, g)
                    upto(pe, s_h2, 1, g - 1)
                upto(pe, s_ox, 4, g, jc)
                for b in range(GI):
                    mm = nc.tensor.matmul(ps_a3[:, b * S:(b + 1) * S], osb[:, b * HH + hh, jj * 128:(jj + 1) * 128],
                                          wT[:, pw, b * HH + hh, :], start=True, stop=True)
                mm.then_inc(s_oxp, 1)

            def body(i, j, p):
                g1, g2, g3, f1, f2, f3 = i - 1, i - 2, i - 3, i - 4, i - 5, i - 6
                T, A1, A2, A3, F1, F2, F3 = (on(i, k) for k in range(7))
                for slot in range(8):
                    if F2:
                        scores(f2, slot, 1 - p)
                    if slot == 0:
                        if F3:
                            upto(pe, s_cx, UNITS, f3)
                            upto(pe, s_gt, 1, f3 - 1)
                            if F1:
                                upto(pe, s_v2, 1, f1 - 1)
                            for b in range(GI):
                                mm = nc.tensor.transpose(ps_f[:, b * S:(b + 1) * S], cx[:, b, :], ident[0:S, 0:S])
                            mm.then_inc(s_cTp, 1)
                        if A2:
                            upto(pe, s_w, 1, g2)
                            upto(pe, s_osb, 2, g2 - 1)
                            for q in range(Q):
                                c0 = (q // 4) * 512 + (q % 4) * S
                                mm = nc.tensor.transpose(ps_a2[:, c0:c0 + S],
                                                         w[:, q // HH, (q % HH) * 128:(q % HH) * 128 + 128], ident[0:S, 0:S])
                            mm.then_inc(s_wTp, 1)
                        if A1:
                            upto(pe, s_hT, 1, g1)
                            upto(pe, s_sub1, 2, g1 - 1)
                            for b in range(GI):
                                mm = nc.tensor.transpose(ps_a1[0:S, b * D:(b + 1) * D], hT[:, b, :], ident[:, :])
                            mm.then_inc(s_hps, 1)
                    if slot == 1:
                        if A2:
                            upto(pe, s_wT, 1, g2)
                            for q in range(Q):
                                mm = nc.tensor.matmul(ps_a2[:, q * 128:(q + 1) * 128],
                                                      w[:, q // HH, (q % HH) * 128:(q % HH) * 128 + 128],
                                                      xn[:, q // HH, :], start=True, stop=True)
                            mm.then_inc(s_gp, 1)
                        if F3:
                            upto(pe, s_cT, 1, f3)
                            for b in range(GI):
                                mm = nc.tensor.matmul(ps_f[0:S, b * D:(b + 1) * D], cxT[:, b * S:(b + 1) * S], wo_sb[:, :],
                                                      start=True, stop=True)
                            mm.then_inc(s_saP, 1)
                    if slot == 2:
                        if A1:
                            upto(pe, s_xn, 1, g1)
                            for b in range(GI):
                                mm = nc.tensor.transpose(ps_a1[:, b * S:(b + 1) * S], xn[:, b, :], ident[0:S, 0:S])
                            mm.then_inc(s_xnTp, 1)
                        if A2:
                            upto(pe, s_gn, 1, g2)
                            for q in range(Q):
                                mm = nc.tensor.transpose(ps_a2[:, q * 128:(q + 1) * 128], gn[:, q, :], ident[:, :])
                            mm.then_inc(s_gTp, 1)
                        if F1:
                            upto(pe, s_xa, 1, f1)
                            upto(pe, s_r3, 1, f3)
                            upto(pe, s_v2, 1, f1 - 1)
                            for b in range(GI):
                                mm = nc.tensor.transpose(ps_f[:, b * S:(b + 1) * S], xa[:, b, :], ident[0:S, 0:S])
                            mm.then_inc(s_xaTp, 1)
                    if slot == 3:
                        if A1:
                            upto(pe, s_xnT, 1, g1)
                            for b in range(2):
                                mm = nc.tensor.matmul(ps_a1[0:S, b * 256:(b + 1) * 256], xnT[:, b * S:(b + 1) * S], w_log[:, :],
                                                      start=True, stop=True)
                            mm.then_inc(s_lg, 1)
                        if A2:
                            upto(pe, s_gT, 1, g2)
                            for h in range(H):
                                mm = nc.tensor.matmul(ps_a2[:, h * 128:(h + 1) * 128], w_stp[:, h, :],
                                                      gnT[:, :, h // 4, h % 4, :], start=True, stop=True)
                            mm.then_inc(s_stp, 1)
                        if F1:
                            upto(pe, s_xaT, 1, f1)
                            nc.tensor.matmul(ps_f[:, 0:R], wq_aug[:, :], xaT[:, :], start=True, stop=True).then_inc(s_qp, 1)
                    if slot == 4:
                        if A1:
                            upto(pe, s_sub1, 2, g1, 1)
                            for b in range(2):
                                mm = nc.tensor.matmul(ps_a1[0:S, b * 256:(b + 1) * 256], xnT[:, (b + 2) * S:(b + 3) * S], w_log[:, :],
                                                      start=True, stop=True)
                            mm.then_inc(s_lg, 1)
                        if A2:
                            upto(pe, s_stT, 1, g2)
                            upto(pe, s_pT, 1, g2)
                            for q in range(Q):
                                mm = nc.tensor.matmul(ps_a2[:, q * 128:(q + 1) * 128], pT[:, q * 128:(q + 1) * 128],
                                                      stT[:, q * 128:(q + 1) * 128], start=True, stop=True)
                            mm.then_inc(s_scp, 1)
                        if F1:
                            upto(pe, s_q, 1, f1)
                            nc.tensor.matmul(ps_f[:, 0:R], wk_aug[:, :], xaT[:, :], start=True, stop=True).then_inc(s_kp, 1)
                    if slot == 5:
                        if A2:
                            upto(pe, s_sc, 1, g2)
                            for q in range(Q):
                                mm = nc.tensor.matmul(ps_a2[:, q * DH:(q + 1) * DH], stT[:, q * 128:(q + 1) * 128],
                                                      wvT[:, :], start=True, stop=True)
                            mm.then_inc(s_vp, 1)
                        if F1:
                            upto(pe, s_k, 1, f1)
                            for b in range(GI):
                                mm = nc.tensor.matmul(ps_f[0:S, b * D:(b + 1) * D], xaT[:, b * S:(b + 1) * S], wv_aug[:, :],
                                                      start=True, stop=True)
                            mm.then_inc(s_vp2, 1)
                    if slot == 6 and F3:
                        upto(pe, s_t, 1, f3)
                        if F1:
                            upto(pe, s_v2, 1, f1)
                        for b in range(GI):
                            mm = nc.tensor.transpose(ps_f[:, b * S:(b + 1) * S], ts[:, b, :], ident[0:S, 0:S])
                        mm.then_inc(s_tTp, 1)
                    if slot == 7:
                        if A2:
                            upto(pe, s_bd, 1, g2)
                            upto(pe, s_v, 1, g2)
                            for q in range(Q):
                                mm = nc.tensor.matmul(ps_a2[:, 512 + q * DH:512 + (q + 1) * DH], bd[:, q, :], v_sb[:, q, :],
                                                      start=True, stop=True)
                            mm.then_inc(s_osp, 1)
                        if F3:
                            upto(pe, s_tT, 1, f3)
                            for b in range(GI):
                                mm = nc.tensor.matmul(ps_f[0:S, b * E:(b + 1) * E], tT[:, b * S:(b + 1) * S], wg_sb[:, :],
                                                      start=True, stop=True)
                            mm.then_inc(s_gtp, 1)
                    if F2:
                        exp_transposes(f2, slot)
                    if A3:
                        if slot < 4:
                            token_outputs(g3, slot, 1 - p)
                        if slot == 4:
                            upto(pe, s_ox, 4, g3)
                            for jc in range(4):
                                mm = nc.tensor.matmul(ps_a3[:, 0:R], woutT[:, jc, :], oxT[:, jc, :],
                                                      start=(jc == 0), stop=(jc == 3))
                            mm.then_inc(s_oTp, 1)
                        if slot == 5:
                            upto(pe, s_oTr, 1, g3)
                            for b in range(GI):
                                mm = nc.tensor.transpose(ps_a3[0:S, b * D:(b + 1) * D], oT[:, b * S:(b + 1) * S], ident[:, :])
                            mm.then_inc(s_hp2, 1)
                    if T:
                        patch_products(i, p, slot)
                    if F2:
                        contexts(f2, slot, 1 - p)

            bodies(pe, body)
            pe_tail(pe)

        @block.scalar
        def _(act):
            act.preload_act_table(ACT.Exp)
            wt4 = w_tok[:, :, :].rearrange("p s n -> p (s n)")
            for k in range(TB):
                act.wait_ge(s_pe0, k + 1)
                n = min(4, STEPS - 4 * k) * 128
                nc.scalar.activation(wt4[:, 512 * k:512 * k + n], ps_a2[:, (k % 2) * 512:(k % 2) * 512 + n], ACT.Copy)\
                    .then_inc(s_act0, 1)

            def copy(dst, src, s):
                nc.scalar.activation(dst, src, ACT.Copy).then_inc(s, 1)

            def body(i, j, p):
                g1, g2, g3, f1, f2, f3 = i - 1, i - 2, i - 3, i - 4, i - 5, i - 6
                T, A1, A2, A3, F1, F2, F3 = (on(i, k) for k in range(7))
                for slot in range(8):
                    if slot == 0:
                        if F3:
                            upto(act, s_cTp, 1, f3)
                            upto(act, s_saP, 1, f3 - 1)
                            copy(cxT[:, :], ps_f[:, 0:R], s_cT)
                        if A2:
                            upto(act, s_wTp, 1, g2)
                            upto(act, s_oxp, 4, g2 - 2)
                            copy(wT[:, p, :, :].rearrange("p (a q) s -> p a (q s)", a=2),
                                 ps_a2[:, :].rearrange("p (a n) -> p a n", a=2)[:, :, 0:4 * S], s_wT)
                    if F2:
                        upto(act, s_s2, UNITS, f2, slot + 1)
                        nc.scalar.activation(e2[:, slot % 2, :], e2[:, slot % 2, :], ACT.Exp).then_inc(s_e2, 1)
                    if slot == 0 and A1:
                        upto(act, s_hT, 1, g1)
                        dst = hT_all[:, bass.ds(g1, 1), :] if not isinstance(g1, int) else hT_all[:, g1:g1 + 1, :]
                        copy(dst, hT[:, :, :].rearrange("p b s -> p (b s)").unsqueeze(1), s_hTc)
                    if slot == 1 and F1:
                        upto(act, s_x2, 1, f1)
                        upto(act, s_xaTp, 1, f1 - 1)
                        src = t_all[:, bass.ds(f1 * GI, GI), 0:D - 1] if not isinstance(f1, int) \
                            else t_all[:, f1 * GI:(f1 + 1) * GI, 0:D - 1]
                        copy(xa[:, :, 0:D - 1], src, s_xa)
                    if slot == 2:
                        if A1:
                            upto(act, s_xnTp, 1, g1)
                            upto(act, s_lg, 2, g1 - 1)
                            copy(xnT[:, :], ps_a1[:, 0:R], s_xnT)
                        if A2:
                            upto(act, s_gTp, 1, g2)
                            copy(gn[:, :, :].rearrange("p q n -> p (q n)"), ps_a2[:, :], s_gT)
                        if F1:
                            upto(act, s_xaTp, 1, f1)
                            upto(act, s_vp2, 1, f1 - 1)
                            copy(xaT[:, :], ps_f[:, 0:R], s_xaT)
                    if slot == 3:
                        if A2:
                            upto(act, s_stp, 1, g2)
                            copy(stT.rearrange("p (b h m) -> p h b m", b=GI, h=H),
                                 ps_a2[0:DH, :].rearrange("p (h b m) -> p h b m", b=GI, h=H), s_stT)
                        if F1:
                            upto(act, s_qp, 1, f1)
                            upto(act, s_s2p, UNITS, f1 - 2)
                            copy(qT[:, p, :], ps_f[:, 0:R], s_q)
                    if slot == 4:
                        if F1:
                            upto(act, s_kp, 1, f1)
                            upto(act, s_km, UNITS, f1 - 2)
                            copy(kT[:, p, :], ps_f[:, 0:R], s_k)
                        if A1:
                            upto(act, s_sub1, 2, g1, 1)
                            nc.scalar.activation(w[:, 0:2, :], w[:, 0:2, :], ACT.Exp).then_inc(s_exp1, 1)
                    if slot == 5:
                        if A2:
                            upto(act, s_vp, 1, g2)
                            upto(act, s_osp, 1, g2 - 1)
                            copy(v_sb[:, :, :].rearrange("p q n -> p (q n)"), ps_a2[:, 0:Q * DH], s_v)
                            upto(act, s_asub, 1, g2)
                            nc.scalar.activation(sc[:, :, :], sc[:, :, :], ACT.Exp).then_inc(s_aexp, 1)
                        if F1:
                            upto(act, s_vp2, 1, f1)
                            upto(act, s_cp, UNITS, f1 - 2)
                            copy(va[:, p, :, :].rearrange("p b (h n) -> p (b h) n", n=VW)[:, :, 0:DH2],
                                 ps_f[0:S, :].rearrange("p (a n) -> p a n", n=DH2), s_v2)
                        if A1:
                            upto(act, s_sub1, 2, g1)
                            nc.scalar.activation(w[:, 2:4, :], w[:, 2:4, :], ACT.Exp).then_inc(s_exp1, 1)
                    if slot == 6 and F3:
                        upto(act, s_tTp, 1, f3)
                        upto(act, s_gtp, 1, f3 - 1)
                        copy(tT[:, :], ps_f[:, 0:R], s_tT)
                        dst = t_all[:, bass.ds(f3 * GI, GI), :] if not isinstance(f3, int) \
                            else t_all[:, f3 * GI:(f3 + 1) * GI, :]
                        copy(dst, ts[:, :, :], s_tk)
                    if F2:
                        upto(act, s_eTp, UNITS, f2, slot + 1)
                        upto(act, s_cp, UNITS, f2, slot - 1)
                        copy(eT[:, slot % 2, :], ps_e[0:S, 0:UW], s_eT)
                    if A3 and slot < 4:
                        upto(act, s_oxp, 4, g3, slot + 1)
                        upto(act, s_oTp, 1, g3 - 1)
                        copy(oxT[:, slot, :], ps_a3[:, 0:R], s_ox)
                    if A3 and slot == 4:
                        upto(act, s_oTp, 1, g3)
                        upto(act, s_hp2, 1, g3 - 1)
                        nc.scalar.activation(oT[:, :], ps_a3[:, 0:R], ACT.Identity, bias=bout_col[:, :]).then_inc(s_oT, 1)
                    if slot == 7 and A2:
                        upto(act, s_osp, 1, g2)
                        upto(act, s_oxp, 4, g2 - 1)
                        for hl in (0, 1):
                            a = nc.scalar.activation(osb[32 * hl:32 * hl + 32, :, hl * DH:(hl + 1) * DH],
                                                     ps_a2[32 * hl:32 * hl + 32, 512:1024].rearrange("p (q n) -> p q n", q=Q),
                                                     ACT.Copy)
                        a.then_inc(s_osb, 1)

            act.wait_ge(s_zero, 16)
            bodies(act, body)
            act_tail(act)

        @block.vector
        def _(dve):
            v = nc.vector
            n0 = [0]

            def step(ins, name=None):
                n0[0] += 1
                if name is not None:
                    assert DVE0[name] == n0[0], (name, n0[0])
                ins.then_inc(s_dve0, 1)
                dve.wait_ge(s_dve0, n0[0])

            v.memset(xbuf[0], 0.0).then_inc(s_xz, 1)
            step(v.memset(osb[:, :, :], 0.0), "zeros")
            step(v.memset(bd[:, :, :], 0.0), "gaps")
            step(v.memset(xn[:, :, D - 1:D], 1.0), "aug1")
            step(v.memset(xa[:, :, D - 1:D], 1.0), "aug2")
            step(v.memset(va[:, :, :, :].rearrange("p a b n -> p (a b n)"), 1.0), "aug3")
            step(v.memset(wpad, 0.0), "pad_zero")
            dve.wait_ge(s_ld[0], 16)
            wn = wtok_nat.rearrange("p (c y x) -> p c y x", c=C, y=PS)
            wp = wpad.rearrange("p (s n) -> p s n", s=STEPS)
            for c in range(C):
                v.tensor_copy(wp[:, :, 32 * c:32 * c + PS], wn[:, c, :, 0:STEPS].rearrange("p y x -> p x y"))
                last = v.tensor_copy(wp[:, c * TAIL:(c + 1) * TAIL, 96:96 + PS],
                                     wn[:, c, :, STEPS:PS].rearrange("p y x -> p x y"))
            step(last, "wpad")
            dve.wait_ge(s_ld[2], 64)
            for nat, bias, n1, n2 in ((wx_nat, bx_nat, "wx1", "wx2"), (wfx_nat, bfx_nat, "wfx1", "wfx2")):
                step(v.tensor_tensor(nat[:, :, 0:D - 1], nat[:, :, 0:D - 1],
                                     nat[:, :, D - 1:D].broadcast_to([DH, H, D - 1]), ALU.subtract), n1)
                step(v.tensor_copy(nat[:, :, D - 1:D], bias.unsqueeze(2)), n2)
            dve.wait_ge(s_pool0, 8)
            v.memset(e_last[:, 0:D - 1], 0.0)
            v.memset(e_last[:, D - 1:D], 1.0)
            dve.wait_ge(s_pe0, TB + PE0["pos"])
            v.tensor_copy(idA[:, 0:DH], ident[0:DH, 0:DH])
            step(v.tensor_copy(wslT, ps_a1[0:DH, 0:M]), "wslT")
            step(v.tensor_copy(wvT[:, :], ps_a1[0:DH, 64:64 + DH]), "wvT")
            step(v.tensor_scalar(idA[:, DH:2 * DH], ps_a1[0:DH, 128:128 + DH], float(DH) ** -0.5, None, ALU.mult), "idA")
            step(v.tensor_copy(posT[:, :], ps_a1[:, 192:192 + S]), "pos")
            dve.wait_ge(s_ld[1], 48)
            step(v.tensor_scalar(hT[:, :, 0:1], posT[:, 0:1].unsqueeze(1).broadcast_to([D, GI, 1]), cls_col, None, ALU.mult), "cls")
            dve.wait_ge(s_ld[4], 48)
            step(v.reciprocal(itemp, temp_bc), "itemp")
            dve.wait_ge(s_pe0, TB + PE0["wlog"])
            step(v.tensor_tensor(w_log[:, :].rearrange("p (h m) -> p h m", h=H),
                                 ps_f[:, 0:H * M].rearrange("p (h m) -> p h m", h=H),
                                 itemp.unsqueeze(2).broadcast_to([D, H, M]), ALU.mult), "wlog")
            dve.wait_ge(s_pe0, TB + PE0["wstp"])
            step(v.tensor_copy(w_stp[:, :, :].rearrange("p h n -> p (h n)"), ps_a2[:, :]), "wstp")
            dve.wait_ge(s_pe0, TB + PE0["wout"])
            step(v.tensor_copy(woutT[:, :, :].rearrange("p h n -> p (h n)"), ps_a3[:, :]), "wout")
            dve.wait_ge(s_ld[5], 9 * 16)
            step(v.tensor_scalar(neg_keep, ident[:, D - 1:D], -1.0, None, ALU.add), "negk")
            step(v.scalar_tensor_tensor(wq_aug[:, :], lastq, neg_keep, natq, ALU.mult, ALU.add), "wqa")
            step(v.tensor_scalar(wq_aug[:, :], wq_aug[:, :], float(DH2) ** -0.5, None, ALU.mult), "wqs")
            step(v.scalar_tensor_tensor(wk_aug[:, :], lastk, neg_keep, natk, ALU.mult, ALU.add), "wka")
            step(v.scalar_tensor_tensor(wv_aug[:, :], lastv, neg_keep, natv, ALU.mult, ALU.add), "wva")
            v.memset(xbuf[1], 0.0).then_inc(s_xz, 1)
            dve.wait_ge(s_ld[7], 96)
            dve.wait_ge(s_zero, 16)

            def norm_stats(name, src, s_chain, g):
                st, mv, ve, _ = lnb[name]
                for b in range(GI):
                    ins = v.bn_stats(st[0:S, b, :], src[:, b, :])
                ins.then_inc(s_chain, 1)
                upto(dve, s_chain, 3, g, 1)
                v.memset(pause[0:S, :], 0.0)
                for b in range(GI):
                    ins = v.bn_aggr(mv[0:S, b, :], st[0:S, b, :])
                ins.then_inc(s_chain, 1)
                upto(dve, s_chain, 3, g, 2)
                v.tensor_scalar(ve[0:S, :].unsqueeze(2), mv[0:S, :, 1:2], EPS, None, ALU.add).then_inc(s_chain, 1)

            def norm_apply(name, dst, src, cols, s_r, s_done, g):
                _, mv, _, rs = lnb[name]
                upto(dve, s_r, 1, g)
                for b in range(GI):
                    ins = v.tensor_scalar(dst(b), src[:, b, 0:cols], mv[0:S, b, 0:1], rs[0:S, b:b + 1],
                                          ALU.subtract, ALU.mult)
                ins.then_inc(s_done, 1)

            def pixel_tails(n, p):
                dve.wait_ge(s_x[p], n * 16 * C * GI)
                px = xbuf[p].rearrange("p (a n) -> p a n", n=PS)
                for c in range(C):
                    v.tensor_copy(px[96:96 + PS, :, c * TAIL:(c + 1) * TAIL],
                                  px[32 * c:32 * c + PS, :, STEPS:PS]).then_inc(s_tail, 1)

            pixel_tails(1, 0)

            def body(i, j, p):
                g1, g2, g3, f1, f2, f3 = i - 1, i - 2, i - 3, i - 4, i - 5, i - 6
                T, A1, A2, A3, F1, F2, F3 = (on(i, k) for k in range(7))
                psh = ps_a1[0:S, :].rearrange("p (b n) -> p b n", b=GI)
                for slot in range(8):
                    if slot == 0 and A1:
                        upto(dve, s_tok, 1, g1)
                        upto(dve, s_hps, 1, g1 - 1)
                        upto(dve, s_hTc, 1, g1 - 1)
                        v.scalar_tensor_tensor(hT[:, :, 1:S], ps_t[:, 0:GI * NPP].rearrange("p (b n) -> p b n", b=GI),
                                               b_tok[:, :], posT[:, 1:S].unsqueeze(1).broadcast_to([D, GI, NPP]),
                                               ALU.add, ALU.mult).then_inc(s_hT, 1)
                    if F2:
                        sv = ps_s[0:S, 0:UW].rearrange("p (h n) -> p h n", h=UH)
                        upto(dve, s_s2p, UNITS, f2, slot + 1)
                        v.tensor_reduce(mx2[:, slot % 2, :], sv, AX, ALU.max).then_inc(s_s2m, 1)
                        upto(dve, s_s2m, UNITS, f2, slot + 1)
                        upto(dve, s_eTp, UNITS, f2, slot - 1)
                        v.tensor_tensor(e2[:, slot % 2, :].rearrange("p (h n) -> p h n", h=UH), sv,
                                        mx2[:, slot % 2, :].unsqueeze(2).broadcast_to([S, UH, S]), ALU.subtract)\
                            .then_inc(s_s2, 1)
                    if slot == 0:
                        if F1:
                            upto(dve, s_h2, 1, f1)
                            norm_stats("f1", h2[:, p, :, :], s_f1c, f1)
                        if A1:
                            upto(dve, s_hps, 1, g1)
                            norm_stats("a1", psh, s_a1c, g1)
                        if F1:
                            def dst(b, g=f1):
                                return t_all[:, bass.ds(g * GI + b, 1), :].rearrange("p o n -> p (o n)") \
                                    if not isinstance(g, int) else t_all[:, g * GI + b, :]
                            norm_apply("f1", dst, h2[:, p, :, :], D, s_f1r, s_x2, f1)
                    if slot == 1:
                        if A2:
                            gp = ps_a2[:, :].rearrange("p (q n) -> p q n", q=Q)
                            upto(dve, s_gp, 1, g2)
                            v.tensor_scalar(rn[:, :].unsqueeze(2), gp[:, :, D - 1:D], EPS, None, ALU.add).then_inc(s_gc, 1)
                            upto(dve, s_gc, 2, g2, 1)
                            v.reciprocal(rn[:, :], rn[:, :]).then_inc(s_gc, 1)
                            upto(dve, s_gc, 2, g2)
                            upto(dve, s_vp, 1, g2 - 1)
                            v.tensor_tensor(gn[:, :, :], gp, rn[:, :].unsqueeze(2).broadcast_to([128, Q, 128]),
                                            ALU.mult).then_inc(s_gn, 1)
                        if A1:
                            upto(dve, s_gp, 1, g2)
                            norm_apply("a1", lambda b: xn[:, b, 0:D - 1], psh, D - 1, s_a1r, s_xn, g1)
                        if F3:
                            upto(dve, s_saP, 1, f3)
                            upto(dve, s_xr, 1, f3)
                            v.tensor_tensor(xr[:, :, :], ps_f[0:S, :].rearrange("p (b n) -> p b n", b=GI), xr[:, :, :],
                                            ALU.add).then_inc(s_r3, 1)
                    if slot == 2 and F3:
                        upto(dve, s_r3, 1, f3)
                        norm_stats("f3", xr[:, :, :], s_f3c, f3)
                    if slot == 3:
                        if A1:
                            self_max(dve, v, g1, 0)
                        if A2:
                            upto(dve, s_stp, 1, g2)
                            v.tensor_copy(pT[:, :].rearrange("p (b h m) -> p h b m", b=GI, h=H),
                                          ps_a2[DH:2 * DH, :].rearrange("p (h b m) -> p h b m", b=GI, h=H)).then_inc(s_pT, 1)
                        if F3:
                            norm_apply("f3", lambda b: xr[:, b, :], xr[:, :, :], D, s_f3r, s_tn, f3)
                    if slot == 4:
                        if A1:
                            self_max(dve, v, g1, 1)
                        if A2:
                            upto(dve, s_scp, 1, g2)
                            gp = ps_a2[:, :].rearrange("p (q n) -> p q n", q=Q)
                            for hl in range(4):
                                ins = v.tensor_copy(sc[32 * hl:32 * hl + 32, :, :], gp[32 * hl:32 * hl + 32, :, 32 * hl:32 * hl + 32])
                            ins.then_inc(s_sc, 1)
                            upto(dve, s_sc, 1, g2)
                            v.tensor_reduce(smx[:, :], sc[:, :, :], AX, ALU.max).then_inc(s_ac, 1)
                            upto(dve, s_ac, 4, g2, 1)
                            v.tensor_tensor(sc[:, :, :], sc[:, :, :], smx[:, :].unsqueeze(2).broadcast_to([128, Q, M]),
                                            ALU.subtract).then_inc(s_asub, 1)
                    if slot == 5:
                        if A1:
                            wv_ = w[:, :, :].rearrange("p b (h m) -> p (b h) m", m=M)
                            upto(dve, s_exp1, 2, g1)
                            v.tensor_reduce(mx1[:, :], wv_, AX, ALU.add).then_inc(s_wc, 1)
                            upto(dve, s_wc, 2, g1, 1)
                            v.reciprocal(mx1[:, :], mx1[:, :]).then_inc(s_wc, 1)
                            upto(dve, s_wc, 2, g1)
                            v.tensor_tensor(wv_, wv_, mx1[:, :].unsqueeze(2).broadcast_to([S, GI * H, M]), ALU.mult).then_inc(s_w, 1)
                        if A2:
                            upto(dve, s_aexp, 1, g2)
                            v.tensor_reduce(smx[:, :], sc[:, :, :], AX, ALU.add).then_inc(s_ac, 1)
                            upto(dve, s_ac, 4, g2, 2)
                            v.reciprocal(smx[:, :], smx[:, :]).then_inc(s_ac, 1)
                            upto(dve, s_ac, 4, g2, 3)
                            v.tensor_tensor(sc[:, :, :], sc[:, :, :], smx[:, :].unsqueeze(2).broadcast_to([128, Q, M]),
                                            ALU.mult).then_inc(s_ac, 1)
                            upto(dve, s_ac, 4, g2)
                            upto(dve, s_osp, 1, g2 - 1)
                            for hl in range(4):
                                ins = v.transpose(bd[32 * hl:32 * hl + 32, :, 32 * hl:32 * hl + 32], sc[32 * hl:32 * hl + 32, :, :])
                            ins.then_inc(s_bd, 1)
                        if A3:
                            upto(dve, s_oT, 1, g3)
                            upto(dve, s_hTc, 1, g3)
                            hv = hT_all[:, bass.ds(g3, 1), :].rearrange("p o n -> p (o n)") if not isinstance(g3, int) \
                                else hT_all[:, g3, :]
                            v.tensor_tensor(oT[:, :], oT[:, :], hv, ALU.add).then_inc(s_oTr, 1)
                    if slot == 6 and T and (not isinstance(i, int) or i + 1 < G):
                        pixel_tails((i + 1) // 2 + 1 if isinstance(i, int) else j + p + 1, 1 - p)
                    if slot == 6 and A3:
                        upto(dve, s_hp2, 1, g3)
                        upto(dve, s_x2, 1, g3 - 2)
                        if not isinstance(g3, int) or g3 >= 2:
                            dve.wait_ge(s_hst[1 - p], 16 * ((g3 - 2) // 2 + 1 if isinstance(g3, int) else j - 2 + p))
                        v.tensor_copy(h2[:, 1 - p, :, :], ps_a3[0:S, :].rearrange("p (b n) -> p b n", b=GI)).then_inc(s_h2, 1)
                    if slot == 7:
                        if A2:
                            upto(dve, s_osp, 1, g2)
                            upto(dve, s_oxp, 4, g2 - 1)
                            for hl in (2, 3):
                                ins = v.tensor_copy(osb[32 * hl:32 * hl + 32, :, hl * DH:(hl + 1) * DH],
                                                    ps_a2[32 * hl:32 * hl + 32, 512:1024].rearrange("p (q n) -> p q n", q=Q))
                            ins.then_inc(s_osb, 1)
                        if F3:
                            upto(dve, s_gtp, 1, f3)
                            dst = gl_all[:, bass.ds(f3 * GI, GI), :] if not isinstance(f3, int) \
                                else gl_all[:, f3 * GI:(f3 + 1) * GI, :]
                            v.tensor_tensor(dst, ps_f[0:S, 0:GI * E].rearrange("p (b n) -> p b n", b=GI),
                                            bg_bc[:, :].unsqueeze(1).broadcast_to([S, GI, E]), ALU.add).then_inc(s_gt, 1)
                    if F2:
                        c0 = 300 + (slot % 2) * UH * VW
                        cv = ps_e[0:S, c0:c0 + UH * VW].rearrange("p (h n) -> p h n", h=UH)
                        upto(dve, s_cp, UNITS, f2, slot + 1)
                        v.reciprocal(mx2[:, slot % 2, :].unsqueeze(2), cv[:, :, DH2:VW]).then_inc(s_cr, 1)
                        upto(dve, s_cr, UNITS, f2, slot + 1)
                        if slot == 0:
                            upto(dve, s_cTp, 1, f2 - 1)
                        b, hf = slot // 2, slot % 2
                        v.tensor_tensor(cx[:, b, hf * UH * DH2:(hf + 1) * UH * DH2].rearrange("p (h n) -> p h n", h=UH),
                                        cv[:, :, 0:DH2], mx2[:, slot % 2, :].unsqueeze(2).broadcast_to([S, UH, DH2]), ALU.mult)\
                            .then_inc(s_cx, 1)

            def self_max(dve, v, g1, r):
                lv = ps_a1[0:S, :].rearrange("p (a m) -> p a m", m=M)
                upto(dve, s_lg, 2, g1, r + 1)
                v.tensor_reduce(mx1[:, 2 * r * H:(2 * r + 2) * H], lv, AX, ALU.max).then_inc(s_mx1, 1)
                upto(dve, s_mx1, 2, g1, r + 1)
                upto(dve, s_gp, 1, g1 - 1)
                v.tensor_tensor(w[:, 2 * r:2 * r + 2, :].rearrange("p b (h m) -> p (b h) m", m=M), lv,
                                mx1[:, 2 * r * H:(2 * r + 2) * H].unsqueeze(2).broadcast_to([S, 2 * H, M]), ALU.subtract)\
                    .then_inc(s_sub1, 1)

            for i in range(LOOP0):
                body(i, i // 2, i % 2)
            with dve.Fori(LOOP0 // 2, G // 2 - 1, 1) as j:
                for p in range(2):
                    body(j * 2 + p, j, p)
            for i in range(G - 2, LAST):
                body(i, i // 2, i % 2)
            dve_tail(dve)



_INS = ['x', 'L0_tok_W', 'L0_tok_b', 'L0_tok_class_token', 'L0_tok_pos_embed',
        'L0_attn_Wx', 'L0_attn_bx', 'L0_attn_Wfx', 'L0_attn_bfx', 'L0_attn_Wslice', 'L0_attn_bslice',
        'L0_attn_Wq', 'L0_attn_Wk', 'L0_attn_Wv', 'L0_attn_Wout', 'L0_attn_bout', 'L0_attn_temperature',
        'L0_ffn_Wq', 'L0_ffn_bq', 'L0_ffn_Wk', 'L0_ffn_bk', 'L0_ffn_Wv', 'L0_ffn_bv', 'L0_ffn_Wo', 'L0_ffn_bo',
        'L0_ffn_g1', 'L0_ffn_beta1', 'L0_ffn_g2', 'L0_ffn_beta2', 'L0_ffn_Wg', 'L0_ffn_bg',
        'L0_ffn_W1', 'L0_ffn_b1', 'L0_ffn_W2', 'L0_ffn_b2']
_OUTS = [((64, 65, 128), 'float32')]


def kernel(**inputs):
    import numpy as _np
    import concourse.bacc as _bacc
    from concourse import mybir as _mybir
    from concourse.bass_utils import run_bass_kernel_spmd as _run

    nc = _bacc.Bacc("TRN2", target_bir_lowering=False, num_devices=1)
    arrays, args = {}, []
    for name in _INS:
        a = _np.ascontiguousarray(inputs[name])
        arrays[f"in_{name}"] = a
        args.append(nc.dram_tensor(f"in_{name}", a.shape, _mybir.dt.from_np(a.dtype), kind="ExternalInput").ap())
    for i, (shape, dtype) in enumerate(_OUTS):
        dt = _mybir.dt.from_np(_np.dtype(dtype))
        args.append(nc.dram_tensor(f"out_{i}", shape, dt, kind="ExternalOutput").ap())
    vit_tower_kernel(nc, *args)
    r = _run(nc, [arrays], core_ids=[0])
    return r.results[0]["out_0"]
```

```python
import concourse.bass as bass
from concourse import mybir
from contextlib import ExitStack


def vit_tower_kernel(nc, x, tok_w, tok_b, tok_cls, tok_pos,
                     wx, bx, wfx, bfx, wslice, bslice, wq, wk, wv, wout, bout, temp,
                     f_wq, f_bq, f_wk, f_bk, f_wv, f_bv, f_wo, f_bo, g1, beta1, g2, beta2,
                     wg, bg, w1, b1, w2, b2, out):
    fp32 = mybir.dt.float32
    int32 = mybir.dt.int32
    uint32 = mybir.dt.uint32
    ALU = mybir.AluOpType
    ACT = mybir.ActivationFunctionType
    AX = mybir.AxisListType.X

    B, C, IMG, _ = x.shape
    D = tok_w.shape[0]
    S = tok_pos.shape[0]
    NP = 8
    PS = IMG // NP
    NPP = NP * NP
    GI = 4
    G = B // GI
    R = GI * S
    H, M = temp.shape[1], wslice.shape[0]
    DH = wslice.shape[1]
    HH = H // 4
    Q = GI * HH
    DH2 = D // H
    E, _, HID = w1.shape
    HC = HID // D
    TAIL = PS // (C + 1)
    STEPS = PS - TAIL
    assert C == 3 and STEPS == C * TAIL and 4 * M == 128 and D == 128
    T128 = 128
    NT = (B * S) // T128 + E
    EPS = 1e-5
    UNITS = 2 * GI
    UH = H // 2
    UW = UH * S
    VW = DH2 + 1
    T_SLOT = [2, 2, 2, 3, 3, 3, 3, 3]
    T_FIRST = [0, 1, 1, 2, 2, 2, 1, 3]
    RANK0 = 300
    assert sum(T_SLOT) == STEPS and G % 2 == 0 and G >= 10
    LOOP0 = 8
    LAST = G + 7
    RW = D + 4
    REG = -(-(B * S) // T128) * T128 + T128
    NONE = E * REG
    BLANK = 2 * E * T128

    ctx = ExitStack()
    with ctx:
        def sb(name, shape, dt=fp32):
            return ctx.enter_context(nc.sbuf_tensor(name, shape, dt))

        def ps(name, cols=512):
            return ctx.enter_context(nc.psum_tensor(name, [128, cols], fp32))

        def sem(name):
            return ctx.enter_context(nc.semaphore(name))

        xs_dram = nc.dram_tensor("rows_by_expert", (E * REG + E * T128, RW), fp32, kind="Internal").ap()
        blank_dram = nc.dram_tensor("blank_rows", (E * T128, RW), fp32, kind="Internal").ap()
        h_dram = nc.dram_tensor("h_rows", (B * S + BLANK, D), fp32, kind="Internal").ap()

        XCOLS = GI * NP * IMG
        arena = sb("arena", [128, 2 * XCOLS])
        xbuf = [arena[:, p * XCOLS:(p + 1) * XCOLS] for p in range(2)]
        W1C = HID + HC
        w1_sb = arena[:, 0:E * W1C].rearrange("p (e n) -> p e n", e=E)
        a0 = E * W1C
        w2_sb = arena[:, a0:a0 + E * HID].rearrange("p (e c n) -> p e c n", e=E, c=HC)
        a0 += E * HID
        b2_bc = arena[:, a0:a0 + E * D].rearrange("p (e n) -> p e n", e=E)
        b1_nat = arena[0:E * HC, a0 + E * D:a0 + E * D + D]
        o = [XCOLS]

        def setup_buf(cols, parts=128):
            o[0] += cols
            assert o[0] <= 2 * XCOLS
            return arena[0:parts, o[0] - cols:o[0]]

        x_all = sb("x_all", [S, B, D])
        hT_all = sb("hT_all", [D, G, R])

        ident = sb("ident", [128, 128])
        ones = sb("ones", [S, 128])
        triu = sb("triu", [S, S])
        head_mask = sb("head_mask", [128, H])
        mhalf = sb("mhalf", [128, GI])
        w_tok = sb("w_tok", [128, STEPS, D])
        b_tok = sb("b_tok", [D, 1])
        posT = sb("posT", [D, S])
        w_log = sb("w_log", [D, H * M])
        w_stp = sb("w_stp", [D, H, 2 * DH])
        wvT = sb("wvT", [DH, DH])
        woutT = sb("woutT", [128, 4, D])
        bout_col = sb("bout_col", [D, 1])
        wq_aug = sb("wq_aug", [D, D])
        wk_aug = sb("wk_aug", [D, D])
        wv_aug = sb("wv_aug", [D, D])
        wo_sb = sb("wo_sb", [D, D])
        wg_sb = sb("wg_sb", [D, E])
        bo_bc = sb("bo_bc", [S, D])
        g1_bc = sb("g1_bc", [S, D])
        beta1_bc = sb("beta1_bc", [S, D])
        g2_bc = sb("g2_bc", [128, D])
        beta2_bc = sb("beta2_bc", [128, D])
        bg_bc = sb("bg_bc", [S, E])

        hT = sb("hT", [D, GI, S])
        xn = sb("xn", [S, GI, D])
        xnT = sb("xnT", [D, R])
        w = sb("w", [S, GI, H * M])
        mx1 = sb("mx1", [S, GI * H])
        wT = sb("wT", [128, 2, Q, S])
        gn = sb("gn", [128, Q, 128])
        gnT = gn[:, :, :].rearrange("p (b hh) (hl m) -> p b hh hl m", b=GI, hl=4)
        stT = gn[0:DH, :, :].rearrange("p q n -> p (q n)")
        pT = sb("pT", [DH, GI * H * M])
        rn = sb("rn", [128, Q])
        sc = sb("sc", [128, Q, M])
        smx = sb("smx", [128, Q])
        v_sb = sb("v_sb", [128, Q, DH])
        bd = sb("bd", [128, Q, 128])
        osb = sb("osb", [128, Q, 4 * DH])
        oxT = sb("oxT", [128, 4, R])
        oT = sb("oT", [D, R])
        h2 = sb("h2", [S, 2, GI, D])
        xa = sb("xa", [S, GI, D])
        xaT = sb("xaT", [D, R])
        qT = sb("qT", [D, 2, R])
        kT = sb("kT", [D, 2, R])
        va = sb("va", [S, 2, GI, H * VW])
        km = sb("km", [D, 2, UH, S])
        e2 = sb("e2", [S, 2, UW])
        eT = sb("eT", [S, 2, UW])
        mx2 = sb("mx2", [S, 2, UH])
        rcx = sb("rcx", [S, 2, UH])
        cx = sb("cx", [S, 2, GI, D])
        cxT = sb("cxT", [D, R])
        xr = sb("xr", [S, GI, D])
        ts = sb("ts", [S, 2, GI, RW])
        tT = sb("tT", [D, R])
        pause = sb("pause", [128, 2])
        pool_pause_out = sb("pool_pause_out", [1, 1])
        glb = sb("glb", [S, GI, E])
        eqb = sb("eqb", [S, GI, E])
        ohb = sb("ohb", [S, GI, E])
        rkb = sb("rkb", [S, GI, E])
        rmx = sb("rmx", [S, 2, GI])
        wsc = sb("wsc", [S, E])
        room = sb("room", [S, E])
        base = sb("base", [S, E])
        pos_f = sb("pos_f", [S, GI])
        pos_i = sb("pos_i", [S, 2, GI], int32)
        lnb = {n: (sb(f"st_{n}", [128, GI, 6]), sb(f"mv_{n}", [128, GI, 2]),
                   sb(f"ve_{n}", [128, GI]), sb(f"rs_{n}", [128, GI])) for n in ("a1", "f1", "f3")}

        ps_t = ps("ps_t")
        ps_a1 = ps("ps_a1")
        ps_a2 = ps("ps_a2", 1024)
        ps_a3 = ps("ps_a3")
        ps_f = ps("ps_f")
        ps_s = ps("ps_s")
        ps_e = ps("ps_e")

        s_ld = [sem(f"weights_loaded{k}") for k in range(8)]
        s_x = [sem(f"pixels_loaded{p}") for p in range(2)]
        s_hst = [sem(f"h_rows_stored{p}") for p in range(2)]
        s_moew = sem("expert_weights_loaded")
        s_dve0 = sem("setup_dve")
        s_pool0 = sem("setup_pool")
        s_pe0 = sem("setup_pe")
        s_act0 = sem("setup_act")
        s_xz = sem("pixel_buffer_zeroed")
        s_tail = sem("pixel_tail_copied")
        s_tok = sem("patch_products")
        s_hT = sem("tokens_transposed")
        s_hTc = sem("tokens_transposed_kept")
        s_hps = sem("tokens_in_psum")
        s_a1c = sem("a1_norm_chain")
        s_a1r = sem("a1_rstd")
        s_xn = sem("a1_normed")
        s_xnTp = sem("a1_normed_T_psum")
        s_xnT = sem("a1_normed_T")
        s_lg = sem("slice_logits")
        s_mx1 = sem("slice_max")
        s_sub1 = sem("slice_logits_less_max")
        s_exp1 = sem("slice_exp")
        s_ws = sem("slice_weight_sums")
        s_wc = sem("slice_weight_recips")
        s_w = sem("slice_weights")
        s_wTp = sem("slice_weights_T_psum")
        s_wT = sem("slice_weights_T")
        s_gp = sem("slice_sums_psum")
        s_gc = sem("slice_sum_chain")
        s_gn = sem("slice_means")
        s_gTp = sem("slice_means_T_psum")
        s_gT = sem("slice_means_T")
        s_stp = sem("slice_tokens_psum")
        s_stT = sem("slice_tokens_T")
        s_pT = sem("slice_queries_T")
        s_scp = sem("slice_scores_psum")
        s_sc = sem("slice_scores")
        s_vp = sem("slice_values_psum")
        s_v = sem("slice_values")
        s_ac = sem("slice_attention_chain")
        s_asub = sem("slice_scores_less_max")
        s_aexp = sem("slice_scores_exp")
        s_bd = sem("slice_attention_T")
        s_osp = sem("slice_outputs_psum")
        s_osb = sem("slice_outputs")
        s_oxp = sem("token_outputs_psum")
        s_ox = sem("token_outputs")
        s_oTp = sem("output_product_psum")
        s_oT = sem("output_product_T")
        s_oTr = sem("output_with_residual")
        s_hp2 = sem("h_in_psum")
        s_h2 = sem("h_rows")
        s_f1c = sem("f1_norm_chain")
        s_f1r = sem("f1_rstd")
        s_x2 = sem("f1_normed_rows")
        s_xa = sem("f1_normed_aug")
        s_xaTp = sem("f1_normed_T_psum")
        s_xaT = sem("f1_normed_T")
        s_qp = sem("q_psum")
        s_q = sem("q_ready")
        s_kp = sem("k_psum")
        s_k = sem("k_ready")
        s_vp2 = sem("v_psum")
        s_v2 = sem("v_ready")
        s_km = sem("k_masked")
        s_s2p = sem("scores_psum")
        s_s2m = sem("scores_max")
        s_s2 = sem("scores_less_max")
        s_e2 = sem("scores_exp")
        s_eTp = sem("exp_T_psum")
        s_eT = sem("exp_T")
        s_cp = sem("context_psum")
        s_cr = sem("context_sum_recip")
        s_cx = sem("context")
        s_cTp = sem("context_T_psum")
        s_cT = sem("context_T")
        s_xr = sem("f3_residual_and_bias")
        s_saP = sem("attention_out_psum")
        s_r3 = sem("f3_sum")
        s_f3c = sem("f3_norm_chain")
        s_f3r = sem("f3_rstd")
        s_tn = sem("f3_normed")
        s_tg = sem("f3_scaled")
        s_t = sem("t_rows")
        s_tTp = sem("t_T_psum")
        s_tT = sem("t_T")
        s_gtp = sem("gate_psum")
        s_gt = sem("gate_logits")
        s_oc = sem("first_largest_chain")
        s_oh = sem("expert_chosen")
        s_rp = sem("ranks_psum")
        s_rkc = sem("row_number_chain")
        s_pos = sem("row_numbers")
        s_base = sem("counts_so_far")
        s_id = sem("token_numbers")
        s_scat = [sem(f"rows_sent{p}") for p in range(2)]

        NTH = -(-(B * S) // T128)
        NR = 4
        cnt, nt, ntc, step_e = (sb(n_, [1, E]) for n_ in ("cnt", "nt", "ntc", "step_e"))
        tail_rows = hT_all[0:1, :, :].rearrange("p g r -> p (g r)")
        cmp_nt = tail_rows[:, 0:E * NTH].rearrange("p (e n) -> p e n", e=E)
        le, lew = (tail_rows[:, k * E * NT:(k + 1) * E * NT].rearrange("p (t e) -> p t e", e=E) for k in (1, 2))
        thr = sb("thr", [1, NTH])
        tix = sb("tix", [1, NT])
        tixe = sb("tixe", [1, NT])
        tef = sb("tef", [1, 2, NT])
        te_i = sb("te_i", [1, NT], int32)
        tr_i = sb("tr_i", [1, NT], int32)
        pad_i = sb("pad_i", [1, E], int32)
        zeros = sb("zeros", [1, E])
        xt = osb[:, 0:3, :].rearrange("p a n -> p (a n)")[:, 0:NR * RW].rearrange("p (a n) -> p a n", a=NR)
        xb = osb[:, 4:6, :].rearrange("p a n -> p (a n)").rearrange("p (a n) -> p a n", a=NR)
        zb = osb[:, 6:8, :].rearrange("p a n -> p (a n)").rearrange("p (a n) -> p a n", a=NR)
        xtT = km[:, :, :, :].rearrange("p a h n -> p a (h n)")[:, :, 0:128]
        w1c = oxT[:, :, :].rearrange("p a n -> p (a n)")[:, 0:2 * W1C].rearrange("p (a n) -> p a n", a=2)
        hbT = bd[:, :, :].rearrange("p (a q) n -> p a q n", a=2)
        idf = sb("idf", [128, NR])
        idx = sb("idx", [128, NR], int32)
        st_m, mv_m, ve_m, rs_m = (sb("st_m", [128, 6]), sb("mv_m", [128, 2, 2]), sb("ve_m", [128, 2]), sb("rs_m", [128, 2]))

        s_iota = sem("routing_constants")
        s_rc = sem("tile_table_chain")
        s_tbl = sem("tile_tables")
        s_padt = sem("pad_tile")
        s_pause = sem("pool_paused")
        s_pads = sem("pads_written")
        s_xt = [sem(f"tile_rows_loaded{q}") for q in range(4)]
        s_xtP = sem("tile_T_psum")
        s_xtT = sem("tile_T")
        s_w1 = sem("hidden_psum")
        s_xb = sem("tile_rows_and_bias")
        s_b1p = sem("b1_columns_psum")
        s_b1 = sem("b1_columns")
        s_w1c = sem("tile_w1")
        s_gl = sem("hidden_gelu")
        s_w2 = sem("expert_out_psum")
        s_ix = sem("tile_token_numbers")
        s_rz = sem("expert_sum")
        s_mc = sem("tile_norm_chain")
        s_mr = sem("tile_rstd")
        s_mn = sem("tile_centred")
        s_z = sem("tile_done")
        s_zadd = [sem(f"tile_added{q}") for q in range(4)]
        s_out = sem("out_stored")

        def tile_bodies(eng, body, last=NT):
            for k in range(8):
                body(k, k // 4, k % 4)
            with eng.Fori(2, last // 4, 1) as j:
                for q in range(4):
                    body(j * 4 + q, j, q)
            for k in range(last // 4 * 4, NT + 3):
                body(k, k // 4, k % 4)

        def tile(k, lag):
            return 0 <= k - lag < NT if isinstance(k, int) else True

        def entry(t, k):
            return t[0:1, k:k + 1] if isinstance(k, int) else t[0:1, bass.ds(k, 1)]

        block = ctx.enter_context(nc.Block())

        def upto(eng, s, per, g, k=None):
            n = g * per + (per if k is None else k)
            if isinstance(g, int) and n <= 0:
                return
            eng.wait_ge(s, n)

        def bodies(eng, body, end=G):
            for i in range(LOOP0):
                body(i, i // 2, i % 2)
            with eng.Fori(LOOP0 // 2, end // 2, 1) as j:
                for p in range(2):
                    body(j * 2 + p, j, p)
            for i in range(end, LAST):
                body(i, i // 2, i % 2)

        def part(t, g, n):
            return t[:, g * n:(g + 1) * n] if isinstance(g, int) else t[:, bass.ds(g * n, n)]

        def on(i, lag):
            return 0 <= i - lag < G if isinstance(i, int) else True

        DVE0 = {}
        n = 0
        for name in ("zeros", "gaps", "aug1", "aug2", "aug3", "pad_zero", "wpad", "wx1", "wx2", "wfx1", "wfx2", "wslT", "wvT", "idA",
                     "pos", "cls", "itemp", "wlog", "wstp", "wout", "negk", "wqa", "wqs", "wka", "wva"):
            n += 1
            DVE0[name] = n
        PE0 = {name: k + 1 for k, name in enumerate(("wslT", "wvT", "A", "pos", "wlog", "wstp", "wout"))}
        TB = (STEPS + 3) // 4

        wtok_nat = setup_buf(C * PS * PS)
        assert C * PS * PS == tok_w.shape[1]
        wpad = setup_buf(STEPS * 128)
        blank = [a.rearrange("p (e n) -> p e n", e=E) for a in
                 (setup_buf(E * RW), hT_all[:, :, :].rearrange("p g r -> p (g r)")[:, 10 * R:10 * R + E * RW])]
        wx_nat = setup_buf(H * D, DH).rearrange("p (h n) -> p h n", h=H)
        wfx_nat = x_all[0:DH, 0:H, :]
        wout_nat = hT_all[:, 0:2, 0:256].rearrange("p a n -> p a n")
        wq_nat = x_all[0:DH, H, 0:DH]
        wk_nat = x_all[0:DH, H, DH:2 * DH]
        wv_nat = x_all[0:DH, H + 1, 0:DH]
        wsl_nat = x_all[0:M, H + 2, 0:DH]
        wslT = x_all[0:DH, H + 3, 0:M]
        idA = x_all[0:DH, H + 4, :]
        pos_nat = x_all[0:S, H + 5, :]
        bsl_row = x_all[0:1, H + 6:H + 8, :]
        e_last = x_all[0:1, H + 8, :]
        bx_nat = x_all[0:DH, H + 9, 0:H]
        bfx_nat = x_all[0:DH, H + 9, H:2 * H]
        temp_bc = hT_all[:, 3, 0:H]
        itemp = hT_all[:, 3, H:2 * H]
        cls_col = hT_all[:, 3, 2 * H:2 * H + 1]
        neg_keep = hT_all[:, 3, 2 * H + 1:2 * H + 2]
        lastq = hT_all[:, 4, 0:D]
        lastk = hT_all[:, 5, 0:D]
        lastv = hT_all[:, 6, 0:D]
        natq = hT_all[:, 7, 0:D]
        natk = hT_all[:, 8, 0:D]
        natv = hT_all[:, 9, 0:D]

        def row(a, n=128):
            return a.rearrange("(o n) -> o n", o=1).broadcast_to([n, a.shape[0]])

        def load_pixels(eng, g, half, p):
            if not isinstance(g, int) or g >= 2:
                upto(eng, s_tok, 1, g - 2)
            for b in range(GI):
                for c in range(C):
                    src = x[bass.ds(g * GI + b, 1), c, :, :].rearrange("o h w -> (o h) w") if not isinstance(g, int) \
                        else x[g * GI + b, c, :, :]
                    dst = xbuf[p][32 * c:32 * c + PS, b * NP * IMG:(b + 1) * NP * IMG].rearrange("p (a w) -> p a w", a=NP)
                    eng.dma_start(dst, src.rearrange("(a y) w -> y a w", y=PS)).then_inc(s_x[p], 16)

        def sp_tail(sp):
            sp.wait_ge(s_tbl, 1)
            for e in range(E):
                first = sp.value_load(entry(pad_i, e), min_val=0, max_val=NONE + (E - 1) * T128)
                sp.dma_start(xs_dram[bass.ds(first, T128), :], blank_dram[e * T128:(e + 1) * T128, :]).then_inc(s_pads, 16)
            for p in range(2):
                sp.wait_ge(s_scat[p], 16 * GI * (G // 2))
            sp.wait_ge(s_pads, 16 * (E + 4))

            def load(k, j, q):
                first = sp.value_load(entry(tr_i, k), min_val=0, max_val=NONE + (E - 1) * T128)
                upto(sp, s_xtP, 1, k - NR)
                upto(sp, s_xb, 1, k - NR)
                sp.dma_start(xt[:, q, :], xs_dram[bass.ds(first, T128), :]).then_inc(s_xt[q], 16)

            for k in range(3):
                load(k, 0, k)

            def body(k, j, q):
                if not isinstance(k, int) or k + 3 < NT:
                    load(k + 3, j, (q + 3) % NR)

            tile_bodies(sp, body, NT - 4)
            for q in range(NR):
                sp.wait_ge(s_zadd[q], 16 * (NT // NR))
            sp.dma_start(out.rearrange("b s d -> b (s d)"), h_dram[0:B * S, :].rearrange("(b s) d -> b (s d)", s=S)).then_inc(s_out, 16)
            sp.wait_ge(s_out, 16)

        def pool_pause(n):
            upto(nc.gpsimd, s_pause, 1, n - 1)
            nc.gpsimd.tensor_tensor(pool_pause_out[:, :], ones[0:1, 0:1], ones[0:1, 0:1], ALU.add).then_inc(s_pause, 1)

        def pool_tail(pool):
            for p in range(2):
                pool.wait_ge(s_hst[p], 16 * (G // 2))
            pool.wait_ge(s_pads, 16 * (E + 4))

            def body(k, j, q):
                if tile(k, 3):
                    t, d = k - 3, (q + 1) % NR
                    upto(pool, s_z, 1, t)
                    upto(pool, s_ix, 1, t)
                    pool_pause(G + t)
                    pool.indirect_dma_start(h_dram, bass.IndirectOffsetOnAxis(ap=idx[:, d:d + 1], axis=0),
                                            zb[:, d, :], None, compute_op=ALU.add).then_inc(s_zadd[d], 16)
                if tile(k, 2):
                    t, a = k - 2, q % 2
                    upto(pool, s_mc, 3, t)
                    nc.gpsimd.tensor_tensor(rs_m[:, a:a + 1], ve_m[:, a:a + 1], mhalf[:, 0:1], ALU.pow).then_inc(s_mr, 1)

            tile_bodies(pool, body)

        def pe_tail(pe):
            pe.wait_ge(s_moew, 64)
            upto(pe, s_base, 1, G - 1)
            nc.tensor.transpose(ps_a1[:, 0:E * HC], b1_nat, ident[0:E * HC, 0:E * HC]).then_inc(s_b1p, 1)
            pe.wait_ge(s_tbl, 1)
            ps_x = (ps_s, ps_e)
            ps_y = (ps_a3, ps_f)

            def body(k, j, q):
                a, o_ = q % 2, (q + 1) % 2
                ed = pe.value_load(entry(te_i, k - 2), min_val=0, max_val=E - 1) if tile(k, 2) else None
                if tile(k, 1):
                    upto(pe, s_xtT, 1, k - 1)
                    upto(pe, s_w1c, 1, k - 1)
                    upto(pe, s_gl, 1, k - 3)
                    for c in range(HC):
                        c0 = o_ * HID + c * 128
                        mm = nc.tensor.matmul(ps_a2[:, c0:c0 + 128], w1c[:, o_, c * 128:(c + 1) * 128], xtT[:, o_, :],
                                              start=True, stop=True)
                    mm.then_inc(s_w1, 1)
                if tile(k, 0):
                    pe.wait_ge(s_xt[q], (j + 1) * 16)
                    upto(pe, s_xtT, 1, k - 2)
                    nc.tensor.transpose(ps_x[a][:, 0:D], xt[:, q, 0:D], ident[:, :]).then_inc(s_xtP, 1)
                if tile(k, 2):
                    upto(pe, s_gl, 1, k - 2)
                    upto(pe, s_rz, 1, k - 4)
                    for c in range(HC):
                        mm = nc.tensor.matmul(ps_y[a][:, 0:D], hbT[:, a, c, :],
                                              w2_sb[:, bass.ds(ed, 1), c, :].rearrange("p o n -> p (o n)"),
                                              start=(c == 0), stop=(c == HC - 1))
                    mm.then_inc(s_w2, 1)

            tile_bodies(pe, body)

        def act_tail(act):
            act.preload_act_table(ACT.Gelu)

            ps_x = (ps_s, ps_e)

            def body(k, j, q):
                a, o_ = q % 2, (q + 1) % 2
                if tile(k, 0):
                    upto(act, s_xtP, 1, k)
                    upto(act, s_w1, 1, k - 2)
                    nc.scalar.activation(xtT[:, a, :], ps_x[a][:, 0:D], ACT.Copy).then_inc(s_xtT, 1)
                if tile(k, 1):
                    upto(act, s_w1, 1, k - 1)
                    upto(act, s_w2, 1, k - 3)
                    for c in range(HC):
                        c0 = o_ * HID + c * 128
                        g = nc.scalar.activation(hbT[:, o_, c, :], ps_a2[:, c0:c0 + 128], ACT.Gelu,
                                                 bias=w1c[:, o_, HID + c:HID + c + 1])
                    g.then_inc(s_gl, 1)

            tile_bodies(act, body)

        RC = {name: k + 1 for k, name in enumerate((
            "cnt", "cmp", "nt", "ntc", "step", "le", "te", "temin", "lew", "row", "row2", "pad"))}

        def dve_tail(dve):
            v = nc.vector
            done = [0]

            def step(ins, name):
                done[0] += 1
                assert RC[name] == done[0], name
                ins.then_inc(s_rc, 1)
                dve.wait_ge(s_rc, done[0])

            upto(dve, s_base, 1, G - 1)
            step(v.tensor_tensor(cnt[:, :], base[0:1, :], room[0:1, :], ALU.subtract), "cnt")
            step(v.tensor_tensor(cmp_nt[:, :, :], cnt[:, :].unsqueeze(2).broadcast_to([1, E, NTH]),
                                 thr[:, :].unsqueeze(1).broadcast_to([1, E, NTH]), ALU.is_gt), "cmp")
            step(v.tensor_reduce(nt[:, :], cmp_nt[:, :, :], AX, ALU.add), "nt")
            step(v.tensor_tensor_scan(ntc[:, :], nt[:, :], zeros[:, :], 0.0, ALU.add, ALU.add), "ntc")
            step(v.tensor_scalar(step_e[:, :], nt[:, :], -float(T128), float(REG), ALU.mult, ALU.add), "step")
            step(v.tensor_tensor(le[:, :, :], ntc[:, :].unsqueeze(1).broadcast_to([1, NT, E]),
                                 tixe[:, :].unsqueeze(2).broadcast_to([1, NT, E]), ALU.is_le), "le")
            step(v.tensor_reduce(tef[:, 0, :], le[:, :, :], AX, ALU.add), "te")
            step(v.tensor_scalar(te_i[:, :], tef[:, 0, :], float(E - 1), None, ALU.min), "temin")
            step(v.tensor_tensor(lew[:, :, :], le[:, :, :], step_e[:, :].unsqueeze(1).broadcast_to([1, NT, E]), ALU.mult), "lew")
            step(v.tensor_reduce(tef[:, 1, :], lew[:, :, :], AX, ALU.add), "row")
            step(v.tensor_tensor(tr_i[:, :], tef[:, 1, :], tix[:, :], ALU.add), "row2")
            step(v.tensor_scalar(pad_i[:, :], base[0:1, :], 1.0, None, ALU.add), "pad")
            v.memset(pause[:, 0:1], 0.0).then_inc(s_tbl, 1)
            dve.wait_ge(s_moew, 64)
            dve.wait_ge(s_b1p, 1)
            v.tensor_copy(w1_sb[:, :, HID:W1C], ps_a1[:, 0:E * HC].rearrange("p (e c) -> p e c", e=E)).then_inc(s_b1, 1)
            dve.wait_ge(s_tbl, 1)
            dve.wait_ge(s_b1, 1)
            ps_y = (ps_a3, ps_f)

            def body(k, j, q):
                a, o_ = q % 2, (q + 1) % 2
                ea = dve.value_load(entry(te_i, k), min_val=0, max_val=E - 1) if tile(k, 0) else None
                if tile(k, 3):
                    t, d = k - 3, (q + 1) % NR
                    upto(dve, s_mr, 1, t)
                    v.scalar_tensor_tensor(zb[:, d, :], zb[:, d, :], mv_m[:, o_, 0:1], g2_bc[:, :], ALU.subtract, ALU.mult)\
                        .then_inc(s_mn, 1)
                if tile(k, 0):
                    upto(dve, s_w1, 1, k - 2)
                    upto(dve, s_gl, 1, k - 2)
                    upto(dve, s_w1c, 1, k - 1)
                    v.memset(pause[:, 1:2], 0.0)
                    v.tensor_copy(w1c[:, a, :], w1_sb[:, bass.ds(ea, 1), :].rearrange("p o n -> p (o n)")).then_inc(s_w1c, 1)
                    dve.wait_ge(s_xt[q], (j + 1) * 16)
                    v.tensor_copy(idf[:, q:q + 1], xt[:, q, D:D + 1])
                    v.tensor_tensor(xb[:, q, :], xt[:, q, 0:D], b2_bc[:, bass.ds(ea, 1), :].rearrange("p o n -> p (o n)"),
                                    ALU.add).then_inc(s_xb, 1)
                if tile(k, 3):
                    upto(dve, s_mn, 1, t)
                    v.scalar_tensor_tensor(zb[:, d, :], zb[:, d, :], rs_m[:, o_:o_ + 1], beta2_bc[:, :], ALU.mult, ALU.add)\
                        .then_inc(s_z, 1)
                if tile(k, 2):
                    t, d = k - 2, (q + 2) % NR
                    if not isinstance(k, int) or t >= NR:
                        dve.wait_ge(s_zadd[d], 16 * (t // NR if isinstance(k, int) else (j if q >= 2 else j - 1)))
                    upto(dve, s_w2, 1, t)
                    upto(dve, s_xb, 1, t)
                    v.tensor_copy(idx[:, d:d + 1], idf[:, d:d + 1]).then_inc(s_ix, 1)
                    v.tensor_tensor(zb[:, d, :], xb[:, d, :], ps_y[a][:, 0:D], ALU.add).then_inc(s_rz, 1)
                    upto(dve, s_rz, 1, t)
                    v.bn_stats(st_m[:, :], zb[:, d, :]).then_inc(s_mc, 1)
                    upto(dve, s_mc, 3, t, 1)
                    v.memset(pause[:, 0:1], 0.0)
                    v.bn_aggr(mv_m[:, a, :], st_m[:, :]).then_inc(s_mc, 1)
                    upto(dve, s_mc, 3, t, 2)
                    v.tensor_scalar(ve_m[:, a:a + 1], mv_m[:, a, 1:2], EPS, None, ALU.add).then_inc(s_mc, 1)

            tile_bodies(dve, body)

        @block.sync
        def _(sp):
            sp.dma_start(wtok_nat, tok_w).then_inc(s_ld[0], 16)
            sp.dma_start(pos_nat, tok_pos).then_inc(s_ld[1], 16)
            sp.dma_start(cls_col, tok_cls.rearrange("o n -> n o")).then_inc(s_ld[1], 16)
            sp.dma_start(b_tok[:, :], tok_b.rearrange("(n o) -> n o", o=1)).then_inc(s_ld[1], 16)
            sp.wait_ge(s_xz, 1)
            load_pixels(sp, 0, 0, 0)
            sp.dma_start(wx_nat, wx.rearrange("(h d) c -> d h c", d=DH)).then_inc(s_ld[2], 16)
            sp.dma_start(wfx_nat, wfx.rearrange("(h d) c -> d h c", d=DH)).then_inc(s_ld[2], 16)
            sp.dma_start(bx_nat, bx.rearrange("(h d) -> d h", d=DH), allow_slow_non_contiguous=True).then_inc(s_ld[2], 16)
            sp.dma_start(bfx_nat, bfx.rearrange("(h d) -> d h", d=DH), allow_slow_non_contiguous=True).then_inc(s_ld[2], 16)
            sp.dma_start(wq_nat, wq).then_inc(s_ld[3], 16)
            sp.dma_start(wk_nat, wk).then_inc(s_ld[3], 16)
            sp.dma_start(wv_nat, wv).then_inc(s_ld[3], 16)
            sp.dma_start(wsl_nat, wslice).then_inc(s_ld[3], 16)
            sp.dma_start(bsl_row.rearrange("p a (h m) -> p (a h) m", m=M),
                         bslice.rearrange("(o n) -> o n", o=1).unsqueeze(1).broadcast_to([1, H, M]))\
              .then_inc(s_ld[3], 16)
            sp.dma_start(wout_nat, wout.rearrange("p (a n) -> p a n", a=2)).then_inc(s_ld[4], 16)
            sp.dma_start(bout_col[:, :], bout.rearrange("(n o) -> n o", o=1)).then_inc(s_ld[4], 16)
            sp.dma_start(temp_bc, row(temp.rearrange("a h b c -> (a h b c)"))).then_inc(s_ld[4], 16)
            for nat, last, wd, bd_ in ((natq, lastq, f_wq, f_bq), (natk, lastk, f_wk, f_bk), (natv, lastv, f_wv, f_bv)):
                sp.dma_start(nat[0:D - 1, :], wd[0:D - 1, :]).then_inc(s_ld[5], 16)
                sp.dma_start(nat[D - 1:D, :], row(bd_, 1)).then_inc(s_ld[5], 16)
                sp.dma_start(last, wd[D - 1:D, :].broadcast_to([D, D])).then_inc(s_ld[5], 16)
            sp.dma_start(wo_sb[:, :], f_wo).then_inc(s_ld[6], 16)
            sp.dma_start(wg_sb[:, :], wg).then_inc(s_ld[6], 16)
            sp.dma_start(bo_bc[:, :], row(f_bo, S)).then_inc(s_ld[7], 16)
            sp.dma_start(g1_bc[:, :], row(g1, S)).then_inc(s_ld[7], 16)
            sp.dma_start(beta1_bc[:, :], row(beta1, S)).then_inc(s_ld[7], 16)
            sp.dma_start(bg_bc[:, :], row(bg, S)).then_inc(s_ld[7], 16)
            sp.dma_start(g2_bc[:, :], row(g2)).then_inc(s_ld[7], 16)
            sp.dma_start(beta2_bc[:, :], row(beta2)).then_inc(s_ld[7], 16)
            sp.wait_ge(s_padt, 5)
            for k, dst in enumerate((blank_dram, xs_dram[NONE:NONE + E * T128, :])):
                first = B * S + k * E * T128
                sp.dma_start(dst.rearrange("(e p) n -> p e n", p=T128), blank[k]).then_inc(s_pads, 16)
                sp.dma_start(h_dram[first:first + E * T128, :].rearrange("(e p) n -> p e n", p=T128), blank[k][:, :, 0:D])\
                  .then_inc(s_pads, 16)
            sp.wait_ge(s_xz, 2)
            load_pixels(sp, 1, 0, 1)

            def body(i, j, p):
                if on(i, 0) and (not isinstance(i, int) or i + 2 < G):
                    load_pixels(sp, i + 2, j + 1, p)
                if on(i, 3):
                    g = i - 3
                    upto(sp, s_h2, 1, g)
                    dst = h_dram[bass.ds(g * R, R), :] if not isinstance(g, int) else h_dram[g * R:(g + 1) * R, :]
                    sp.dma_start(dst.rearrange("(b s) d -> s b d", s=S), h2[:, 1 - p, :, :]).then_inc(s_hst[1 - p], 16)

            bodies(sp, body, G - 2)
            upto(sp, s_tok, 1, G - 1)
            sp.dma_start(w1_sb[:, :, 0:HID], w1.rearrange("e c n -> c e n")).then_inc(s_moew, 16)
            sp.dma_start(w2_sb, w2.rearrange("e (c p) n -> p e c n", p=D)).then_inc(s_moew, 16)
            sp.dma_start(b1_nat, b1.rearrange("e (c n) -> (e c) n", c=HC)).then_inc(s_moew, 16)
            sp.dma_start(b2_bc, b2.rearrange("(o e) n -> o e n", o=1).broadcast_to([128, E, D])).then_inc(s_moew, 16)
            sp_tail(sp)

        @block.gpsimd
        def _(pool):
            nc.gpsimd.memset(ident[:, :], 0.0).then_inc(s_pool0, 1)
            pool.wait_ge(s_pool0, 1)
            nc.gpsimd.affine_select(out=ident[:, :], in_=ident[:, :], compare_op=ALU.not_equal, fill=1.0,
                                    base=0, pattern=[[-1, 128]], channel_multiplier=1).then_inc(s_pool0, 1)
            nc.gpsimd.memset(mhalf[:, :], -0.5).then_inc(s_pool0, 1)
            nc.gpsimd.memset(ones[:, :], 1.0).then_inc(s_pool0, 1)
            pool.wait_ge(s_pool0, 4)
            nc.gpsimd.affine_select(out=triu[:, :], in_=ones[0:S, 0:S], compare_op=ALU.is_ge, fill=0.0,
                                    base=0, pattern=[[1, S]], channel_multiplier=-1).then_inc(s_pool0, 1)
            nc.gpsimd.memset(head_mask[:, :], 1.0).then_inc(s_pool0, 1)
            pool.wait_ge(s_pool0, 6)
            nc.gpsimd.affine_select(out=head_mask[:, :], in_=head_mask[:, :], compare_op=ALU.is_ge, fill=0.0,
                                    base=0, pattern=[[-DH2, H]], channel_multiplier=1).then_inc(s_pool0, 1)
            pool.wait_ge(s_pool0, 7)
            nc.gpsimd.affine_select(out=head_mask[:, :], in_=head_mask[:, :], compare_op=ALU.is_ge, fill=0.0,
                                    base=DH2 - 1, pattern=[[DH2, H]], channel_multiplier=-1).then_inc(s_pool0, 1)
            io = dict(channel_multiplier=0, allow_small_or_imprecise_dtypes=True)
            nc.gpsimd.iota(wsc[:, :], [[-1, E]], base=E, **io).then_inc(s_iota, 1)
            nc.gpsimd.iota(room[:, :], [[REG, E]], base=-1, **io).then_inc(s_iota, 1)
            nc.gpsimd.iota(base[:, :], [[REG, E]], base=-1, **io).then_inc(s_iota, 1)
            nc.gpsimd.iota(thr[:, :], [[T128, NTH]], base=0, **io).then_inc(s_iota, 1)
            nc.gpsimd.iota(tix[:, :], [[T128, NT]], base=0, **io).then_inc(s_iota, 1)
            nc.gpsimd.iota(tixe[:, :], [[1, NT]], base=0, **io).then_inc(s_iota, 1)
            nc.gpsimd.memset(ts[:, :, :, :], 0.0).then_inc(s_padt, 1)
            for k in range(2):
                nc.gpsimd.memset(blank[k], 0.0).then_inc(s_padt, 1)
            pool.wait_ge(s_padt, 3)
            for p in range(2):
                nc.gpsimd.iota(ts[:, p, :, D:D + 1], [[S, GI], [0, 1]], base=(p - 2) * R, channel_multiplier=1,
                               allow_small_or_imprecise_dtypes=True).then_inc(s_iota, 1)
            for k in range(2):
                nc.gpsimd.iota(blank[k][:, :, D:D + 1], [[T128, E], [0, 1]], base=B * S + k * E * T128, channel_multiplier=1,
                               allow_small_or_imprecise_dtypes=True).then_inc(s_padt, 1)
            pool.wait_ge(s_pool0, 8)
            pool.wait_ge(s_iota, 8)
            pool.wait_ge(s_ld[7], 96)

            def rstd(name, s_chain, s_r, g):
                _, _, ve, rs = lnb[name]
                upto(pool, s_chain, 3, g)
                nc.gpsimd.tensor_tensor(rs[0:S, :], ve[0:S, :], mhalf[0:S, :], ALU.pow).then_inc(s_r, 1)

            def masked_k(g, u, p):
                b, hf = u // 2, u % 2
                upto(pool, s_s2p, UNITS, g, u - 1)
                kv = kT[:, p, b * S:(b + 1) * S].unsqueeze(1).broadcast_to([D, UH, S])
                mv = head_mask[:, hf * UH:(hf + 1) * UH].unsqueeze(2).broadcast_to([D, UH, S])
                nc.gpsimd.tensor_tensor(km[:, u % 2, :, :], kv, mv, ALU.mult).then_inc(s_km, 1)

            def body(i, j, p):
                g1, f1, f2, f3, f4 = i - 1, i - 4, i - 5, i - 6, i - 7
                A1, F1, F2, F3, F4 = (on(i, k) for k in (1, 4, 5, 6, 7))

                def masks(*units):
                    if F2:
                        for u in units:
                            masked_k(f2, u, 1 - p)

                if F2:
                    upto(pool, s_k, 1, f2)
                masks(0, 1)
                if F1:
                    rstd("f1", s_f1c, s_f1r, f1)
                if F3:
                    upto(pool, s_x2, 1, f3)
                    upto(pool, s_t, 1, f3 - 1)
                    nc.gpsimd.tensor_tensor(xr[:, :, :], part(x_all, f3, GI), bo_bc[:, :].unsqueeze(1).broadcast_to([S, GI, D]),
                                            ALU.add).then_inc(s_xr, 1)
                if A1:
                    rstd("a1", s_a1c, s_a1r, g1)
                masks(2, 3, 4)
                if F3:
                    rstd("f3", s_f3c, s_f3r, f3)
                masks(5)
                if F3:
                    upto(pool, s_tn, 1, f3)
                    nc.gpsimd.tensor_tensor(xr[:, :, :], xr[:, :, :], g1_bc[:, :].unsqueeze(1).broadcast_to([S, GI, D]),
                                            ALU.mult).then_inc(s_tg, 1)
                    upto(pool, s_tg, 1, f3)
                    upto(pool, s_tTp, 1, f3 - 2)
                    if not isinstance(f3, int) or f3 >= 2:
                        pool.wait_ge(s_scat[p], 16 * GI * ((f3 - 2) // 2 + 1 if isinstance(f3, int) else j - 3))
                    nc.gpsimd.tensor_tensor(ts[:, p, :, 0:D], xr[:, :, :], beta1_bc[:, :].unsqueeze(1).broadcast_to([S, GI, D]),
                                            ALU.add).then_inc(s_t, 1)
                masks(6, 7)
                if A1:
                    weights(g1, 0)
                if F4:
                    upto(pool, s_t, 1, f4)
                    upto(pool, s_id, 1, f4)
                    upto(pool, s_pos, 1, f4)
                    pool_pause(f4)
                    for b in range(GI):
                        pool.indirect_dma_start(xs_dram, bass.IndirectOffsetOnAxis(ap=pos_i[:, 1 - p, b:b + 1], axis=0),
                                                ts[:, 1 - p, b, :], None).then_inc(s_scat[1 - p], 16)
                if A1:
                    weights(g1, 1)

            def weights(g1, r):
                wv_ = w[:, 2 * r:2 * r + 2, :].rearrange("p b (h m) -> p (b h) m", m=M)
                upto(pool, s_wc, 2, g1, r + 1)
                nc.gpsimd.tensor_tensor(wv_, wv_, mx1[:, 2 * r * H:(2 * r + 2) * H].unsqueeze(2).broadcast_to([S, 2 * H, M]),
                                        ALU.mult).then_inc(s_w, 1)

            bodies(pool, body)
            pool_tail(pool)

        @block.tensor
        def _(pe):
            pe.wait_ge(s_pool0, 8)
            pe.wait_ge(s_dve0, DVE0["wpad"])
            wp = wpad.rearrange("p (s n) -> p s n", s=STEPS)
            for k in range(TB):
                if k >= 2:
                    pe.wait_ge(s_act0, k - 1)
                for q in range(4 * k, min(4 * k + 4, STEPS)):
                    last = nc.tensor.transpose(ps_a2[:, (q % 8) * 128:(q % 8) * 128 + 128], wp[:, q, :], ident[:, :])
                last.then_inc(s_pe0, 1)
            pe.wait_ge(s_ld[3], 80)
            nc.tensor.transpose(ps_a1[0:DH, 0:M], wsl_nat, ident[0:M, 0:M]).then_inc(s_pe0, 1)
            nc.tensor.transpose(ps_a1[0:DH, 64:64 + DH], wv_nat, ident[0:DH, 0:DH]).then_inc(s_pe0, 1)
            nc.tensor.matmul(ps_a1[0:DH, 128:128 + DH], wq_nat, wk_nat, start=True, stop=True).then_inc(s_pe0, 1)
            pe.wait_ge(s_ld[1], 48)
            nc.tensor.transpose(ps_a1[:, 192:192 + S], pos_nat, ident[0:S, 0:S]).then_inc(s_pe0, 1)
            pe.wait_ge(s_dve0, DVE0["wslT"])
            nc.tensor.matmul(ps_f[:, 0:H * M], e_last, bsl_row.rearrange("p a n -> p (a n)"), start=True, stop=False)
            for h in range(H):
                last = nc.tensor.matmul(ps_f[:, h * M:(h + 1) * M], wx_nat[:, h, :], wslT, start=False, stop=(h == H - 1))
            last.then_inc(s_pe0, 1)
            pe.wait_ge(s_act0, TB)
            pe.wait_ge(s_dve0, DVE0["idA"])
            for h in range(H):
                last = nc.tensor.matmul(ps_a2[:, h * 128:(h + 1) * 128], wfx_nat[:, h, :], idA, start=True, stop=True)
            last.then_inc(s_pe0, 1)
            pe.wait_ge(s_ld[4], 48)
            wo4 = wout_nat.rearrange("p a (c n) -> p a c n", c=2)
            for k in range(4):
                last = nc.tensor.transpose(ps_a3[:, k * 128:(k + 1) * 128], wo4[:, k // 2, k % 2, :], ident[:, :])
            last.then_inc(s_pe0, 1)
            pe.wait_ge(s_dve0, DVE0["wva"])
            pe.wait_ge(s_ld[6], 32)

            def patch_products(i, p, slot, half):
                g = i
                if slot == 0 and half == 1:
                    upto(pe, s_hT, 1, g - 1)
                v = xbuf[p].rearrange("p (a n) -> p a n", n=PS)
                s0, n_, n0_ = sum(T_SLOT[:slot]), T_SLOT[slot], T_FIRST[slot]
                mm = None
                for s in range(s0, s0 + n0_) if half == 0 else range(s0 + n0_, s0 + n_):
                    if s % TAIL == 0:
                        upto(pe, s_tail, C, g, s // TAIL + 1)
                    mm = nc.tensor.matmul(ps_t[:, 0:GI * NPP], w_tok[:, s, :], v[:, :, s],
                                          start=(s == 0), stop=(s == STEPS - 1))
                if slot == 7 and half == 0:
                    mm.then_inc(s_tok, 1)

            def scores(g, u, pq):
                b = u // 2
                upto(pe, s_km, UNITS, g, u + 1)
                if u == 0:
                    upto(pe, s_q, 1, g)
                upto(pe, s_s2, UNITS, g, u)
                nc.tensor.matmul(ps_s[0:S, 0:UW], qT[:, pq, b * S:(b + 1) * S],
                                 km[:, u % 2, :, :].rearrange("p h s -> p (h s)"), start=True, stop=True)\
                    .then_inc(s_s2p, 1)

            def exp_transposes(g, u):
                upto(pe, s_e2, UNITS, g, u + 1)
                upto(pe, s_eT, UNITS, g, u)
                upto(pe, s_cx, UNITS, g, u)
                for h in range(UH):
                    mm = nc.tensor.transpose(ps_e[0:S, h * S:(h + 1) * S], e2[:, u % 2, h * S:(h + 1) * S], ident[0:S, 0:S])
                mm.then_inc(s_eTp, 1)

            def contexts(g, u, pq):
                b, hf = u // 2, u % 2
                upto(pe, s_eT, UNITS, g, u + 1)
                if u == 0:
                    upto(pe, s_v2, 1, g)
                c0 = 300 + (u % 2) * UH * VW
                for h in range(UH):
                    hd = hf * UH + h
                    mm = nc.tensor.matmul(ps_e[0:S, c0 + h * VW:c0 + (h + 1) * VW], eT[:, u % 2, h * S:(h + 1) * S],
                                          va[:, pq, b, hd * VW:(hd + 1) * VW], start=True, stop=True)
                mm.then_inc(s_cp, 1)

            def token_outputs(g, jc, pw):
                hh, jj = jc // 2, jc % 2
                if jc == 0:
                    upto(pe, s_osb, 2, g)
                    upto(pe, s_wT, 1, g)
                    upto(pe, s_h2, 1, g - 1)
                upto(pe, s_ox, 4, g, jc)
                for b in range(GI):
                    mm = nc.tensor.matmul(ps_a3[:, b * S:(b + 1) * S], osb[:, b * HH + hh, jj * 128:(jj + 1) * 128],
                                          wT[:, pw, b * HH + hh, :], start=True, stop=True)
                mm.then_inc(s_oxp, 1)

            def body(i, j, p):
                g1, g2, g3, f1, f2, f3, f4 = (i - k for k in range(1, 8))
                T, A1, A2, A3, F1, F2, F3, F4 = (on(i, k) for k in range(8))
                for slot in range(8):
                    gc_, uc, pc, C_ = (f3, 7, p, F3) if slot == 0 else (f2, slot - 1, 1 - p, F2)
                    if F2:
                        if slot == 5 and F4:
                            upto(pe, s_base, 1, f4)
                        scores(f2, slot, 1 - p)
                    if slot == 1 and A2:
                        upto(pe, s_wT, 1, g2)
                        for q in range(Q):
                            mm = nc.tensor.matmul(ps_a2[:, q * 128:(q + 1) * 128],
                                                  w[:, q // HH, (q % HH) * 128:(q % HH) * 128 + 128],
                                                  xn[:, q // HH, :], start=True, stop=True)
                        mm.then_inc(s_gp, 1)
                    if slot == 3 and F3:
                        upto(pe, s_cT, 1, f3)
                        for b in range(GI):
                            mm = nc.tensor.matmul(ps_f[0:S, b * D:(b + 1) * D], cxT[:, b * S:(b + 1) * S], wo_sb[:, :],
                                                  start=True, stop=True)
                        mm.then_inc(s_saP, 1)
                    if slot == 4:
                        if A3:
                            upto(pe, s_ox, 4, g3)
                            for jc in range(4):
                                mm = nc.tensor.matmul(ps_a3[:, 0:R], woutT[:, jc, :], oxT[:, jc, :],
                                                      start=(jc == 0), stop=(jc == 3))
                            mm.then_inc(s_oTp, 1)
                        if F1:
                            upto(pe, s_q, 1, f1)
                            nc.tensor.matmul(ps_f[:, 0:R], wk_aug[:, :], xaT[:, :], start=True, stop=True).then_inc(s_kp, 1)
                    if T:
                        patch_products(i, p, slot, 0)
                    if C_:
                        exp_transposes(gc_, uc)
                    if slot == 0:
                        if A1:
                            upto(pe, s_hT, 1, g1)
                            upto(pe, s_sub1, 2, g1 - 1)
                            for b in range(GI):
                                mm = nc.tensor.transpose(ps_a1[0:S, b * D:(b + 1) * D], hT[:, b, :], ident[:, :])
                            mm.then_inc(s_hps, 1)
                        if A2:
                            upto(pe, s_w, 2, g2)
                            upto(pe, s_osb, 2, g2 - 1)
                            for q in range(Q):
                                c0 = (q // 4) * 512 + (q % 4) * S
                                mm = nc.tensor.transpose(ps_a2[:, c0:c0 + S],
                                                         w[:, q // HH, (q % HH) * 128:(q % HH) * 128 + 128], ident[0:S, 0:S])
                            mm.then_inc(s_wTp, 1)
                    if slot == 1:
                        if F1:
                            upto(pe, s_xa, 1, f1)
                            upto(pe, s_gt, 1, f3 - 1)
                            upto(pe, s_v2, 1, f1 - 1)
                            for b in range(GI):
                                mm = nc.tensor.transpose(ps_f[:, b * S:(b + 1) * S], xa[:, b, :], ident[0:S, 0:S])
                            mm.then_inc(s_xaTp, 1)
                    if slot == 2:
                        if A1:
                            upto(pe, s_xn, 1, g1)
                            for b in range(GI):
                                mm = nc.tensor.transpose(ps_a1[:, b * S:(b + 1) * S], xn[:, b, :], ident[0:S, 0:S])
                            mm.then_inc(s_xnTp, 1)
                        if A2:
                            upto(pe, s_gn, 1, g2)
                            for q in range(Q):
                                mm = nc.tensor.transpose(ps_a2[:, q * 128:(q + 1) * 128], gn[:, q, :], ident[:, :])
                            mm.then_inc(s_gTp, 1)
                        if F3:
                            upto(pe, s_cx, UNITS, f3)
                            if F1:
                                upto(pe, s_xaT, 1, f1)
                            else:
                                upto(pe, s_gt, 1, f3 - 1)
                            for b in range(GI):
                                mm = nc.tensor.transpose(ps_f[:, b * S:(b + 1) * S], cx[:, p, b, :], ident[0:S, 0:S])
                            mm.then_inc(s_cTp, 1)
                    if slot == 3:
                        if A1:
                            upto(pe, s_xnT, 1, g1)
                            for b in range(2):
                                mm = nc.tensor.matmul(ps_a1[0:S, b * 256:(b + 1) * 256], xnT[:, b * S:(b + 1) * S], w_log[:, :],
                                                      start=True, stop=True)
                            mm.then_inc(s_lg, 1)
                        if A2:
                            upto(pe, s_gT, 1, g2)
                            for h in range(H):
                                mm = nc.tensor.matmul(ps_a2[:, h * 128:(h + 1) * 128], w_stp[:, h, :],
                                                      gnT[:, :, h // 4, h % 4, :], start=True, stop=True)
                            mm.then_inc(s_stp, 1)
                        if F1:
                            upto(pe, s_xaT, 1, f1)
                            upto(pe, s_r3, 1, f3)
                            nc.tensor.matmul(ps_f[:, 0:R], wq_aug[:, :], xaT[:, :], start=True, stop=True).then_inc(s_qp, 1)
                    if slot == 4:
                        if A1:
                            upto(pe, s_sub1, 2, g1, 1)
                            for b in range(2):
                                mm = nc.tensor.matmul(ps_a1[0:S, b * 256:(b + 1) * 256], xnT[:, (b + 2) * S:(b + 3) * S], w_log[:, :],
                                                      start=True, stop=True)
                            mm.then_inc(s_lg, 1)
                        if A2:
                            upto(pe, s_stT, 1, g2)
                            upto(pe, s_pT, 1, g2)
                            for q in range(Q):
                                mm = nc.tensor.matmul(ps_a2[:, q * 128:(q + 1) * 128], pT[:, q * 128:(q + 1) * 128],
                                                      stT[:, q * 128:(q + 1) * 128], start=True, stop=True)
                            mm.then_inc(s_scp, 1)
                    if slot == 5:
                        if A3:
                            upto(pe, s_oTr, 1, g3)
                            for b in range(GI):
                                mm = nc.tensor.transpose(ps_a3[0:S, b * D:(b + 1) * D], oT[:, b * S:(b + 1) * S], ident[:, :])
                            mm.then_inc(s_hp2, 1)
                        if F1:
                            upto(pe, s_k, 1, f1)
                            for b in range(GI):
                                mm = nc.tensor.matmul(ps_f[0:S, b * D:(b + 1) * D], xaT[:, b * S:(b + 1) * S], wv_aug[:, :],
                                                      start=True, stop=True)
                            mm.then_inc(s_vp2, 1)
                        if A2:
                            upto(pe, s_sc, 1, g2)
                            for q in range(Q):
                                mm = nc.tensor.matmul(ps_a2[:, q * DH:(q + 1) * DH], stT[:, q * 128:(q + 1) * 128],
                                                      wvT[:, :], start=True, stop=True)
                            mm.then_inc(s_vp, 1)
                    if slot == 6 and F3:
                        upto(pe, s_t, 1, f3)
                        if F1:
                            upto(pe, s_v2, 1, f1)
                        for b in range(GI):
                            mm = nc.tensor.transpose(ps_f[:, b * S:(b + 1) * S], ts[:, p, b, 0:D], ident[0:S, 0:S])
                        mm.then_inc(s_tTp, 1)
                    if slot == 7:
                        if F3:
                            upto(pe, s_tT, 1, f3)
                            for b in range(GI):
                                mm = nc.tensor.matmul(ps_f[0:S, b * E:(b + 1) * E], tT[:, b * S:(b + 1) * S], wg_sb[:, :],
                                                      start=True, stop=True)
                            mm.then_inc(s_gtp, 1)
                        if A2:
                            upto(pe, s_bd, 1, g2)
                            upto(pe, s_v, 1, g2)
                            for q in range(Q):
                                mm = nc.tensor.matmul(ps_a2[:, 512 + q * DH:512 + (q + 1) * DH], bd[:, q, :], v_sb[:, q, :],
                                                      start=True, stop=True)
                            mm.then_inc(s_osp, 1)
                    if T and slot == 6:
                        patch_products(i, p, slot, 1)
                    if A3 and slot < 4:
                        token_outputs(g3, slot, 1 - p)
                    if C_:
                        contexts(gc_, uc, pc)
                    if F4 and slot == 3:
                        upto(pe, s_oh, 1, f4)
                        if F2:
                            upto(pe, s_s2, UNITS, f2, slot + 1)
                        upto(pe, s_base, 1, f4 - 1)
                        upto(pe, s_pos, 1, f4 - 1)
                        c0, c1 = RANK0, RANK0 + GI * E
                        nc.tensor.matmul(ps_s[0:S, c0:c1], triu[:, :], ohb[:, :, :].rearrange("p b e -> p (b e)"),
                                         start=True, stop=False)
                        for sh in range(1, GI):
                            nc.tensor.matmul(ps_s[0:S, c0 + sh * E:c1], ones[0:S, 0:S],
                                             ohb[:, 0:GI - sh, :].rearrange("p b e -> p (b e)"),
                                             start=False, stop=(sh == GI - 1))
                        for b in range(GI):
                            mm = nc.tensor.matmul(ps_s[0:S, c1:c1 + E], ones[0:S, 0:S], ohb[:, b, :],
                                                  start=(b == 0), stop=(b == GI - 1))
                        mm.then_inc(s_rp, 1)
                    if T and slot < 6:
                        patch_products(i, p, slot, 1)

            bodies(pe, body)
            pe_tail(pe)

        @block.scalar
        def _(act):
            act.preload_act_table(ACT.Exp)
            wt4 = w_tok[:, :, :].rearrange("p s n -> p (s n)")
            for k in range(TB):
                act.wait_ge(s_pe0, k + 1)
                n = min(4, STEPS - 4 * k) * 128
                nc.scalar.activation(wt4[:, 512 * k:512 * k + n], ps_a2[:, (k % 2) * 512:(k % 2) * 512 + n], ACT.Copy)\
                    .then_inc(s_act0, 1)

            def pixel_tail(n, p, c):
                if c == 0:
                    act.wait_ge(s_x[p], n * 16 * C * GI)
                px = xbuf[p].rearrange("p (a n) -> p a n", n=PS)
                copy(px[96:96 + PS, :, c * TAIL:(c + 1) * TAIL], px[32 * c:32 * c + PS, :, STEPS:PS], s_tail)

            def copy(dst, src, s):
                nc.scalar.activation(dst, src, ACT.Copy).then_inc(s, 1)

            pixel_tail(1, 0, 0)

            def body(i, j, p):
                g1, g2, g3, f1, f2, f3 = (i - k for k in range(1, 7))
                T, A1, A2, A3, F1, F2, F3 = (on(i, k) for k in range(7))
                for slot in range(8):
                    gc_, uc, C_ = (f3, 7, F3) if slot == 0 else (f2, slot - 1, F2)
                    if C_:
                        upto(act, s_eTp, UNITS, gc_, uc + 1)
                        upto(act, s_cp, UNITS, gc_, uc - 1)
                        copy(eT[:, uc % 2, :], ps_e[0:S, 0:UW], s_eT)
                    if F2:
                        upto(act, s_s2, UNITS, f2, slot + 1)
                        nc.scalar.activation(e2[:, slot % 2, :], e2[:, slot % 2, :], ACT.Exp).then_inc(s_e2, 1)
                    if slot == 0:
                        if A2:
                            upto(act, s_wTp, 1, g2)
                            upto(act, s_oxp, 4, g2 - 2)
                            copy(wT[:, p, :, :].rearrange("p (a q) s -> p a (q s)", a=2),
                                 ps_a2[:, :].rearrange("p (a n) -> p a n", a=2)[:, :, 0:4 * S], s_wT)
                        if A1:
                            upto(act, s_hT, 1, g1)
                            copy(part(hT_all, g1, 1), hT[:, :, :].rearrange("p b s -> p (b s)").unsqueeze(1), s_hTc)
                        if F1:
                            upto(act, s_x2, 1, f1)
                            upto(act, s_xaTp, 1, f1 - 1)
                            copy(xa[:, :, 0:D - 1], part(x_all, f1, GI)[:, :, 0:D - 1], s_xa)
                    if slot == 1 and F1:
                        upto(act, s_xaTp, 1, f1)
                        upto(act, s_vp2, 1, f1 - 1)
                        copy(xaT[:, :], ps_f[:, 0:R], s_xaT)
                    if slot == 2:
                        if A1:
                            upto(act, s_xnTp, 1, g1)
                            upto(act, s_lg, 2, g1 - 1)
                            copy(xnT[:, :], ps_a1[:, 0:R], s_xnT)
                        if A2:
                            upto(act, s_gTp, 1, g2)
                            copy(gn[:, :, :].rearrange("p q n -> p (q n)"), ps_a2[:, :], s_gT)
                        if F3:
                            upto(act, s_cTp, 1, f3)
                            upto(act, s_saP, 1, f3 - 1)
                            copy(cxT[:, :], ps_f[:, 0:R], s_cT)
                    if slot == 3:
                        if A2:
                            upto(act, s_stp, 1, g2)
                            copy(stT.rearrange("p (b h m) -> p h b m", b=GI, h=H),
                                 ps_a2[0:DH, :].rearrange("p (h b m) -> p h b m", b=GI, h=H), s_stT)
                            copy(pT[:, :].rearrange("p (b h m) -> p h b m", b=GI, h=H),
                                 ps_a2[DH:2 * DH, :].rearrange("p (h b m) -> p h b m", b=GI, h=H), s_pT)
                        if F1:
                            upto(act, s_qp, 1, f1)
                            upto(act, s_s2p, UNITS, f1 - 2)
                            copy(qT[:, p, :], ps_f[:, 0:R], s_q)
                    if slot == 4:
                        if F1:
                            upto(act, s_kp, 1, f1)
                            upto(act, s_km, UNITS, f1 - 2)
                            copy(kT[:, p, :], ps_f[:, 0:R], s_k)
                        if A3:
                            upto(act, s_oTp, 1, g3)
                            upto(act, s_hp2, 1, g3 - 1)
                            nc.scalar.activation(oT[:, :], ps_a3[:, 0:R], ACT.Identity, bias=bout_col[:, :]).then_inc(s_oT, 1)
                        if A1:
                            upto(act, s_sub1, 2, g1, 1)
                            nc.scalar.activation(w[:, 0:2, :], w[:, 0:2, :], ACT.Exp).then_inc(s_exp1, 1)
                        if A2:
                            upto(act, s_scp, 1, g2)
                            gp = ps_a2[:, :].rearrange("p (q n) -> p q n", q=Q)
                            for hl in range(4):
                                a = nc.scalar.activation(sc[32 * hl:32 * hl + 32, :, :],
                                                         gp[32 * hl:32 * hl + 32, :, 32 * hl:32 * hl + 32], ACT.Copy)
                            a.then_inc(s_sc, 1)
                    if slot == 5:
                        if A2:
                            upto(act, s_asub, 1, g2)
                            nc.scalar.activation(sc[:, :, :], sc[:, :, :], ACT.Exp).then_inc(s_aexp, 1)
                            upto(act, s_vp, 1, g2)
                            upto(act, s_osp, 1, g2 - 1)
                            copy(v_sb[:, :, :].rearrange("p q n -> p (q n)"), ps_a2[:, 0:Q * DH], s_v)
                        if A1:
                            upto(act, s_sub1, 2, g1)
                            nc.scalar.activation(w[:, 2:4, :], w[:, 2:4, :], ACT.Exp).then_inc(s_exp1, 1)
                        if F1:
                            upto(act, s_vp2, 1, f1)
                            upto(act, s_cp, UNITS, f1 - 2)
                            copy(va[:, p, :, :].rearrange("p b (h n) -> p (b h) n", n=VW)[:, :, 0:DH2],
                                 ps_f[0:S, :].rearrange("p (a n) -> p a n", n=DH2), s_v2)
                    if slot == 6:
                        if A3:
                            upto(act, s_hp2, 1, g3)
                            upto(act, s_x2, 1, g3 - 2)
                            if not isinstance(g3, int) or g3 >= 2:
                                act.wait_ge(s_hst[1 - p], 16 * ((g3 - 2) // 2 + 1 if isinstance(g3, int) else j - 2 + p))
                            copy(h2[:, 1 - p, :, :], ps_a3[0:S, :].rearrange("p (b n) -> p b n", b=GI), s_h2)
                        if F3:
                            upto(act, s_tTp, 1, f3)
                            upto(act, s_gtp, 1, f3 - 1)
                            copy(tT[:, :], ps_f[:, 0:R], s_tT)
                    if slot == 7 and A2:
                        upto(act, s_osp, 1, g2)
                        upto(act, s_oxp, 4, g2 - 1)
                        for hl in (0, 1):
                            a = nc.scalar.activation(osb[32 * hl:32 * hl + 32, :, hl * DH:(hl + 1) * DH],
                                                     ps_a2[32 * hl:32 * hl + 32, 512:1024].rearrange("p (q n) -> p q n", q=Q),
                                                     ACT.Copy)
                        a.then_inc(s_osb, 1)
                    if slot == 6 and T and (not isinstance(i, int) or i + 1 < G):
                        pixel_tail((i + 1) // 2 + 1 if isinstance(i, int) else j + p + 1, 1 - p, 0)
                    if A3 and slot < 4:
                        upto(act, s_oxp, 4, g3, slot + 1)
                        upto(act, s_oTp, 1, g3 - 1)
                        copy(oxT[:, slot, :], ps_a3[:, 0:R], s_ox)
                    if slot in (1, 3) and T:
                        pixel_tail(i // 2 + 1 if isinstance(i, int) else j + 1, p, (slot + 1) // 2)

            bodies(act, body, G - 2)
            act_tail(act)

        @block.vector
        def _(dve):
            v = nc.vector
            n0 = [0]

            def step(ins, name=None):
                n0[0] += 1
                if name is not None:
                    assert DVE0[name] == n0[0], (name, n0[0])
                ins.then_inc(s_dve0, 1)
                dve.wait_ge(s_dve0, n0[0])

            v.memset(xbuf[0], 0.0).then_inc(s_xz, 1)
            step(v.memset(osb[:, :, :], 0.0), "zeros")
            step(v.memset(bd[:, :, :], 0.0), "gaps")
            step(v.memset(xn[:, :, D - 1:D], 1.0), "aug1")
            step(v.memset(xa[:, :, D - 1:D], 1.0), "aug2")
            step(v.memset(va[:, :, :, :].rearrange("p a b n -> p (a b n)"), 1.0), "aug3")
            step(v.memset(wpad, 0.0), "pad_zero")
            dve.wait_ge(s_ld[0], 16)
            wn = wtok_nat.rearrange("p (c y x) -> p c y x", c=C, y=PS)
            wp = wpad.rearrange("p (s n) -> p s n", s=STEPS)
            for c in range(C):
                v.tensor_copy(wp[:, :, 32 * c:32 * c + PS], wn[:, c, :, 0:STEPS].rearrange("p y x -> p x y"))
                last = v.tensor_copy(wp[:, c * TAIL:(c + 1) * TAIL, 96:96 + PS],
                                     wn[:, c, :, STEPS:PS].rearrange("p y x -> p x y"))
            step(last, "wpad")
            dve.wait_ge(s_ld[2], 64)
            for nat, bias, n1, n2 in ((wx_nat, bx_nat, "wx1", "wx2"), (wfx_nat, bfx_nat, "wfx1", "wfx2")):
                step(v.tensor_tensor(nat[:, :, 0:D - 1], nat[:, :, 0:D - 1],
                                     nat[:, :, D - 1:D].broadcast_to([DH, H, D - 1]), ALU.subtract), n1)
                step(v.tensor_copy(nat[:, :, D - 1:D], bias.unsqueeze(2)), n2)
            dve.wait_ge(s_pool0, 8)
            v.memset(e_last[:, 0:D - 1], 0.0)
            v.memset(e_last[:, D - 1:D], 1.0)
            dve.wait_ge(s_pe0, TB + PE0["pos"])
            v.tensor_copy(idA[:, 0:DH], ident[0:DH, 0:DH])
            step(v.tensor_copy(wslT, ps_a1[0:DH, 0:M]), "wslT")
            step(v.tensor_copy(wvT[:, :], ps_a1[0:DH, 64:64 + DH]), "wvT")
            step(v.tensor_scalar(idA[:, DH:2 * DH], ps_a1[0:DH, 128:128 + DH], float(DH) ** -0.5, None, ALU.mult), "idA")
            step(v.tensor_copy(posT[:, :], ps_a1[:, 192:192 + S]), "pos")
            dve.wait_ge(s_ld[1], 48)
            step(v.tensor_scalar(hT[:, :, 0:1], posT[:, 0:1].unsqueeze(1).broadcast_to([D, GI, 1]), cls_col, None, ALU.mult), "cls")
            dve.wait_ge(s_ld[4], 48)
            step(v.reciprocal(itemp, temp_bc), "itemp")
            dve.wait_ge(s_pe0, TB + PE0["wlog"])
            step(v.tensor_tensor(w_log[:, :].rearrange("p (h m) -> p h m", h=H),
                                 ps_f[:, 0:H * M].rearrange("p (h m) -> p h m", h=H),
                                 itemp.unsqueeze(2).broadcast_to([D, H, M]), ALU.mult), "wlog")
            dve.wait_ge(s_pe0, TB + PE0["wstp"])
            step(v.tensor_copy(w_stp[:, :, :].rearrange("p h n -> p (h n)"), ps_a2[:, :]), "wstp")
            dve.wait_ge(s_pe0, TB + PE0["wout"])
            step(v.tensor_copy(woutT[:, :, :].rearrange("p h n -> p (h n)"), ps_a3[:, :]), "wout")
            dve.wait_ge(s_ld[5], 9 * 16)
            step(v.tensor_scalar(neg_keep, ident[:, D - 1:D], -1.0, None, ALU.add), "negk")
            step(v.scalar_tensor_tensor(wq_aug[:, :], lastq, neg_keep, natq, ALU.mult, ALU.add), "wqa")
            step(v.tensor_scalar(wq_aug[:, :], wq_aug[:, :], float(DH2) ** -0.5, None, ALU.mult), "wqs")
            step(v.scalar_tensor_tensor(wk_aug[:, :], lastk, neg_keep, natk, ALU.mult, ALU.add), "wka")
            step(v.scalar_tensor_tensor(wv_aug[:, :], lastv, neg_keep, natv, ALU.mult, ALU.add), "wva")
            dve.wait_ge(s_pads, 64)
            v.memset(xbuf[1], 0.0).then_inc(s_xz, 1)
            v.memset(zeros[:, :], 0.0)
            dve.wait_ge(s_ld[7], 96)
            dve.wait_ge(s_iota, 8)

            def norm_stats(name, src, s_chain, g):
                st, mv, ve, _ = lnb[name]
                for b in range(GI):
                    ins = v.bn_stats(st[0:S, b, :], src[:, b, :])
                ins.then_inc(s_chain, 1)
                upto(dve, s_chain, 3, g, 1)
                v.memset(pause[0:S, 0:1], 0.0)
                for b in range(GI):
                    ins = v.bn_aggr(mv[0:S, b, :], st[0:S, b, :])
                ins.then_inc(s_chain, 1)
                upto(dve, s_chain, 3, g, 2)
                v.tensor_scalar(ve[0:S, :].unsqueeze(2), mv[0:S, :, 1:2], EPS, None, ALU.add).then_inc(s_chain, 1)

            def norm_apply(name, dst, src, cols, s_r, s_done, g):
                _, mv, _, rs = lnb[name]
                upto(dve, s_r, 1, g)
                for b in range(GI):
                    ins = v.tensor_scalar(dst(b), src[:, b, 0:cols], mv[0:S, b, 0:1], rs[0:S, b:b + 1],
                                          ALU.subtract, ALU.mult)
                ins.then_inc(s_done, 1)

            def body(i, j, p):
                g1, g2, g3, f1, f2, f3, f4 = (i - k for k in range(1, 8))
                T, A1, A2, A3, F1, F2, F3, F4 = (on(i, k) for k in range(8))
                psh = ps_a1[0:S, :].rearrange("p (b n) -> p b n", b=GI)
                for slot in range(8):
                    gc_, uc, C_ = (f3, 7, F3) if slot == 0 else (f2, slot - 1, F2)
                    if F2:
                        sv = ps_s[0:S, 0:UW].rearrange("p (h n) -> p h n", h=UH)
                        upto(dve, s_s2p, UNITS, f2, slot + 1)
                        v.tensor_reduce(mx2[:, slot % 2, :], sv, AX, ALU.max).then_inc(s_s2m, 1)
                        upto(dve, s_s2m, UNITS, f2, slot + 1)
                        upto(dve, s_eTp, UNITS, f2, slot - 1)
                        v.tensor_tensor(e2[:, slot % 2, :].rearrange("p (h n) -> p h n", h=UH), sv,
                                        mx2[:, slot % 2, :].unsqueeze(2).broadcast_to([S, UH, S]), ALU.subtract)\
                            .then_inc(s_s2, 1)
                    if slot == 7:
                        if f1_next(i):
                            upto(dve, s_h2, 1, f1 + 1)
                            norm_stats("f1", h2[:, 1 - p, :, :], s_f1c, f1 + 1)
                        if T:
                            upto(dve, s_tok, 1, i)
                            upto(dve, s_hps, 1, g1)
                            upto(dve, s_hTc, 1, g1)
                            v.scalar_tensor_tensor(hT[:, :, 1:S], ps_t[:, 0:GI * NPP].rearrange("p (b n) -> p b n", b=GI),
                                                   b_tok[:, :], posT[:, 1:S].unsqueeze(1).broadcast_to([D, GI, NPP]),
                                                   ALU.add, ALU.mult).then_inc(s_hT, 1)
                    if slot == 0:
                        if F1:
                            norm_apply("f1", lambda b: part(x_all, f1 * GI + b, 1).rearrange("p o n -> p (o n)"),
                                       h2[:, p, :, :], D, s_f1r, s_x2, f1)
                        if F4:
                            upto(dve, s_gt, 1, f4)
                            v.tensor_reduce(rmx[:, 0, :], glb[:, :, :], AX, ALU.max).then_inc(s_oc, 1)
                            upto(dve, s_oc, 4, f4, 1)
                            v.tensor_tensor(eqb[:, :, :], glb[:, :, :], rmx[:, 0, :].unsqueeze(2).broadcast_to([S, GI, E]),
                                            ALU.is_equal).then_inc(s_oc, 1)
                            upto(dve, s_oc, 4, f4, 2)
                            v.tensor_tensor(eqb[:, :, :], eqb[:, :, :], wsc[:, :].unsqueeze(1).broadcast_to([S, GI, E]),
                                            ALU.mult).then_inc(s_oc, 1)
                            upto(dve, s_oc, 4, f4, 3)
                            v.tensor_reduce(rmx[:, 1, :], eqb[:, :, :], AX, ALU.max).then_inc(s_oc, 1)
                            upto(dve, s_oc, 4, f4)
                            upto(dve, s_rp, 1, f4 - 1)
                            v.tensor_tensor(ohb[:, :, :], eqb[:, :, :], rmx[:, 1, :].unsqueeze(2).broadcast_to([S, GI, E]),
                                            ALU.is_equal).then_inc(s_oh, 1)
                    if slot == 1:
                        if A1:
                            upto(dve, s_hps, 1, g1)
                            norm_stats("a1", psh, s_a1c, g1)
                        if A2:
                            gp = ps_a2[:, :].rearrange("p (q n) -> p q n", q=Q)
                            upto(dve, s_gp, 1, g2)
                            v.tensor_scalar(rn[:, :].unsqueeze(2), gp[:, :, D - 1:D], EPS, None, ALU.add).then_inc(s_gc, 1)
                            upto(dve, s_gc, 2, g2, 1)
                            v.reciprocal(rn[:, :], rn[:, :]).then_inc(s_gc, 1)
                            upto(dve, s_gc, 2, g2)
                            upto(dve, s_vp, 1, g2 - 1)
                            v.tensor_tensor(gn[:, :, :], gp, rn[:, :].unsqueeze(2).broadcast_to([128, Q, 128]),
                                            ALU.mult).then_inc(s_gn, 1)
                        if A1:
                            upto(dve, s_gp, 1, g2)
                            norm_apply("a1", lambda b: xn[:, b, 0:D - 1], psh, D - 1, s_a1r, s_xn, g1)
                    if slot == 3:
                        if F3:
                            upto(dve, s_saP, 1, f3)
                            upto(dve, s_xr, 1, f3)
                            v.tensor_tensor(xr[:, :, :], ps_f[0:S, :].rearrange("p (b n) -> p b n", b=GI), xr[:, :, :],
                                            ALU.add).then_inc(s_r3, 1)
                            upto(dve, s_r3, 1, f3)
                            norm_stats("f3", xr[:, :, :], s_f3c, f3)
                        if A1:
                            self_max(dve, v, g1, 0)
                    if slot == 4:
                        if F4:
                            c0, c1 = RANK0, RANK0 + GI * E
                            upto(dve, s_rp, 1, f4)
                            upto(dve, s_base, 1, f4 - 1)
                            v.tensor_tensor(rkb[:, :, :], ps_s[0:S, c0:c1].rearrange("p (b e) -> p b e", e=E),
                                            base[:, :].unsqueeze(1).broadcast_to([S, GI, E]), ALU.add).then_inc(s_rkc, 1)
                            upto(dve, s_rkc, 3, f4, 1)
                            v.tensor_tensor(base[:, :], base[:, :], ps_s[0:S, c1:c1 + E], ALU.add).then_inc(s_base, 1)
                            v.tensor_tensor(rkb[:, :, :], rkb[:, :, :], ohb[:, :, :], ALU.mult).then_inc(s_rkc, 1)
                            upto(dve, s_rkc, 3, f4, 2)
                            v.tensor_reduce(pos_f[:, :], rkb[:, :, :], AX, ALU.add).then_inc(s_rkc, 1)
                            upto(dve, s_rkc, 3, f4)
                            v.tensor_copy(pos_i[:, 1 - p, :], pos_f[:, :]).then_inc(s_pos, 1)
                        if F3:
                            norm_apply("f3", lambda b: xr[:, b, :], xr[:, :, :], D, s_f3r, s_tn, f3)
                    if slot == 5:
                        if A3:
                            upto(dve, s_oT, 1, g3)
                            upto(dve, s_hTc, 1, g3)
                            v.tensor_tensor(oT[:, :], oT[:, :], part(hT_all, g3, 1).rearrange("p o n -> p (o n)"), ALU.add)\
                                .then_inc(s_oTr, 1)
                        if A2:
                            upto(dve, s_sc, 1, g2)
                            v.tensor_reduce(smx[:, :], sc[:, :, :], AX, ALU.max).then_inc(s_ac, 1)
                            upto(dve, s_ac, 4, g2, 1)
                            v.tensor_tensor(sc[:, :, :], sc[:, :, :], smx[:, :].unsqueeze(2).broadcast_to([128, Q, M]),
                                            ALU.subtract).then_inc(s_asub, 1)
                        if A1:
                            self_max(dve, v, g1, 1)
                            weight_sums(g1, 0)
                        if F3:
                            if not isinstance(f3, int) or f3 >= 2:
                                dve.wait_ge(s_scat[p], 16 * GI * ((f3 - 2) // 2 + 1 if isinstance(f3, int) else j - 3))
                            tid = ts[:, p, :, D:D + 1]
                            v.tensor_scalar(tid, tid, float(2 * R), None, ALU.add).then_inc(s_id, 1)
                    if slot == 6 and A2:
                        upto(dve, s_aexp, 1, g2)
                        v.tensor_reduce(smx[:, :], sc[:, :, :], AX, ALU.add).then_inc(s_ac, 1)
                        upto(dve, s_ac, 4, g2, 2)
                        v.reciprocal(smx[:, :], smx[:, :]).then_inc(s_ac, 1)
                        upto(dve, s_ac, 4, g2, 3)
                        v.tensor_tensor(sc[:, :, :], sc[:, :, :], smx[:, :].unsqueeze(2).broadcast_to([128, Q, M]),
                                        ALU.mult).then_inc(s_ac, 1)
                        upto(dve, s_ac, 4, g2)
                        upto(dve, s_osp, 1, g2 - 1)
                        for hl in range(4):
                            ins = v.transpose(bd[32 * hl:32 * hl + 32, :, 32 * hl:32 * hl + 32], sc[32 * hl:32 * hl + 32, :, :])
                        ins.then_inc(s_bd, 1)
                    if C_:
                        c0 = 300 + (uc % 2) * UH * VW
                        cv = ps_e[0:S, c0:c0 + UH * VW].rearrange("p (h n) -> p h n", h=UH)
                        upto(dve, s_cp, UNITS, gc_, uc + 1)
                        v.reciprocal(rcx[:, uc % 2, :].unsqueeze(2), cv[:, :, DH2:VW]).then_inc(s_cr, 1)
                        upto(dve, s_cr, UNITS, gc_, uc + 1)
                        if uc == 0:
                            upto(dve, s_cTp, 1, gc_ - 2)
                        b, hf = uc // 2, uc % 2
                        v.tensor_tensor(cx[:, p if slot == 0 else 1 - p, b, hf * UH * DH2:(hf + 1) * UH * DH2].rearrange("p (h n) -> p h n", h=UH),
                                        cv[:, :, 0:DH2], rcx[:, uc % 2, :].unsqueeze(2).broadcast_to([S, UH, DH2]), ALU.mult)\
                            .then_inc(s_cx, 1)
                    if slot == 6:
                        if A1:
                            weight_sums(g1, 1)
                    if slot == 7:
                        if A2:
                            upto(dve, s_osp, 1, g2)
                            upto(dve, s_oxp, 4, g2 - 1)
                            for hl in (2, 3):
                                ins = v.tensor_copy(osb[32 * hl:32 * hl + 32, :, hl * DH:(hl + 1) * DH],
                                                    ps_a2[32 * hl:32 * hl + 32, 512:1024].rearrange("p (q n) -> p q n", q=Q))
                            ins.then_inc(s_osb, 1)
                        if F3:
                            upto(dve, s_gtp, 1, f3)
                            v.tensor_tensor(glb[:, :, :], ps_f[0:S, 0:GI * E].rearrange("p (b n) -> p b n", b=GI),
                                            bg_bc[:, :].unsqueeze(1).broadcast_to([S, GI, E]), ALU.add).then_inc(s_gt, 1)
            def weight_sums(g1, r):
                m = mx1[:, 2 * r * H:(2 * r + 2) * H]
                upto(dve, s_exp1, 2, g1, r + 1)
                v.tensor_reduce(m, w[:, 2 * r:2 * r + 2, :].rearrange("p b (h m) -> p (b h) m", m=M), AX, ALU.add).then_inc(s_ws, 1)
                upto(dve, s_ws, 2, g1, r + 1)
                v.reciprocal(m, m).then_inc(s_wc, 1)

            def f1_next(i):
                return on(i, 3)

            def self_max(dve, v, g1, r):
                lv = ps_a1[0:S, :].rearrange("p (a m) -> p a m", m=M)
                upto(dve, s_lg, 2, g1, r + 1)
                v.tensor_reduce(mx1[:, 2 * r * H:(2 * r + 2) * H], lv, AX, ALU.max).then_inc(s_mx1, 1)
                upto(dve, s_mx1, 2, g1, r + 1)
                upto(dve, s_gp, 1, g1 - 1)
                v.tensor_tensor(w[:, 2 * r:2 * r + 2, :].rearrange("p b (h m) -> p (b h) m", m=M), lv,
                                mx1[:, 2 * r * H:(2 * r + 2) * H].unsqueeze(2).broadcast_to([S, 2 * H, M]), ALU.subtract)\
                    .then_inc(s_sub1, 1)

            bodies(dve, body)
            dve_tail(dve)



_INS = ['x', 'L0_tok_W', 'L0_tok_b', 'L0_tok_class_token', 'L0_tok_pos_embed',
        'L0_attn_Wx', 'L0_attn_bx', 'L0_attn_Wfx', 'L0_attn_bfx', 'L0_attn_Wslice', 'L0_attn_bslice',
        'L0_attn_Wq', 'L0_attn_Wk', 'L0_attn_Wv', 'L0_attn_Wout', 'L0_attn_bout', 'L0_attn_temperature',
        'L0_ffn_Wq', 'L0_ffn_bq', 'L0_ffn_Wk', 'L0_ffn_bk', 'L0_ffn_Wv', 'L0_ffn_bv', 'L0_ffn_Wo', 'L0_ffn_bo',
        'L0_ffn_g1', 'L0_ffn_beta1', 'L0_ffn_g2', 'L0_ffn_beta2', 'L0_ffn_Wg', 'L0_ffn_bg',
        'L0_ffn_W1', 'L0_ffn_b1', 'L0_ffn_W2', 'L0_ffn_b2']
_OUTS = [((64, 65, 128), 'float32')]


def kernel(**inputs):
    import numpy as _np
    import concourse.bacc as _bacc
    from concourse import mybir as _mybir
    from concourse.bass_utils import run_bass_kernel_spmd as _run

    nc = _bacc.Bacc("TRN2", target_bir_lowering=False, num_devices=1)
    arrays, args = {}, []
    for name in _INS:
        a = _np.ascontiguousarray(inputs[name])
        arrays[f"in_{name}"] = a
        args.append(nc.dram_tensor(f"in_{name}", a.shape, _mybir.dt.from_np(a.dtype), kind="ExternalInput").ap())
    for i, (shape, dtype) in enumerate(_OUTS):
        dt = _mybir.dt.from_np(_np.dtype(dtype))
        args.append(nc.dram_tensor(f"out_{i}", shape, dt, kind="ExternalOutput").ap())
    vit_tower_kernel(nc, *args)
    r = _run(nc, [arrays], core_ids=[0])
    return r.results[0]["out_0"]
```

```python
import concourse.bass as bass
from concourse import mybir
from contextlib import ExitStack


def vit_tower_kernel(nc, x, tok_w, tok_b, tok_cls, tok_pos,
                     wx, bx, wfx, bfx, wslice, bslice, wq, wk, wv, wout, bout, temp,
                     f_wq, f_bq, f_wk, f_bk, f_wv, f_bv, f_wo, f_bo, g1, beta1, g2, beta2,
                     wg, bg, w1, b1, w2, b2, out):
    fp32 = mybir.dt.float32
    int32 = mybir.dt.int32
    ALU = mybir.AluOpType
    ACT = mybir.ActivationFunctionType
    AX = mybir.AxisListType.X

    B, C, IMG, _ = x.shape
    D = tok_w.shape[0]
    S = tok_pos.shape[0]
    NP = 8
    PS = IMG // NP
    NPP = NP * NP
    GI = 4
    G = B // GI
    R = GI * S
    H, M = temp.shape[1], wslice.shape[0]
    DH = wslice.shape[1]
    HH = H // 4
    Q = GI * HH
    DH2 = D // H
    E, _, HID = w1.shape
    HC = HID // D
    TAIL = PS // (C + 1)
    STEPS = PS - TAIL
    assert C == 3 and STEPS == C * TAIL and 4 * M == 128 and D == 128
    T128 = 128
    NT = (B * S) // T128 + E
    EPS = 1e-5
    UNITS = 2 * GI
    UH = H // 2
    UW = UH * S
    VW = DH2 + 1
    T_SLOT = [2, 2, 2, 3, 3, 3, 3, 3]
    T_FIRST = [0, 1, 1, 2, 2, 2, 1, 3]
    RANK0 = 300
    assert sum(T_SLOT) == STEPS and G % 2 == 0 and G >= 10
    LOOP0 = 8
    LAST = G + 7
    RW = D + 4
    REG = -(-(B * S) // T128) * T128 + T128
    NONE = E * REG
    BLANK = 2 * E * T128

    ctx = ExitStack()
    with ctx:
        def sb(name, shape, dt=fp32):
            return ctx.enter_context(nc.sbuf_tensor(name, shape, dt))

        def ps(name, cols=512):
            return ctx.enter_context(nc.psum_tensor(name, [128, cols], fp32))

        def sem(name):
            return ctx.enter_context(nc.semaphore(name))

        xs_dram = nc.dram_tensor("rows_by_expert", (E * REG + E * T128, RW), fp32, kind="Internal").ap()
        blank_dram = nc.dram_tensor("blank_rows", (E * T128, RW), fp32, kind="Internal").ap()
        h_dram = nc.dram_tensor("h_rows", (B * S + BLANK, D), fp32, kind="Internal").ap()

        XCOLS = GI * NP * IMG
        arena = sb("arena", [128, 2 * XCOLS])
        xbuf = [arena[:, p * XCOLS:(p + 1) * XCOLS] for p in range(2)]
        W1C = HID + HC
        w1_sb = arena[:, 0:E * W1C].rearrange("p (e n) -> p e n", e=E)
        a0 = E * W1C
        w2_sb = arena[:, a0:a0 + E * HID].rearrange("p (e c n) -> p e c n", e=E, c=HC)
        a0 += E * HID
        b2_bc = arena[:, a0:a0 + E * D].rearrange("p (e n) -> p e n", e=E)
        b1_nat = arena[0:E * HC, a0 + E * D:a0 + E * D + D]
        x_all = sb("x_all", [S, B, D])
        hT_all = sb("hT_all", [D, G, R])

        ident = sb("ident", [128, 128])
        ones = sb("ones", [S, 128])
        triu = sb("triu", [S, S])
        head_mask = sb("head_mask", [128, H])
        mhalf = sb("mhalf", [128, GI])
        w_tok = sb("w_tok", [128, STEPS, D])
        b_tok = sb("b_tok", [D, 1])
        posT = sb("posT", [D, S])
        w_log = sb("w_log", [D, H * M])
        w_stp = sb("w_stp", [D, H, 2 * DH])
        woutT = sb("woutT", [128, 4, D])
        bout_col = sb("bout_col", [D, 1])
        wq_aug = sb("wq_aug", [D, D])
        wk_aug = sb("wk_aug", [D, D])
        wv_aug = sb("wv_aug", [D, D])
        wo_sb = sb("wo_sb", [D, D])
        wg_sb = sb("wg_sb", [D, E])
        bo_bc = sb("bo_bc", [S, D])
        g1_bc = sb("g1_bc", [S, D])
        beta1_bc = sb("beta1_bc", [S, D])
        g2_bc = sb("g2_bc", [128, D])
        beta2_bc = sb("beta2_bc", [128, D])
        bg_bc = sb("bg_bc", [S, E])

        hT = sb("hT", [D, GI, S])
        xn = sb("xn", [S, GI, D])
        xnT = sb("xnT", [D, R])
        w = sb("w", [S, GI, H * M])
        mx1 = sb("mx1", [S, GI * H])
        wT = sb("wT", [128, 2, Q, S])
        gn = sb("gn", [128, Q, 128])
        gnT = gn[:, :, :].rearrange("p (b hh) (hl m) -> p b hh hl m", b=GI, hl=4)
        stT = gn[0:DH, :, :].rearrange("p q n -> p (q n)")
        pT = sb("pT", [DH, GI * H * M])
        rn = sb("rn", [128, Q])
        sc = sb("sc", [128, Q, M])
        smx = sb("smx", [128, Q])
        v_sb = sb("v_sb", [128, Q, DH])
        bd = sb("bd", [128, Q, 128])
        osb = sb("osb", [128, Q, 4 * DH])
        oxT = sb("oxT", [128, 4, R])
        oT = sb("oT", [D, R])
        h2 = sb("h2", [S, 2, GI, D])
        xa = sb("xa", [S, GI, D])
        xaT = sb("xaT", [D, R])
        qT = sb("qT", [D, 2, R])
        kT = sb("kT", [D, 2, R])
        va = sb("va", [S, 2, GI, H * VW])
        km = sb("km", [D, 2, UH, S])
        e2 = sb("e2", [S, 2, UW])
        eT = sb("eT", [S, 2, UW])
        mx2 = sb("mx2", [S, 2, UH])
        rcx = sb("rcx", [S, 2, UH])
        cx = sb("cx", [S, 2, GI, D])
        cxT = sb("cxT", [D, R])
        xr = sb("xr", [S, GI, D])
        ts = sb("ts", [S, 2, GI, RW])
        tT = sb("tT", [D, R])
        pause = sb("pause", [128, 2])
        pool_pause_out = sb("pool_pause_out", [1, 1])
        glb = sb("glb", [S, GI, E])
        eqb = sb("eqb", [S, GI, E])
        ohb = sb("ohb", [S, GI, E])
        rkb = sb("rkb", [S, GI, E])
        rmx = sb("rmx", [S, 2, GI])
        wsc = sb("wsc", [S, E])
        room = sb("room", [S, E])
        base = sb("base", [S, E])
        pos_f = sb("pos_f", [S, GI])
        pos_i = sb("pos_i", [S, 2, GI], int32)
        lnb = {n: (sb(f"st_{n}", [128, GI, 6]), sb(f"mv_{n}", [128, GI, 2]),
                   sb(f"ve_{n}", [128, GI]), sb(f"rs_{n}", [128, GI])) for n in ("a1", "f1", "f3")}

        ps_t = ps("ps_t")
        ps_a1 = ps("ps_a1")
        ps_a2 = ps("ps_a2", 1024)
        ps_a3 = ps("ps_a3")
        ps_f = ps("ps_f")
        ps_s = ps("ps_s")
        ps_e = ps("ps_e")

        s_ld = [sem(f"weights_loaded{k}") for k in range(8)]
        s_x = [sem(f"pixels_loaded{p}") for p in range(2)]
        s_hst = [sem(f"h_rows_stored{p}") for p in range(2)]
        s_moew = sem("expert_weights_loaded")
        s_dve0 = sem("setup_dve")
        s_pool0 = sem("setup_pool")
        s_pe0 = sem("setup_pe")
        s_wt = sem("patch_weights")
        s_xz = sem("pixel_buffers_zeroed_by_pool")
        s_xzd = sem("pixel_buffer_zeroed_by_dve")
        s_wv2 = sem("wv_blocks_zeroed")
        s_ldv = sem("wv_blocks_loaded")
        s_gapz = sem("blocks_zeroed")
        s_tail = sem("pixel_tail_copied")
        s_tok = sem("patch_products")
        s_hT = sem("tokens_transposed")
        s_hTc = sem("tokens_transposed_kept")
        s_hps = sem("tokens_in_psum")
        s_a1c = sem("a1_norm_chain")
        s_a1r = sem("a1_rstd")
        s_xn = sem("a1_normed")
        s_xnTp = sem("a1_normed_T_psum")
        s_xnT = sem("a1_normed_T")
        s_lg = sem("slice_logits")
        s_mx1 = sem("slice_max")
        s_sub1 = sem("slice_logits_less_max")
        s_exp1 = sem("slice_exp")
        s_ws = sem("slice_weight_sums")
        s_wc = sem("slice_weight_recips")
        s_w = sem("slice_weights")
        s_wTp = sem("slice_weights_T_psum")
        s_wT = sem("slice_weights_T")
        s_gp = sem("slice_sums_psum")
        s_gc = sem("slice_sum_chain")
        s_gn = sem("slice_means")
        s_gTp = sem("slice_means_T_psum")
        s_gT = sem("slice_means_T")
        s_stp = sem("slice_tokens_psum")
        s_stT = sem("slice_tokens_T")
        s_pT = sem("slice_queries_T")
        s_scp = sem("slice_scores_psum")
        s_sc = sem("slice_scores")
        s_vp = sem("slice_token_rows_psum")
        s_v = sem("slice_token_rows")
        s_ac = sem("slice_attention_chain")
        s_asub = sem("slice_scores_less_max")
        s_aexp = sem("slice_scores_exp")
        s_bd = sem("slice_attention_T")
        s_osp = sem("slice_outputs_psum")
        s_osb = sem("slice_outputs")
        s_oxp = sem("token_outputs_psum")
        s_ox = sem("token_outputs")
        s_oTp = sem("output_product_psum")
        s_oT = sem("output_product_T")
        s_oTr = sem("output_with_residual")
        s_hp2 = sem("h_in_psum")
        s_h2 = sem("h_rows")
        s_f1c = sem("f1_norm_chain")
        s_f1r = sem("f1_rstd")
        s_x2 = sem("f1_normed_rows")
        s_xa = sem("f1_normed_aug")
        s_xaTp = sem("f1_normed_T_psum")
        s_xaT = sem("f1_normed_T")
        s_qp = sem("q_psum")
        s_q = sem("q_ready")
        s_kp = sem("k_psum")
        s_k = sem("k_ready")
        s_vp2 = sem("v_psum")
        s_v2 = sem("v_ready")
        s_km = sem("k_masked")
        s_s2p = sem("scores_psum")
        s_s2m = sem("scores_max")
        s_s2 = sem("scores_less_max")
        s_e2 = sem("scores_exp")
        s_eTp = sem("exp_T_psum")
        s_eT = sem("exp_T")
        s_cp = sem("context_psum")
        s_cr = sem("context_sum_recip")
        s_cx = sem("context")
        s_cTp = sem("context_T_psum")
        s_cT = sem("context_T")
        s_xr = sem("f3_residual_and_bias")
        s_saP = sem("attention_out_psum")
        s_r3 = sem("f3_sum")
        s_f3c = sem("f3_norm_chain")
        s_f3r = sem("f3_rstd")
        s_tn = sem("f3_normed")
        s_tg = sem("f3_scaled")
        s_t = sem("t_rows")
        s_tTp = sem("t_T_psum")
        s_tT = sem("t_T")
        s_gtp = sem("gate_psum")
        s_gt = sem("gate_logits")
        s_oc = sem("first_largest_chain")
        s_oh = sem("expert_chosen")
        s_rp = sem("ranks_psum")
        s_rkc = sem("row_number_chain")
        s_pos = sem("row_numbers")
        s_base = sem("counts_so_far")
        s_id = sem("token_numbers")
        s_scat = [sem(f"rows_sent{p}") for p in range(2)]

        NTH = -(-(B * S) // T128)
        NR = 4
        cnt, nt, ntc, step_e = (sb(n_, [1, E]) for n_ in ("cnt", "nt", "ntc", "step_e"))
        tail_rows = hT_all[0:1, :, :].rearrange("p g r -> p (g r)")
        cmp_nt = tail_rows[:, 0:E * NTH].rearrange("p (e n) -> p e n", e=E)
        le, lew = (tail_rows[:, k * E * NT:(k + 1) * E * NT].rearrange("p (t e) -> p t e", e=E) for k in (1, 2))
        thr = sb("thr", [1, NTH])
        tix = sb("tix", [1, NT])
        tixe = sb("tixe", [1, NT])
        tef = sb("tef", [1, 2, NT])
        NJ = NT // 4 + 1
        te_f = sb("te_f", [1, 2 + 4 * NJ])
        digit = sb("digit", [1, 4])
        pk_f = sb("pk_f", [1, NJ, 4])
        pk_s = sb("pk_s", [1, 2, NJ])
        pk_i = sb("pk_i", [1, 2, NJ], int32)
        pk_w1, pk_w2 = pk_i[:, 0, :], pk_i[:, 1, :]
        tr_i = sb("tr_i", [1, NT], int32)
        pad_i = sb("pad_i", [1, E], int32)
        zeros = sb("zeros", [1, E])
        xt = osb[:, 0:3, :].rearrange("p a n -> p (a n)")[:, 0:NR * RW].rearrange("p (a n) -> p a n", a=NR)
        xb = osb[:, 4:6, :].rearrange("p a n -> p (a n)").rearrange("p (a n) -> p a n", a=NR)
        zb = osb[:, 6:8, :].rearrange("p a n -> p (a n)").rearrange("p (a n) -> p a n", a=NR)
        xtT = km[:, :, :, :].rearrange("p a h n -> p a (h n)")[:, :, 0:128]
        w1c = oxT[:, :, :].rearrange("p a n -> p (a n)")[:, 0:2 * W1C].rearrange("p (a n) -> p a n", a=2)
        hbT = bd[:, :, :].rearrange("p (a q) n -> p a q n", a=2)
        idf = sb("idf", [128, NR])
        idx = sb("idx", [128, NR], int32)
        st_m, mv_m, ve_m, rs_m = (sb("st_m", [128, 6]), sb("mv_m", [128, 2, 2]), sb("ve_m", [128, 2]), sb("rs_m", [128, 2]))

        s_iota = sem("routing_constants")
        s_rc = sem("tile_table_chain")
        s_padi = sem("blank_rows_places")
        s_tbl = sem("tile_tables")
        s_pk = sem("packed_experts")
        s_padt = sem("pad_tile")
        s_pause = sem("pool_paused")
        s_pads = sem("pads_written")
        s_xt = [sem(f"tile_rows_loaded{q}") for q in range(4)]
        s_xtP = sem("tile_T_psum")
        s_xtT = sem("tile_T")
        s_w1 = sem("hidden_psum")
        s_xb = sem("tile_rows_and_bias")
        s_b1p = sem("b1_columns_psum")
        s_b1 = sem("b1_columns")
        s_w1c = sem("tile_w1")
        s_gl = sem("hidden_gelu")
        s_w2 = sem("expert_out_psum")
        s_ix = sem("tile_token_numbers")
        s_rz = sem("expert_sum")
        s_mc = sem("tile_norm_chain")
        s_mr = sem("tile_rstd")
        s_mn = sem("tile_centred")
        s_z = sem("tile_done")
        s_zadd = [sem(f"tile_added{q}") for q in range(4)]
        s_out = sem("out_stored")

        def tile_bodies(eng, body, last=NT):
            for k in range(8):
                body(k, k // 4, k % 4)
            with eng.Fori(2, last // 4, 1) as j:
                for q in range(4):
                    body(j * 4 + q, j, q)
            for k in range(last // 4 * 4, NT + 5):
                body(k, k // 4, k % 4)

        def tile(k, lag):
            return 0 <= k - lag < NT if isinstance(k, int) else True

        def entry(t, k):
            return t[0:1, k:k + 1] if isinstance(k, int) else t[0:1, bass.ds(k, 1)]

        PACK = 4

        def tile_experts(eng, table, lag):
            held = {}

            def expert(k, j, q):
                if q == 0 and any(tile(k + n, lag) for n in range(PACK)):
                    held[0] = eng.value_load(entry(table, j), min_val=0, max_val=E ** PACK - 1)
                if not tile(k, lag):
                    return None
                return (held[0] // E ** q) % E

            return expert

        block = ctx.enter_context(nc.Block())

        def upto(eng, s, per, g, k=None):
            n = g * per + (per if k is None else k)
            if isinstance(g, int) and n <= 0:
                return
            eng.wait_ge(s, n)

        def bodies(eng, body, end=G, start=0):
            for i in range(start, LOOP0):
                body(i, i // 2, i % 2)
            with eng.Fori(LOOP0 // 2, end // 2, 1) as j:
                for p in range(2):
                    body(j * 2 + p, j, p)
            for i in range(end, LAST):
                body(i, i // 2, i % 2)

        def part(t, g, n):
            return t[:, g * n:(g + 1) * n] if isinstance(g, int) else t[:, bass.ds(g * n, n)]

        def on(i, lag):
            return 0 <= i - lag < G if isinstance(i, int) else True

        DVE0 = {}
        n = 0
        for name in ("pad_zero", "wpad", "aug1", "aug2", "aug3", "wx1", "wx2", "wfx1", "wfx2", "wslT", "idA",
                     "pos", "cls", "itemp", "wlog", "wstp", "wout", "negk", "wqa", "wqs", "wka", "wva", "wvo"):
            n += 1
            DVE0[name] = n
        PE0 = {name: k + 1 for k, name in enumerate(("wslT", "A", "pos", "wlog", "wstp", "wout", "wvo"))}
        TB = (STEPS + 3) // 4

        wtok_nat = xbuf[1][:, 0:C * PS * PS]
        assert C * PS * PS == tok_w.shape[1]
        wpad = xbuf[1][:, C * PS * PS:C * PS * PS + STEPS * 128]
        hT_cols = hT_all[:, :, :].rearrange("p g r -> p (g r)")
        blank = [hT_cols[:, c0:c0 + E * RW].rearrange("p (e n) -> p e n", e=E) for c0 in (7 * R, 7 * R + E * RW)]
        wx_nat = x_all[0:DH, 3 * H:4 * H, :]
        wfx_nat = x_all[0:DH, 0:H, :]
        wout_nat = hT_all[:, 0:2, 0:256].rearrange("p a n -> p a n")
        wq_nat = x_all[0:DH, H, 0:DH]
        wk_nat = x_all[0:DH, H, DH:2 * DH]
        wv2 = kT[:, 0, 0:2 * DH]
        wout_raw = km[:, :, :, :].rearrange("p a h n -> p (a h n)")[:, 0:4 * D]
        wsl_nat = x_all[0:M, H + 2, 0:DH]
        wslT = x_all[0:DH, H + 3, 0:M]
        idA = x_all[0:DH, H + 4, :]
        pos_nat = x_all[0:S, H + 5, :]
        bsl_row = x_all[0:1, H + 6:H + 8, :]
        e_last = x_all[0:1, H + 8, :]
        bx_nat = x_all[0:DH, H + 9, 0:H]
        bfx_nat = x_all[0:DH, H + 9, H:2 * H]
        temp_bc = hT_all[:, 3, 0:H]
        itemp = hT_all[:, 3, H:2 * H]
        cls_col = hT_all[:, 3, 2 * H:2 * H + 1]
        neg_keep = hT_all[:, 3, 2 * H + 1:2 * H + 2]
        lastq = hT_all[:, 4, 0:D]
        lastk = hT_all[:, 5, 0:D]
        lastv = hT_all[:, 6, 0:D]
        natq = hT_all[:, 4, D:2 * D]
        natk = hT_all[:, 5, D:2 * D]
        natv = hT_all[:, 6, D:2 * D]

        def row(a, n=128):
            return a.rearrange("(o n) -> o n", o=1).broadcast_to([n, a.shape[0]])

        def image_of(p, b):
            return xbuf[p][:, b * NP * IMG:(b + 1) * NP * IMG]

        def load_pixels(eng, g, p, zeroed=None):
            if not isinstance(g, int) or g >= 2:
                upto(eng, s_tok, 1, g - 2)
            for b in range(GI):
                if zeroed is not None:
                    eng.wait_ge(*zeroed[b])
                for c in range(C):
                    src = x[bass.ds(g * GI + b, 1), c, :, :].rearrange("o h w -> (o h) w") if not isinstance(g, int) \
                        else x[g * GI + b, c, :, :]
                    dst = image_of(p, b)[32 * c:32 * c + PS, :].rearrange("p (a w) -> p a w", a=NP)
                    eng.dma_start(dst, src.rearrange("(a y) w -> y a w", y=PS)).then_inc(s_x[p], 16)

        def blank_rows(eng, experts):
            eng.wait_ge(s_padi, 1)
            for e in experts:
                first = eng.value_load(entry(pad_i, e), min_val=0, max_val=NONE)
                eng.dma_start(xs_dram[bass.ds(first, T128), :], blank_dram[e * T128:(e + 1) * T128, :]).then_inc(s_pads, 16)

        def sp_tail(sp):
            blank_rows(sp, range(0, 4))
            sp.wait_ge(s_tbl, 1)
            firsts = [sp.value_load(entry(tr_i, k), min_val=0, max_val=NONE + (E - 1) * T128) for k in range(3)]
            for p in range(2):
                sp.wait_ge(s_scat[p], 16 * GI * (G // 2))
            sp.wait_ge(s_pads, 16 * (E + 4))

            def load(k, j, q):
                first = firsts[k] if isinstance(k, int) and k < 3 else sp.value_load(entry(tr_i, k), min_val=0, max_val=NONE + (E - 1) * T128)
                upto(sp, s_xtP, 1, k - NR)
                upto(sp, s_xb, 1, k - NR)
                sp.dma_start(xt[:, q, :], xs_dram[bass.ds(first, T128), :]).then_inc(s_xt[q], 16)

            for k in range(3):
                load(k, 0, k)

            def body(k, j, q):
                if not isinstance(k, int) or k + 3 < NT:
                    load(k + 3, j, (q + 3) % NR)

            tile_bodies(sp, body, NT - 4)
            for q in range(NR):
                sp.wait_ge(s_zadd[q], 16 * (NT // NR))
            sp.dma_start(out.rearrange("b s d -> b (s d)"), h_dram[0:B * S, :].rearrange("(b s) d -> b (s d)", s=S)).then_inc(s_out, 16)
            sp.wait_ge(s_out, 16)

        def pool_pause(n):
            upto(nc.gpsimd, s_pause, 1, n - 1)
            nc.gpsimd.tensor_tensor(pool_pause_out[:, :], ones[0:1, 0:1], ones[0:1, 0:1], ALU.add).then_inc(s_pause, 1)

        def pool_tail(pool):
            for p in range(2):
                pool.wait_ge(s_hst[p], 16 * (G // 2))
            pool.wait_ge(s_pads, 16 * (E + 4))

            def body(k, j, q):
                if tile(k, 5):
                    t, d = k - 5, (q + 3) % NR
                    upto(pool, s_z, 1, t)
                    upto(pool, s_ix, 1, t)
                    pool_pause(G + t)
                    pool.indirect_dma_start(h_dram, bass.IndirectOffsetOnAxis(ap=idx[:, d:d + 1], axis=0),
                                            zb[:, d, :], None, compute_op=ALU.add).then_inc(s_zadd[d], 16)
                if tile(k, 3):
                    t, a = k - 3, (q + 1) % 2
                    upto(pool, s_mc, 3, t)
                    nc.gpsimd.tensor_tensor(rs_m[:, a:a + 1], ve_m[:, a:a + 1], mhalf[:, 0:1], ALU.pow).then_inc(s_mr, 1)

            tile_bodies(pool, body)

        def pe_tail(pe):
            pe.wait_ge(s_moew, 64)
            upto(pe, s_base, 1, G - 1)
            nc.tensor.transpose(ps_a1[:, 0:E * HC], b1_nat, ident[0:E * HC, 0:E * HC]).then_inc(s_b1p, 1)
            pe.wait_ge(s_pk, 1)
            expert = tile_experts(pe, pk_w2, 2)
            ps_x = (ps_s, ps_e)
            ps_y = (ps_a3, ps_f)

            def body(k, j, q):
                a, o_ = q % 2, (q + 1) % 2
                ed = expert(k, j, q)
                if tile(k, 0):
                    pe.wait_ge(s_xt[q], (j + 1) * 16)
                    upto(pe, s_xtT, 1, k - 2)
                    nc.tensor.transpose(ps_x[a][:, 0:D], xt[:, q, 0:D], ident[:, :]).then_inc(s_xtP, 1)
                if tile(k, 1):
                    upto(pe, s_xtT, 1, k - 1)
                    upto(pe, s_w1c, 1, k - 1)
                    upto(pe, s_gl, 1, k - 3)
                    for c in range(HC):
                        c0 = o_ * HID + c * 128
                        mm = nc.tensor.matmul(ps_a2[:, c0:c0 + 128], w1c[:, o_, c * 128:(c + 1) * 128], xtT[:, o_, :],
                                              start=True, stop=True)
                    mm.then_inc(s_w1, 1)
                if tile(k, 2):
                    upto(pe, s_gl, 1, k - 2)
                    upto(pe, s_rz, 1, k - 4)
                    for c in range(HC):
                        mm = nc.tensor.matmul(ps_y[a][:, 0:D], hbT[:, a, c, :],
                                              w2_sb[:, bass.ds(ed, 1), c, :].rearrange("p o n -> p (o n)"),
                                              start=(c == 0), stop=(c == HC - 1))
                    mm.then_inc(s_w2, 1)

            tile_bodies(pe, body)

        def act_tail(act):
            blank_rows(act, range(4, E))
            act.preload_act_table(ACT.Gelu)

            act.wait_ge(s_moew, 64)
            act.wait_ge(s_pk, 1)
            act.wait_ge(s_b1, 1)
            expert = tile_experts(act, pk_w1, 0)
            ps_x = (ps_s, ps_e)

            def body(k, j, q):
                a, o_ = q % 2, (q + 1) % 2
                ea = expert(k, j, q)
                if tile(k, 0):
                    upto(act, s_xtP, 1, k)
                    upto(act, s_w1, 1, k - 2)
                    upto(act, s_gl, 1, k - 2)
                    nc.scalar.activation(xtT[:, a, :], ps_x[a][:, 0:D], ACT.Copy).then_inc(s_xtT, 1)
                    nc.scalar.activation(w1c[:, a, :], w1_sb[:, bass.ds(ea, 1), :].rearrange("p o n -> p (o n)"), ACT.Copy)\
                      .then_inc(s_w1c, 1)
                if tile(k, 1):
                    upto(act, s_w1, 1, k - 1)
                    upto(act, s_w1c, 1, k - 1)
                    upto(act, s_w2, 1, k - 3)
                    for c in range(HC):
                        c0 = o_ * HID + c * 128
                        g = nc.scalar.activation(hbT[:, o_, c, :], ps_a2[:, c0:c0 + 128], ACT.Gelu,
                                                 bias=w1c[:, o_, HID + c:HID + c + 1])
                    g.then_inc(s_gl, 1)

            tile_bodies(act, body)

        RC = {name: k + 1 for k, name in enumerate((
            "pad", "cnt", "cmp", "nt", "ntc", "step", "le", "te", "lew", "row", "row2", "tef", "pk1", "pk1s", "pk2", "pk2s", "pki"))}

        def dve_tail(dve):
            v = nc.vector
            done = [0]

            def step(ins, name):
                done[0] += 1
                assert RC[name] == done[0], name
                ins.then_inc(s_rc, 1)
                dve.wait_ge(s_rc, done[0])

            upto(dve, s_base, 1, G - 1)
            step(v.tensor_scalar(pad_i[:, :], base[0:1, :], 1.0, None, ALU.add), "pad")
            v.memset(pause[:, 1:2], 0.0).then_inc(s_padi, 1)
            step(v.tensor_tensor(cnt[:, :], base[0:1, :], room[0:1, :], ALU.subtract), "cnt")
            step(v.tensor_tensor(cmp_nt[:, :, :], cnt[:, :].unsqueeze(2).broadcast_to([1, E, NTH]),
                                 thr[:, :].unsqueeze(1).broadcast_to([1, E, NTH]), ALU.is_gt), "cmp")
            step(v.tensor_reduce(nt[:, :], cmp_nt[:, :, :], AX, ALU.add), "nt")
            step(v.tensor_tensor_scan(ntc[:, :], nt[:, :], zeros[:, :], 0.0, ALU.add, ALU.add), "ntc")
            step(v.tensor_scalar(step_e[:, :], nt[:, :], -float(T128), float(REG), ALU.mult, ALU.add), "step")
            step(v.tensor_tensor(le[:, :, :], ntc[:, :].unsqueeze(1).broadcast_to([1, NT, E]),
                                 tixe[:, :].unsqueeze(2).broadcast_to([1, NT, E]), ALU.is_le), "le")
            step(v.tensor_reduce(tef[:, 0, :], le[:, :, :], AX, ALU.add), "te")
            step(v.tensor_tensor(lew[:, :, :], le[:, :, :], step_e[:, :].unsqueeze(1).broadcast_to([1, NT, E]), ALU.mult), "lew")
            step(v.tensor_reduce(tef[:, 1, :], lew[:, :, :], AX, ALU.add), "row")
            step(v.tensor_tensor(tr_i[:, :], tef[:, 1, :], tix[:, :], ALU.add), "row2")
            v.memset(pause[:, 0:1], 0.0).then_inc(s_tbl, 1)
            step(v.tensor_scalar(te_f[:, 2:2 + NT], tef[:, 0, :], float(E - 1), None, ALU.min), "tef")
            for first, packed, n1, n2 in ((2, 0, "pk1", "pk1s"), (0, 1, "pk2", "pk2s")):
                step(v.tensor_tensor(pk_f[:, :, :], te_f[:, first:first + 4 * NJ].rearrange("p (j n) -> p j n", n=4),
                                     digit[:, :].unsqueeze(1).broadcast_to([1, NJ, 4]), ALU.mult), n1)
                step(v.tensor_reduce(pk_s[:, packed, :], pk_f[:, :, :], AX, ALU.add), n2)
            step(v.tensor_copy(pk_i[:, :, :], pk_s[:, :, :]), "pki")
            v.memset(pause[:, 1:2], 0.0).then_inc(s_pk, 1)
            dve.wait_ge(s_moew, 64)
            dve.wait_ge(s_b1p, 1)
            v.tensor_copy(w1_sb[:, :, HID:W1C], ps_a1[:, 0:E * HC].rearrange("p (e c) -> p e c", e=E)).then_inc(s_b1, 1)
            dve.wait_ge(s_pk, 1)
            dve.wait_ge(s_b1, 1)
            expert = tile_experts(dve, pk_w1, 0)
            ps_y = (ps_a3, ps_f)

            def body(k, j, q):
                a, o_ = q % 2, (q + 1) % 2
                ea = expert(k, j, q)
                z = tile(k, 4)
                if tile(k, 3):
                    t, d = k - 3, (q + 1) % NR
                    if not isinstance(k, int) or t >= NR:
                        dve.wait_ge(s_zadd[d], 16 * (t // NR if isinstance(k, int) else (j if q == 3 else j - 1)))
                    upto(dve, s_w2, 1, t)
                    upto(dve, s_xb, 1, t)
                    v.tensor_tensor(zb[:, d, :], xb[:, d, :], ps_y[o_][:, 0:D], ALU.add).then_inc(s_rz, 1)
                    v.tensor_copy(idx[:, d:d + 1], idf[:, d:d + 1]).then_inc(s_ix, 1)
                if tile(k, 0):
                    dve.wait_ge(s_xt[q], (j + 1) * 16)
                    v.tensor_copy(idf[:, q:q + 1], xt[:, q, D:D + 1])
                    v.tensor_tensor(xb[:, q, :], xt[:, q, 0:D], b2_bc[:, bass.ds(ea, 1), :].rearrange("p o n -> p (o n)"),
                                    ALU.add).then_inc(s_xb, 1)
                if tile(k, 3):
                    upto(dve, s_rz, 1, t)
                    v.bn_stats(st_m[:, :], zb[:, d, :]).then_inc(s_mc, 1)
                if z:
                    v.scalar_tensor_tensor(zb[:, q, :], zb[:, q, :], mv_m[:, a, 0:1], g2_bc[:, :], ALU.subtract, ALU.mult)\
                        .then_inc(s_mn, 1)
                if tile(k, 3):
                    upto(dve, s_mc, 3, t, 1)
                    v.memset(pause[:, 0:1], 0.0)
                    v.bn_aggr(mv_m[:, o_, :], st_m[:, :]).then_inc(s_mc, 1)
                if z:
                    upto(dve, s_mr, 1, k - 4)
                    upto(dve, s_mn, 1, k - 4)
                    v.scalar_tensor_tensor(zb[:, q, :], zb[:, q, :], rs_m[:, a:a + 1], beta2_bc[:, :], ALU.mult, ALU.add)\
                        .then_inc(s_z, 1)
                if tile(k, 3):
                    upto(dve, s_mc, 3, t, 2)
                    v.tensor_scalar(ve_m[:, o_:o_ + 1], mv_m[:, o_, 1:2], EPS, None, ALU.add).then_inc(s_mc, 1)

            tile_bodies(dve, body)

        @block.sync
        def _(sp):
            sp.dma_start(wtok_nat, tok_w).then_inc(s_ld[0], 16)
            sp.dma_start(pos_nat, tok_pos).then_inc(s_ld[1], 16)
            sp.dma_start(cls_col, tok_cls.rearrange("o n -> n o")).then_inc(s_ld[1], 16)
            sp.dma_start(b_tok[:, :], tok_b.rearrange("(n o) -> n o", o=1)).then_inc(s_ld[1], 16)
            load_pixels(sp, 0, 0, ((s_xzd, 1), (s_xzd, 2), (s_xz, 1), (s_xz, 2)))
            for nat, last, wd, bd_ in ((natq, lastq, f_wq, f_bq), (natk, lastk, f_wk, f_bk), (natv, lastv, f_wv, f_bv)):
                sp.dma_start(nat[0:D - 1, :], wd[0:D - 1, :]).then_inc(s_ld[5], 16)
                sp.dma_start(nat[D - 1:D, :], row(bd_, 1)).then_inc(s_ld[5], 16)
                sp.dma_start(last, wd[D - 1:D, :].broadcast_to([D, D])).then_inc(s_ld[5], 16)
            sp.dma_start(wo_sb[:, :], f_wo).then_inc(s_ld[6], 16)
            sp.dma_start(wg_sb[:, :], wg).then_inc(s_ld[6], 16)
            sp.dma_start(bo_bc[:, :], row(f_bo, S)).then_inc(s_ld[7], 16)
            sp.dma_start(g1_bc[:, :], row(g1, S)).then_inc(s_ld[7], 16)
            sp.dma_start(beta1_bc[:, :], row(beta1, S)).then_inc(s_ld[7], 16)
            sp.dma_start(bg_bc[:, :], row(bg, S)).then_inc(s_ld[7], 16)
            sp.dma_start(g2_bc[:, :], row(g2)).then_inc(s_ld[7], 16)
            sp.dma_start(beta2_bc[:, :], row(beta2)).then_inc(s_ld[7], 16)
            load_pixels(sp, 1, 1, tuple((s_xz, 3 + b) for b in range(GI)))
            sp.wait_ge(s_padt, 5)
            for k, dst in enumerate((blank_dram, xs_dram[NONE:NONE + E * T128, :])):
                first = B * S + k * E * T128
                sp.dma_start(dst.rearrange("(e p) n -> p e n", p=T128), blank[k]).then_inc(s_pads, 16)
                sp.dma_start(h_dram[first:first + E * T128, :].rearrange("(e p) n -> p e n", p=T128), blank[k][:, :, 0:D])\
                  .then_inc(s_pads, 16)

            def body(i, j, p):
                if on(i, 0) and (not isinstance(i, int) or i + 2 < G):
                    load_pixels(sp, i + 2, p)
                if on(i, 3):
                    g = i - 3
                    upto(sp, s_h2, 1, g)
                    dst = h_dram[bass.ds(g * R, R), :] if not isinstance(g, int) else h_dram[g * R:(g + 1) * R, :]
                    sp.dma_start(dst.rearrange("(b s) d -> s b d", s=S), h2[:, 1 - p, :, :]).then_inc(s_hst[1 - p], 16)

            bodies(sp, body, G - 2)
            upto(sp, s_tok, 1, G - 1)
            sp.dma_start(w1_sb[:, :, 0:HID], w1.rearrange("e c n -> c e n")).then_inc(s_moew, 16)
            sp.dma_start(w2_sb, w2.rearrange("e (c p) n -> p e c n", p=D)).then_inc(s_moew, 16)
            sp.dma_start(b1_nat, b1.rearrange("e (c n) -> (e c) n", c=HC)).then_inc(s_moew, 16)
            sp.dma_start(b2_bc, b2.rearrange("(o e) n -> o e n", o=1).broadcast_to([128, E, D])).then_inc(s_moew, 16)
            sp_tail(sp)

        @block.gpsimd
        def _(pool):
            nc.gpsimd.memset(ident[:, :], 0.0).then_inc(s_pool0, 1)
            pool.wait_ge(s_pool0, 1)
            nc.gpsimd.affine_select(out=ident[:, :], in_=ident[:, :], compare_op=ALU.not_equal, fill=1.0,
                                    base=0, pattern=[[-1, 128]], channel_multiplier=1).then_inc(s_pool0, 1)
            nc.gpsimd.memset(wv2, 0.0).then_inc(s_wv2, 1)
            for b in (2, 3):
                nc.gpsimd.memset(image_of(0, b), 0.0).then_inc(s_xz, 1)
            nc.gpsimd.memset(mhalf[:, :], -0.5).then_inc(s_pool0, 1)
            nc.gpsimd.memset(ones[:, :], 1.0).then_inc(s_pool0, 1)
            pool.wait_ge(s_pool0, 4)
            nc.gpsimd.affine_select(out=triu[:, :], in_=ones[0:S, 0:S], compare_op=ALU.is_ge, fill=0.0,
                                    base=0, pattern=[[1, S]], channel_multiplier=-1).then_inc(s_pool0, 1)
            nc.gpsimd.memset(head_mask[:, :], 1.0).then_inc(s_pool0, 1)
            pool.wait_ge(s_pool0, 6)
            nc.gpsimd.affine_select(out=head_mask[:, :], in_=head_mask[:, :], compare_op=ALU.is_ge, fill=0.0,
                                    base=0, pattern=[[-DH2, H]], channel_multiplier=1).then_inc(s_pool0, 1)
            pool.wait_ge(s_pool0, 7)
            nc.gpsimd.affine_select(out=head_mask[:, :], in_=head_mask[:, :], compare_op=ALU.is_ge, fill=0.0,
                                    base=DH2 - 1, pattern=[[DH2, H]], channel_multiplier=-1).then_inc(s_pool0, 1)
            nc.gpsimd.memset(bd[:, :, :], 0.0).then_inc(s_gapz, 1)
            nc.gpsimd.memset(osb[:, :, :], 0.0).then_inc(s_gapz, 1)
            io = dict(channel_multiplier=0, allow_small_or_imprecise_dtypes=True)
            nc.gpsimd.iota(wsc[:, :], [[-1, E]], base=E, **io).then_inc(s_iota, 1)
            nc.gpsimd.iota(room[:, :], [[REG, E]], base=-1, **io).then_inc(s_iota, 1)
            nc.gpsimd.iota(base[:, :], [[REG, E]], base=-1, **io).then_inc(s_iota, 1)
            nc.gpsimd.memset(te_f[:, :], 0.0).then_inc(s_iota, 1)
            for n in range(4):
                nc.gpsimd.memset(digit[:, n:n + 1], float(E ** n)).then_inc(s_iota, 1)
            nc.gpsimd.iota(thr[:, :], [[T128, NTH]], base=0, **io).then_inc(s_iota, 1)
            nc.gpsimd.iota(tix[:, :], [[T128, NT]], base=0, **io).then_inc(s_iota, 1)
            nc.gpsimd.iota(tixe[:, :], [[1, NT]], base=0, **io).then_inc(s_iota, 1)
            nc.gpsimd.memset(ts[:, :, :, :], 0.0).then_inc(s_padt, 1)
            for k in range(2):
                nc.gpsimd.memset(blank[k], 0.0).then_inc(s_padt, 1)
            pool.wait_ge(s_padt, 3)
            for p in range(2):
                nc.gpsimd.iota(ts[:, p, :, D:D + 1], [[S, GI], [0, 1]], base=(p - 2) * R, channel_multiplier=1,
                               allow_small_or_imprecise_dtypes=True).then_inc(s_iota, 1)
            for k in range(2):
                nc.gpsimd.iota(blank[k][:, :, D:D + 1], [[T128, E], [0, 1]], base=B * S + k * E * T128, channel_multiplier=1,
                               allow_small_or_imprecise_dtypes=True).then_inc(s_padt, 1)
            pool.wait_ge(s_pe0, TB)
            for b in range(GI):
                nc.gpsimd.memset(image_of(1, b), 0.0).then_inc(s_xz, 1)
            pool.wait_ge(s_pool0, 8)
            pool.wait_ge(s_iota, 13)
            pool.wait_ge(s_ld[7], 96)

            def rstd(name, s_chain, s_r, g):
                _, _, ve, rs = lnb[name]
                upto(pool, s_chain, 3, g)
                nc.gpsimd.tensor_tensor(rs[0:S, :], ve[0:S, :], mhalf[0:S, :], ALU.pow).then_inc(s_r, 1)

            def masked_k(g, u, p):
                b, hf = u // 2, u % 2
                upto(pool, s_s2p, UNITS, g, u - 1)
                kv = kT[:, p, b * S:(b + 1) * S].unsqueeze(1).broadcast_to([D, UH, S])
                mv = head_mask[:, hf * UH:(hf + 1) * UH].unsqueeze(2).broadcast_to([D, UH, S])
                nc.gpsimd.tensor_tensor(km[:, u % 2, :, :], kv, mv, ALU.mult).then_inc(s_km, 1)

            def body(i, j, p):
                g1, f1, f2, f3, f4 = i - 1, i - 4, i - 5, i - 6, i - 7
                A1, F1, F2, F3, F4 = (on(i, k) for k in (1, 4, 5, 6, 7))

                def masks(*units):
                    if F2:
                        for u in units:
                            masked_k(f2, u, 1 - p)

                if F2:
                    upto(pool, s_k, 1, f2)
                masks(0, 1)
                if F1:
                    rstd("f1", s_f1c, s_f1r, f1)
                if F3:
                    upto(pool, s_x2, 1, f3)
                    upto(pool, s_t, 1, f3 - 1)
                    nc.gpsimd.tensor_tensor(xr[:, :, :], part(x_all, f3, GI), bo_bc[:, :].unsqueeze(1).broadcast_to([S, GI, D]),
                                            ALU.add).then_inc(s_xr, 1)
                masks(2, 3)
                if A1:
                    rstd("a1", s_a1c, s_a1r, g1)
                masks(4)
                if F3:
                    rstd("f3", s_f3c, s_f3r, f3)
                masks(5)
                if F3:
                    upto(pool, s_tn, 1, f3)
                    nc.gpsimd.tensor_tensor(xr[:, :, :], xr[:, :, :], g1_bc[:, :].unsqueeze(1).broadcast_to([S, GI, D]),
                                            ALU.mult).then_inc(s_tg, 1)
                    upto(pool, s_tg, 1, f3)
                    upto(pool, s_tTp, 1, f3 - 2)
                    if not isinstance(f3, int) or f3 >= 2:
                        pool.wait_ge(s_scat[p], 16 * GI * ((f3 - 2) // 2 + 1 if isinstance(f3, int) else j - 3))
                    nc.gpsimd.tensor_tensor(ts[:, p, :, 0:D], xr[:, :, :], beta1_bc[:, :].unsqueeze(1).broadcast_to([S, GI, D]),
                                            ALU.add).then_inc(s_t, 1)
                masks(6, 7)
                if A1:
                    weights(g1, 0)
                if F4:
                    upto(pool, s_t, 1, f4)
                    upto(pool, s_id, 1, f4)
                    upto(pool, s_pos, 1, f4)
                    pool_pause(f4)
                    for b in range(GI):
                        pool.indirect_dma_start(xs_dram, bass.IndirectOffsetOnAxis(ap=pos_i[:, 1 - p, b:b + 1], axis=0),
                                                ts[:, 1 - p, b, :], None).then_inc(s_scat[1 - p], 16)
                if A1:
                    weights(g1, 1)

            def weights(g1, r):
                wv_ = w[:, 2 * r:2 * r + 2, :].rearrange("p b (h m) -> p (b h) m", m=M)
                upto(pool, s_wc, 2, g1, r + 1)
                nc.gpsimd.tensor_tensor(wv_, wv_, mx1[:, 2 * r * H:(2 * r + 2) * H].unsqueeze(2).broadcast_to([S, 2 * H, M]),
                                        ALU.mult).then_inc(s_w, 1)

            bodies(pool, body)
            pool_tail(pool)

        @block.tensor
        def _(pe):
            pe.wait_ge(s_pool0, 8)
            pe.wait_ge(s_dve0, DVE0["wpad"])
            wp = wpad.rearrange("p (s n) -> p s n", s=STEPS)
            for k in range(TB):
                if k >= 2:
                    pe.wait_ge(s_wt, k - 1)
                for q in range(4 * k, min(4 * k + 4, STEPS)):
                    last = nc.tensor.transpose(ps_a2[:, (q % 8) * 128:(q % 8) * 128 + 128], wp[:, q, :], ident[:, :])
                last.then_inc(s_pe0, 1)
            pe.wait_ge(s_ld[3], 64)
            nc.tensor.transpose(ps_a1[0:DH, 0:M], wsl_nat, ident[0:M, 0:M]).then_inc(s_pe0, 1)
            nc.tensor.matmul(ps_a1[0:DH, 128:128 + DH], wq_nat, wk_nat, start=True, stop=True).then_inc(s_pe0, 1)
            pe.wait_ge(s_ld[1], 48)
            nc.tensor.transpose(ps_a1[:, 192:192 + S], pos_nat, ident[0:S, 0:S]).then_inc(s_pe0, 1)
            def patch_products(i, p, slot, half):
                g = i
                if slot == 0 and half == 1:
                    upto(pe, s_hT, 1, g - 1)
                v = xbuf[p].rearrange("p (a n) -> p a n", n=PS)
                s0, n_, n0_ = sum(T_SLOT[:slot]), T_SLOT[slot], T_FIRST[slot]
                mm = None
                for s in range(s0, s0 + n0_) if half == 0 else range(s0 + n0_, s0 + n_):
                    if s % TAIL == 0:
                        upto(pe, s_tail, C, g, s // TAIL + 1)
                    mm = nc.tensor.matmul(ps_t[:, 0:GI * NPP], w_tok[:, s, :], v[:, :, s],
                                          start=(s == 0), stop=(s == STEPS - 1))
                if slot == 7 and half == 0:
                    mm.then_inc(s_tok, 1)

            def scores(g, u, pq):
                b = u // 2
                upto(pe, s_km, UNITS, g, u + 1)
                if u == 0:
                    upto(pe, s_q, 1, g)
                upto(pe, s_s2, UNITS, g, u)
                nc.tensor.matmul(ps_s[0:S, 0:UW], qT[:, pq, b * S:(b + 1) * S],
                                 km[:, u % 2, :, :].rearrange("p h s -> p (h s)"), start=True, stop=True)\
                    .then_inc(s_s2p, 1)

            def exp_transposes(g, u):
                upto(pe, s_e2, UNITS, g, u + 1)
                upto(pe, s_eT, UNITS, g, u)
                upto(pe, s_cx, UNITS, g, u)
                for h in range(UH):
                    mm = nc.tensor.transpose(ps_e[0:S, h * S:(h + 1) * S], e2[:, u % 2, h * S:(h + 1) * S], ident[0:S, 0:S])
                mm.then_inc(s_eTp, 1)

            def contexts(g, u, pq):
                b, hf = u // 2, u % 2
                upto(pe, s_eT, UNITS, g, u + 1)
                if u == 0:
                    upto(pe, s_v2, 1, g)
                c0 = 300 + (u % 2) * UH * VW
                for h in range(UH):
                    hd = hf * UH + h
                    mm = nc.tensor.matmul(ps_e[0:S, c0 + h * VW:c0 + (h + 1) * VW], eT[:, u % 2, h * S:(h + 1) * S],
                                          va[:, pq, b, hd * VW:(hd + 1) * VW], start=True, stop=True)
                mm.then_inc(s_cp, 1)

            def token_outputs(g, jc, pw):
                hh, jj = jc // 2, jc % 2
                if jc == 0:
                    upto(pe, s_osb, 2, g)
                    upto(pe, s_wT, 1, g)
                    upto(pe, s_h2, 1, g - 1)
                upto(pe, s_ox, 4, g, jc)
                for b in range(GI):
                    mm = nc.tensor.matmul(ps_a3[:, b * S:(b + 1) * S], osb[:, b * HH + hh, jj * 128:(jj + 1) * 128],
                                          wT[:, pw, b * HH + hh, :], start=True, stop=True)
                mm.then_inc(s_oxp, 1)

            def body(i, j, p):
                g1, g2, g3, f1, f2, f3, f4 = (i - k for k in range(1, 8))
                T, A1, A2, A3, F1, F2, F3, F4 = (on(i, k) for k in range(8))
                for slot in range(8):
                    gc_, uc, pc, C_ = (f3, 7, p, F3) if slot == 0 else (f2, slot - 1, 1 - p, F2)
                    if F2:
                        if slot == 5 and F4:
                            upto(pe, s_base, 1, f4)
                        scores(f2, slot, 1 - p)
                    if slot == 1 and A2:
                        upto(pe, s_wT, 1, g2)
                        for q in range(Q):
                            mm = nc.tensor.matmul(ps_a2[:, q * 128:(q + 1) * 128],
                                                  w[:, q // HH, (q % HH) * 128:(q % HH) * 128 + 128],
                                                  xn[:, q // HH, :], start=True, stop=True)
                        mm.then_inc(s_gp, 1)
                    if slot == 3 and F3:
                        upto(pe, s_cT, 1, f3)
                        for b in range(GI):
                            mm = nc.tensor.matmul(ps_f[0:S, b * D:(b + 1) * D], cxT[:, b * S:(b + 1) * S], wo_sb[:, :],
                                                  start=True, stop=True)
                        mm.then_inc(s_saP, 1)
                    if slot == 4:
                        if A3:
                            upto(pe, s_ox, 4, g3)
                            for jc in range(4):
                                mm = nc.tensor.matmul(ps_a3[:, 0:R], woutT[:, jc, :], oxT[:, jc, :],
                                                      start=(jc == 0), stop=(jc == 3))
                            mm.then_inc(s_oTp, 1)
                        if F1:
                            upto(pe, s_q, 1, f1)
                            nc.tensor.matmul(ps_f[:, 0:R], wk_aug[:, :], xaT[:, :], start=True, stop=True).then_inc(s_kp, 1)
                    if T:
                        patch_products(i, p, slot, 0)
                    if slot == 0 and A1:
                        upto(pe, s_hT, 1, g1)
                        upto(pe, s_sub1, 2, g1 - 1)
                        for b in range(GI):
                            mm = nc.tensor.transpose(ps_a1[0:S, b * D:(b + 1) * D], hT[:, b, :], ident[:, :])
                        mm.then_inc(s_hps, 1)
                    if C_:
                        exp_transposes(gc_, uc)
                    if slot == 0:
                        if T:
                            patch_products(i, p, slot, 1)
                        if A2:
                            upto(pe, s_w, 2, g2)
                            upto(pe, s_osb, 2, g2 - 1)
                            for q in range(Q):
                                c0 = (q // 4) * 512 + (q % 4) * S
                                mm = nc.tensor.transpose(ps_a2[:, c0:c0 + S],
                                                         w[:, q // HH, (q % HH) * 128:(q % HH) * 128 + 128], ident[0:S, 0:S])
                            mm.then_inc(s_wTp, 1)
                    if slot == 1:
                        if F1:
                            upto(pe, s_xa, 1, f1)
                            upto(pe, s_gt, 1, f3 - 1)
                            upto(pe, s_v2, 1, f1 - 1)
                            for b in range(GI):
                                mm = nc.tensor.transpose(ps_f[:, b * S:(b + 1) * S], xa[:, b, :], ident[0:S, 0:S])
                            mm.then_inc(s_xaTp, 1)
                    if slot == 2:
                        if A2:
                            upto(pe, s_gn, 1, g2)
                            for q in range(Q):
                                mm = nc.tensor.transpose(ps_a2[:, q * 128:(q + 1) * 128], gn[:, q, :], ident[:, :])
                            mm.then_inc(s_gTp, 1)
                        if A1:
                            upto(pe, s_xn, 1, g1)
                            for b in range(GI):
                                mm = nc.tensor.transpose(ps_a1[:, b * S:(b + 1) * S], xn[:, b, :], ident[0:S, 0:S])
                            mm.then_inc(s_xnTp, 1)
                        if F3:
                            upto(pe, s_cx, UNITS, f3)
                            if F1:
                                upto(pe, s_xaT, 1, f1)
                            else:
                                upto(pe, s_gt, 1, f3 - 1)
                            for b in range(GI):
                                mm = nc.tensor.transpose(ps_f[:, b * S:(b + 1) * S], cx[:, p, b, :], ident[0:S, 0:S])
                            mm.then_inc(s_cTp, 1)
                    if slot == 3:
                        if A1:
                            upto(pe, s_xnT, 1, g1)
                            for b in range(2):
                                mm = nc.tensor.matmul(ps_a1[0:S, b * 256:(b + 1) * 256], xnT[:, b * S:(b + 1) * S], w_log[:, :],
                                                      start=True, stop=True)
                            mm.then_inc(s_lg, 1)
                        if A2:
                            upto(pe, s_gT, 1, g2)
                            for h in range(H):
                                mm = nc.tensor.matmul(ps_a2[:, h * 128:(h + 1) * 128], w_stp[:, h, :],
                                                      gnT[:, :, h // 4, h % 4, :], start=True, stop=True)
                            mm.then_inc(s_stp, 1)
                        if F1:
                            upto(pe, s_xaT, 1, f1)
                            upto(pe, s_r3, 1, f3)
                            nc.tensor.matmul(ps_f[:, 0:R], wq_aug[:, :], xaT[:, :], start=True, stop=True).then_inc(s_qp, 1)
                    if slot == 4:
                        if A1:
                            upto(pe, s_sub1, 2, g1, 1)
                            for b in range(2):
                                mm = nc.tensor.matmul(ps_a1[0:S, b * 256:(b + 1) * 256], xnT[:, (b + 2) * S:(b + 3) * S], w_log[:, :],
                                                      start=True, stop=True)
                            mm.then_inc(s_lg, 1)
                        if A2:
                            upto(pe, s_stT, 1, g2)
                            upto(pe, s_pT, 1, g2)
                            for q in range(Q):
                                mm = nc.tensor.matmul(ps_a2[:, q * 128:(q + 1) * 128], pT[:, q * 128:(q + 1) * 128],
                                                      stT[:, q * 128:(q + 1) * 128], start=True, stop=True)
                            mm.then_inc(s_scp, 1)
                    if slot == 5:
                        if A3:
                            upto(pe, s_oTr, 1, g3)
                            for b in range(GI):
                                mm = nc.tensor.transpose(ps_a3[0:S, b * D:(b + 1) * D], oT[:, b * S:(b + 1) * S], ident[:, :])
                            mm.then_inc(s_hp2, 1)
                        if A2:
                            upto(pe, s_sc, 1, g2)
                        if F1:
                            upto(pe, s_k, 1, f1)
                            for b in range(GI):
                                mm = nc.tensor.matmul(ps_f[0:S, b * D:(b + 1) * D], xaT[:, b * S:(b + 1) * S], wv_aug[:, :],
                                                      start=True, stop=True)
                            mm.then_inc(s_vp2, 1)
                        if A2:
                            for q in range(Q):
                                mm = nc.tensor.transpose(ps_a2[:, q * DH:(q + 1) * DH], stT[:, q * 128:(q + 1) * 128],
                                                         ident[0:DH, 0:DH])
                            mm.then_inc(s_vp, 1)
                    if slot == 6 and F3:
                        upto(pe, s_t, 1, f3)
                        if F1:
                            upto(pe, s_v2, 1, f1)
                        for b in range(GI):
                            mm = nc.tensor.transpose(ps_f[:, b * S:(b + 1) * S], ts[:, p, b, 0:D], ident[0:S, 0:S])
                        mm.then_inc(s_tTp, 1)
                    if slot == 7:
                        if F3:
                            upto(pe, s_tT, 1, f3)
                            for b in range(GI):
                                mm = nc.tensor.matmul(ps_f[0:S, b * E:(b + 1) * E], tT[:, b * S:(b + 1) * S], wg_sb[:, :],
                                                      start=True, stop=True)
                            mm.then_inc(s_gtp, 1)
                        if A2:
                            upto(pe, s_bd, 1, g2)
                            upto(pe, s_v, 1, g2)
                            for q in range(Q):
                                mm = nc.tensor.matmul(ps_a2[:, 512 + q * DH:512 + (q + 1) * DH], bd[:, q, :], v_sb[:, q, :],
                                                      start=True, stop=True)
                            mm.then_inc(s_osp, 1)
                    if T and slot == 6:
                        patch_products(i, p, slot, 1)
                    if A3 and slot < 4:
                        token_outputs(g3, slot, 1 - p)
                    if C_:
                        contexts(gc_, uc, pc)
                    if F4 and slot == 3:
                        upto(pe, s_oh, 1, f4)
                        if F2:
                            upto(pe, s_s2, UNITS, f2, slot + 1)
                        upto(pe, s_base, 1, f4 - 1)
                        upto(pe, s_pos, 1, f4 - 1)
                        c0, c1 = RANK0, RANK0 + GI * E
                        nc.tensor.matmul(ps_s[0:S, c0:c1], triu[:, :], ohb[:, :, :].rearrange("p b e -> p (b e)"),
                                         start=True, stop=False)
                        for sh in range(1, GI):
                            nc.tensor.matmul(ps_s[0:S, c0 + sh * E:c1], ones[0:S, 0:S],
                                             ohb[:, 0:GI - sh, :].rearrange("p b e -> p (b e)"),
                                             start=False, stop=(sh == GI - 1))
                        for b in range(GI):
                            mm = nc.tensor.matmul(ps_s[0:S, c1:c1 + E], ones[0:S, 0:S], ohb[:, b, :],
                                                  start=(b == 0), stop=(b == GI - 1))
                        mm.then_inc(s_rp, 1)
                    if T and 0 < slot < 6:
                        patch_products(i, p, slot, 1)

            pe.wait_ge(s_wt, TB)
            body(0, 0, 0)
            pe.wait_ge(s_dve0, DVE0["wslT"])
            nc.tensor.matmul(ps_f[:, 0:H * M], e_last, bsl_row.rearrange("p a n -> p (a n)"), start=True, stop=False)
            for h in range(H):
                last = nc.tensor.matmul(ps_f[:, h * M:(h + 1) * M], wx_nat[:, h, :], wslT, start=False, stop=(h == H - 1))
            last.then_inc(s_pe0, 1)
            pe.wait_ge(s_dve0, DVE0["idA"])
            for h in range(H):
                last = nc.tensor.matmul(ps_a2[:, h * 128:(h + 1) * 128], wfx_nat[:, h, :], idA, start=True, stop=True)
            last.then_inc(s_pe0, 1)
            pe.wait_ge(s_ld[4], 48)
            wo4 = wout_nat.rearrange("p a (c n) -> p a c n", c=2)
            for k in range(4):
                last = nc.tensor.transpose(ps_a3[:, k * 128:(k + 1) * 128], wo4[:, k // 2, k % 2, :], ident[:, :])
            last.then_inc(s_pe0, 1)
            pe.wait_ge(s_dve0, DVE0["wlog"])
            body(1, 0, 1)
            pe.wait_ge(s_dve0, DVE0["wva"])
            pe.wait_ge(s_ldv, 32)
            nc.tensor.matmul(ps_a3[:, :], wv2, wout_raw, start=True, stop=True).then_inc(s_pe0, 1)
            body(2, 1, 0)
            pe.wait_ge(s_dve0, DVE0["wvo"])
            pe.wait_ge(s_ld[6], 32)
            bodies(pe, body, start=3)
            pe_tail(pe)

        @block.scalar
        def _(act):
            act.dma_start(wx_nat, wx.rearrange("(h d) c -> d h c", d=DH)).then_inc(s_ld[2], 16)
            act.dma_start(wfx_nat, wfx.rearrange("(h d) c -> d h c", d=DH)).then_inc(s_ld[2], 16)
            act.dma_start(bx_nat, bx.rearrange("(h d) -> d h", d=DH), allow_slow_non_contiguous=True).then_inc(s_ld[2], 16)
            act.dma_start(bfx_nat, bfx.rearrange("(h d) -> d h", d=DH), allow_slow_non_contiguous=True).then_inc(s_ld[2], 16)
            act.dma_start(wq_nat, wq).then_inc(s_ld[3], 16)
            act.dma_start(wk_nat, wk).then_inc(s_ld[3], 16)
            act.dma_start(wsl_nat, wslice).then_inc(s_ld[3], 16)
            act.wait_ge(s_wv2, 1)
            for k in range(2):
                act.dma_start(wv2[k * DH:(k + 1) * DH, k * DH:(k + 1) * DH], wv).then_inc(s_ldv, 16)
            act.dma_start(bsl_row.rearrange("p a (h m) -> p (a h) m", m=M),
                         bslice.rearrange("(o n) -> o n", o=1).unsqueeze(1).broadcast_to([1, H, M]))\
              .then_inc(s_ld[3], 16)
            act.dma_start(wout_nat, wout.rearrange("p (a n) -> p a n", a=2)).then_inc(s_ld[4], 16)
            act.dma_start(bout_col[:, :], bout.rearrange("(n o) -> n o", o=1)).then_inc(s_ld[4], 16)
            act.dma_start(temp_bc, row(temp.rearrange("a h b c -> (a h b c)"))).then_inc(s_ld[4], 16)
            act.preload_act_table(ACT.Exp)
            def pixel_tail(n, p, c):
                if c == 0:
                    act.wait_ge(s_x[p], n * 16 * C * GI)
                px = xbuf[p].rearrange("p (a n) -> p a n", n=PS)
                copy(px[96:96 + PS, :, c * TAIL:(c + 1) * TAIL], px[32 * c:32 * c + PS, :, STEPS:PS], s_tail)

            def copy(dst, src, s):
                nc.scalar.activation(dst, src, ACT.Copy).then_inc(s, 1)

            pixel_tail(1, 0, 0)

            def body(i, j, p):
                g1, g2, g3, f1, f2, f3 = (i - k for k in range(1, 7))
                T, A1, A2, A3, F1, F2, F3 = (on(i, k) for k in range(7))
                if isinstance(i, int) and i == 1:
                    act.wait_ge(s_pe0, TB + PE0["wout"])
                if isinstance(i, int) and i == 3:
                    act.wait_ge(s_dve0, DVE0["wva"])
                if isinstance(i, int) and i == 7:
                    act.wait_ge(s_pads, 64)
                for slot in range(8):
                    gc_, uc, C_ = (f3, 7, F3) if slot == 0 else (f2, slot - 1, F2)
                    if C_:
                        upto(act, s_eTp, UNITS, gc_, uc + 1)
                        upto(act, s_cp, UNITS, gc_, uc - 1)
                        copy(eT[:, uc % 2, :], ps_e[0:S, 0:UW], s_eT)
                    if slot == 0:
                        if A1:
                            upto(act, s_hT, 1, g1)
                            copy(part(hT_all, g1, 1), hT[:, :, :].rearrange("p b s -> p (b s)").unsqueeze(1), s_hTc)
                        if A2:
                            upto(act, s_wTp, 1, g2)
                            upto(act, s_oxp, 4, g2 - 2)
                            copy(wT[:, p, :, :].rearrange("p (a q) s -> p a (q s)", a=2),
                                 ps_a2[:, :].rearrange("p (a n) -> p a n", a=2)[:, :, 0:4 * S], s_wT)
                    if F2:
                        upto(act, s_s2, UNITS, f2, slot + 1)
                        nc.scalar.activation(e2[:, slot % 2, :], e2[:, slot % 2, :], ACT.Exp).then_inc(s_e2, 1)
                    if slot == 0:
                        if F1:
                            upto(act, s_x2, 1, f1)
                            upto(act, s_xaTp, 1, f1 - 1)
                            copy(xa[:, :, 0:D - 1], part(x_all, f1, GI)[:, :, 0:D - 1], s_xa)
                    if slot == 1 and F1:
                        upto(act, s_xaTp, 1, f1)
                        upto(act, s_vp2, 1, f1 - 1)
                        copy(xaT[:, :], ps_f[:, 0:R], s_xaT)
                    if slot == 2:
                        if A2:
                            upto(act, s_gTp, 1, g2)
                            copy(gn[:, :, :].rearrange("p q n -> p (q n)"), ps_a2[:, :], s_gT)
                        if A1:
                            upto(act, s_xnTp, 1, g1)
                            upto(act, s_lg, 2, g1 - 1)
                            copy(xnT[:, :], ps_a1[:, 0:R], s_xnT)
                        if F3:
                            upto(act, s_cTp, 1, f3)
                            upto(act, s_saP, 1, f3 - 1)
                            copy(cxT[:, :], ps_f[:, 0:R], s_cT)
                    if slot == 3:
                        if A2:
                            upto(act, s_stp, 1, g2)
                            copy(stT.rearrange("p (b h m) -> p h b m", b=GI, h=H),
                                 ps_a2[0:DH, :].rearrange("p (h b m) -> p h b m", b=GI, h=H), s_stT)
                            copy(pT[:, :].rearrange("p (b h m) -> p h b m", b=GI, h=H),
                                 ps_a2[DH:2 * DH, :].rearrange("p (h b m) -> p h b m", b=GI, h=H), s_pT)
                        if F1:
                            upto(act, s_qp, 1, f1)
                            upto(act, s_s2p, UNITS, f1 - 2)
                            copy(qT[:, p, :], ps_f[:, 0:R], s_q)
                    if slot == 4:
                        if F1:
                            upto(act, s_kp, 1, f1)
                            upto(act, s_km, UNITS, f1 - 2)
                            copy(kT[:, p, :], ps_f[:, 0:R], s_k)
                        if A3:
                            upto(act, s_oTp, 1, g3)
                            upto(act, s_hp2, 1, g3 - 1)
                            nc.scalar.activation(oT[:, :], ps_a3[:, 0:R], ACT.Identity, bias=bout_col[:, :]).then_inc(s_oT, 1)
                        if A1:
                            upto(act, s_sub1, 2, g1, 1)
                            nc.scalar.activation(w[:, 0:2, :], w[:, 0:2, :], ACT.Exp).then_inc(s_exp1, 1)
                        if A2:
                            upto(act, s_scp, 1, g2)
                            gp = ps_a2[:, :].rearrange("p (q n) -> p q n", q=Q)
                            for hl in range(4):
                                a = nc.scalar.activation(sc[32 * hl:32 * hl + 32, :, :],
                                                         gp[32 * hl:32 * hl + 32, :, 32 * hl:32 * hl + 32], ACT.Copy)
                            a.then_inc(s_sc, 1)
                    if slot == 5:
                        if A2:
                            upto(act, s_asub, 1, g2)
                            nc.scalar.activation(sc[:, :, :], sc[:, :, :], ACT.Exp).then_inc(s_aexp, 1)
                            upto(act, s_vp, 1, g2)
                            upto(act, s_osp, 1, g2 - 1)
                            copy(v_sb[:, :, :].rearrange("p q n -> p (q n)"), ps_a2[:, 0:Q * DH], s_v)
                        if A1:
                            upto(act, s_sub1, 2, g1)
                            nc.scalar.activation(w[:, 2:4, :], w[:, 2:4, :], ACT.Exp).then_inc(s_exp1, 1)
                        if F1:
                            upto(act, s_vp2, 1, f1)
                            upto(act, s_cp, UNITS, f1 - 2)
                            copy(va[:, p, :, :].rearrange("p b (h n) -> p (b h) n", n=VW)[:, :, 0:DH2],
                                 ps_f[0:S, :].rearrange("p (a n) -> p a n", n=DH2), s_v2)
                    if slot == 6:
                        if A3:
                            upto(act, s_hp2, 1, g3)
                            upto(act, s_x2, 1, g3 - 2)
                            if not isinstance(g3, int) or g3 >= 2:
                                act.wait_ge(s_hst[1 - p], 16 * ((g3 - 2) // 2 + 1 if isinstance(g3, int) else j - 2 + p))
                            copy(h2[:, 1 - p, :, :], ps_a3[0:S, :].rearrange("p (b n) -> p b n", b=GI), s_h2)
                        if F3:
                            upto(act, s_tTp, 1, f3)
                            upto(act, s_gtp, 1, f3 - 1)
                            copy(tT[:, :], ps_f[:, 0:R], s_tT)
                    if slot == 7 and A2:
                        upto(act, s_osp, 1, g2)
                        upto(act, s_oxp, 4, g2 - 1)
                        for hl in (0, 1):
                            a = nc.scalar.activation(osb[32 * hl:32 * hl + 32, :, hl * DH:(hl + 1) * DH],
                                                     ps_a2[32 * hl:32 * hl + 32, 512:1024].rearrange("p (q n) -> p q n", q=Q),
                                                     ACT.Copy)
                        a.then_inc(s_osb, 1)
                    if slot == 6 and T and (not isinstance(i, int) or i + 1 < G):
                        pixel_tail((i + 1) // 2 + 1 if isinstance(i, int) else j + p + 1, 1 - p, 0)
                    if A3 and slot < 4:
                        upto(act, s_oxp, 4, g3, slot + 1)
                        upto(act, s_oTp, 1, g3 - 1)
                        copy(oxT[:, slot, :], ps_a3[:, 0:R], s_ox)
                    if slot in (1, 3) and T:
                        pixel_tail(i // 2 + 1 if isinstance(i, int) else j + 1, p, (slot + 1) // 2)

            act.wait_ge(s_gapz, 2)
            bodies(act, body, G - 2)
            act_tail(act)

        @block.vector
        def _(dve):
            v = nc.vector
            n0 = [0]

            def step(ins, name=None):
                n0[0] += 1
                if name is not None:
                    assert DVE0[name] == n0[0], (name, n0[0])
                ins.then_inc(s_dve0, 1)
                dve.wait_ge(s_dve0, n0[0])

            wp = wpad.rearrange("p (s n) -> p s n", s=STEPS)
            step(v.memset(wpad.rearrange("p (s c n) -> p s c n", s=STEPS, c=4)[:, :, :, PS:32], 0.0), "pad_zero")
            for b in (0, 1):
                v.memset(image_of(0, b), 0.0).then_inc(s_xzd, 1)
            dve.wait_ge(s_ld[0], 16)
            wn = wtok_nat.rearrange("p (c y x) -> p c y x", c=C, y=PS)
            for c in range(C):
                v.tensor_copy(wp[:, :, 32 * c:32 * c + PS], wn[:, c, :, 0:STEPS].rearrange("p y x -> p x y"))
                last = v.tensor_copy(wp[:, c * TAIL:(c + 1) * TAIL, 96:96 + PS],
                                     wn[:, c, :, STEPS:PS].rearrange("p y x -> p x y"))
            step(last, "wpad")
            wt4 = w_tok[:, :, :].rearrange("p s n -> p (s n)")
            for k in range(TB):
                dve.wait_ge(s_pe0, k + 1)
                n = min(4, STEPS - 4 * k) * 128
                v.tensor_copy(wt4[:, 512 * k:512 * k + n], ps_a2[:, (k % 2) * 512:(k % 2) * 512 + n]).then_inc(s_wt, 1)
            step(v.memset(xn[:, :, D - 1:D], 1.0), "aug1")
            step(v.memset(xa[:, :, D - 1:D], 1.0), "aug2")
            step(v.memset(va[:, :, :, :].rearrange("p a b n -> p (a b n)"), 1.0), "aug3")
            dve.wait_ge(s_ld[2], 64)
            for nat, bias, n1, n2 in ((wx_nat, bx_nat, "wx1", "wx2"), (wfx_nat, bfx_nat, "wfx1", "wfx2")):
                step(v.tensor_tensor(nat[:, :, 0:D - 1], nat[:, :, 0:D - 1],
                                     nat[:, :, D - 1:D].broadcast_to([DH, H, D - 1]), ALU.subtract), n1)
                step(v.tensor_copy(nat[:, :, D - 1:D], bias.unsqueeze(2)), n2)
            dve.wait_ge(s_pool0, 8)
            v.memset(e_last[:, 0:D - 1], 0.0)
            v.memset(e_last[:, D - 1:D], 1.0)
            dve.wait_ge(s_pe0, TB + PE0["pos"])
            v.tensor_copy(idA[:, 0:DH], ident[0:DH, 0:DH])
            step(v.tensor_copy(wslT, ps_a1[0:DH, 0:M]), "wslT")
            step(v.tensor_scalar(idA[:, DH:2 * DH], ps_a1[0:DH, 128:128 + DH], float(DH) ** -0.5, None, ALU.mult), "idA")
            step(v.tensor_copy(posT[:, :], ps_a1[:, 192:192 + S]), "pos")
            dve.wait_ge(s_ld[1], 48)
            step(v.tensor_scalar(hT[:, :, 0:1], posT[:, 0:1].unsqueeze(1).broadcast_to([D, GI, 1]), cls_col, None, ALU.mult), "cls")
            dve.wait_ge(s_ld[4], 48)
            step(v.reciprocal(itemp, temp_bc), "itemp")
            dve.wait_ge(s_gapz, 2)
            v.memset(zeros[:, :], 0.0)
            dve.wait_ge(s_ld[7], 96)
            dve.wait_ge(s_iota, 13)

            def norm_sums(name, src, s_chain, g):
                st = lnb[name][0]
                for b in range(GI):
                    ins = v.bn_stats(st[0:S, b, :], src[:, b, :])
                ins.then_inc(s_chain, 1)

            def norm_moments(name, s_chain, g):
                st, mv, ve, _ = lnb[name]
                upto(dve, s_chain, 3, g, 1)
                v.memset(pause[0:S, 0:1], 0.0)
                for b in range(GI):
                    ins = v.bn_aggr(mv[0:S, b, :], st[0:S, b, :])
                ins.then_inc(s_chain, 1)
                upto(dve, s_chain, 3, g, 2)
                v.tensor_scalar(ve[0:S, :].unsqueeze(2), mv[0:S, :, 1:2], EPS, None, ALU.add).then_inc(s_chain, 1)

            def norm_stats(name, src, s_chain, g):
                norm_sums(name, src, s_chain, g)
                norm_moments(name, s_chain, g)

            def norm_apply(name, dst, src, cols, s_r, s_done, g):
                _, mv, _, rs = lnb[name]
                upto(dve, s_r, 1, g)
                for b in range(GI):
                    ins = v.tensor_scalar(dst(b), src[:, b, 0:cols], mv[0:S, b, 0:1], rs[0:S, b:b + 1],
                                          ALU.subtract, ALU.mult)
                ins.then_inc(s_done, 1)

            def body(i, j, p):
                g1, g2, g3, f1, f2, f3, f4 = (i - k for k in range(1, 8))
                T, A1, A2, A3, F1, F2, F3, F4 = (on(i, k) for k in range(8))
                psh = ps_a1[0:S, :].rearrange("p (b n) -> p b n", b=GI)
                for slot in range(8):
                    gc_, uc, C_ = (f3, 7, F3) if slot == 0 else (f2, slot - 1, F2)
                    if slot == 5 and A3:
                        upto(dve, s_oT, 1, g3)
                        upto(dve, s_hTc, 1, g3)
                        v.tensor_tensor(oT[:, :], oT[:, :], part(hT_all, g3, 1).rearrange("p o n -> p (o n)"), ALU.add)\
                            .then_inc(s_oTr, 1)
                    if F2:
                        sv = ps_s[0:S, 0:UW].rearrange("p (h n) -> p h n", h=UH)
                        upto(dve, s_s2p, UNITS, f2, slot + 1)
                        v.tensor_reduce(mx2[:, slot % 2, :], sv, AX, ALU.max).then_inc(s_s2m, 1)
                        upto(dve, s_s2m, UNITS, f2, slot + 1)
                        upto(dve, s_eTp, UNITS, f2, slot - 1)
                        v.tensor_tensor(e2[:, slot % 2, :].rearrange("p (h n) -> p h n", h=UH), sv,
                                        mx2[:, slot % 2, :].unsqueeze(2).broadcast_to([S, UH, S]), ALU.subtract)\
                            .then_inc(s_s2, 1)
                    if slot == 7:
                        if T:
                            upto(dve, s_tok, 1, i)
                            upto(dve, s_hps, 1, g1)
                            upto(dve, s_hTc, 1, g1)
                            v.scalar_tensor_tensor(hT[:, :, 1:S], ps_t[:, 0:GI * NPP].rearrange("p (b n) -> p b n", b=GI),
                                                   b_tok[:, :], posT[:, 1:S].unsqueeze(1).broadcast_to([D, GI, NPP]),
                                                   ALU.add, ALU.mult).then_inc(s_hT, 1)
                        if on(i, 3):
                            upto(dve, s_h2, 1, g3)
                            norm_sums("f1", h2[:, 1 - p, :, :], s_f1c, g3)
                    if slot == 0:
                        if F1:
                            norm_apply("f1", lambda b: part(x_all, f1 * GI + b, 1).rearrange("p o n -> p (o n)"),
                                       h2[:, p, :, :], D, s_f1r, s_x2, f1)
                    if slot == 1:
                        if A2:
                            gp = ps_a2[:, :].rearrange("p (q n) -> p q n", q=Q)
                            upto(dve, s_gp, 1, g2)
                            v.tensor_scalar(rn[:, :].unsqueeze(2), gp[:, :, D - 1:D], EPS, None, ALU.add).then_inc(s_gc, 1)
                            upto(dve, s_gc, 2, g2, 1)
                            v.reciprocal(rn[:, :], rn[:, :]).then_inc(s_gc, 1)
                            upto(dve, s_gc, 2, g2)
                            upto(dve, s_vp, 1, g2 - 1)
                            v.tensor_tensor(gn[:, :, :], gp, rn[:, :].unsqueeze(2).broadcast_to([128, Q, 128]),
                                            ALU.mult).then_inc(s_gn, 1)
                    if slot == 2:
                        if F4:
                            upto(dve, s_gt, 1, f4)
                            v.tensor_reduce(rmx[:, 0, :], glb[:, :, :], AX, ALU.max).then_inc(s_oc, 1)
                            upto(dve, s_oc, 4, f4, 1)
                            v.tensor_tensor(eqb[:, :, :], glb[:, :, :], rmx[:, 0, :].unsqueeze(2).broadcast_to([S, GI, E]),
                                            ALU.is_equal).then_inc(s_oc, 1)
                            upto(dve, s_oc, 4, f4, 2)
                            v.tensor_tensor(eqb[:, :, :], eqb[:, :, :], wsc[:, :].unsqueeze(1).broadcast_to([S, GI, E]),
                                            ALU.mult).then_inc(s_oc, 1)
                            upto(dve, s_oc, 4, f4, 3)
                            v.tensor_reduce(rmx[:, 1, :], eqb[:, :, :], AX, ALU.max).then_inc(s_oc, 1)
                            upto(dve, s_oc, 4, f4)
                            upto(dve, s_rp, 1, f4 - 1)
                            v.tensor_tensor(ohb[:, :, :], eqb[:, :, :], rmx[:, 1, :].unsqueeze(2).broadcast_to([S, GI, E]),
                                            ALU.is_equal).then_inc(s_oh, 1)
                    if slot == 3:
                        if F3:
                            upto(dve, s_saP, 1, f3)
                            upto(dve, s_xr, 1, f3)
                            v.tensor_tensor(xr[:, :, :], ps_f[0:S, :].rearrange("p (b n) -> p b n", b=GI), xr[:, :, :],
                                            ALU.add).then_inc(s_r3, 1)
                            upto(dve, s_r3, 1, f3)
                            norm_stats("f3", xr[:, :, :], s_f3c, f3)
                        if A1:
                            self_max(dve, v, g1, 0)
                    if slot == 4:
                        if F4:
                            c0, c1 = RANK0, RANK0 + GI * E
                            upto(dve, s_rp, 1, f4)
                            upto(dve, s_base, 1, f4 - 1)
                            v.tensor_tensor(rkb[:, :, :], ps_s[0:S, c0:c1].rearrange("p (b e) -> p b e", e=E),
                                            base[:, :].unsqueeze(1).broadcast_to([S, GI, E]), ALU.add).then_inc(s_rkc, 1)
                            upto(dve, s_rkc, 3, f4, 1)
                            v.tensor_tensor(base[:, :], base[:, :], ps_s[0:S, c1:c1 + E], ALU.add).then_inc(s_base, 1)
                            v.tensor_tensor(rkb[:, :, :], rkb[:, :, :], ohb[:, :, :], ALU.mult).then_inc(s_rkc, 1)
                            upto(dve, s_rkc, 3, f4, 2)
                            v.tensor_reduce(pos_f[:, :], rkb[:, :, :], AX, ALU.add).then_inc(s_rkc, 1)
                            upto(dve, s_rkc, 3, f4)
                            v.tensor_copy(pos_i[:, 1 - p, :], pos_f[:, :]).then_inc(s_pos, 1)
                        if F3:
                            norm_apply("f3", lambda b: xr[:, b, :], xr[:, :, :], D, s_f3r, s_tn, f3)
                    if slot == 5:
                        if A2:
                            upto(dve, s_sc, 1, g2)
                            v.tensor_reduce(smx[:, :], sc[:, :, :], AX, ALU.max).then_inc(s_ac, 1)
                            upto(dve, s_ac, 4, g2, 1)
                            v.tensor_tensor(sc[:, :, :], sc[:, :, :], smx[:, :].unsqueeze(2).broadcast_to([128, Q, M]),
                                            ALU.subtract).then_inc(s_asub, 1)
                        if A1:
                            self_max(dve, v, g1, 1)
                            weight_sums(g1, 0)
                        if F3:
                            if not isinstance(f3, int) or f3 >= 2:
                                dve.wait_ge(s_scat[p], 16 * GI * ((f3 - 2) // 2 + 1 if isinstance(f3, int) else j - 3))
                            tid = ts[:, p, :, D:D + 1]
                            v.tensor_scalar(tid, tid, float(2 * R), None, ALU.add).then_inc(s_id, 1)
                    if slot == 6 and A2:
                        upto(dve, s_aexp, 1, g2)
                        v.tensor_reduce(smx[:, :], sc[:, :, :], AX, ALU.add).then_inc(s_ac, 1)
                        upto(dve, s_ac, 4, g2, 2)
                        v.reciprocal(smx[:, :], smx[:, :]).then_inc(s_ac, 1)
                        upto(dve, s_ac, 4, g2, 3)
                        v.tensor_tensor(sc[:, :, :], sc[:, :, :], smx[:, :].unsqueeze(2).broadcast_to([128, Q, M]),
                                        ALU.mult).then_inc(s_ac, 1)
                        upto(dve, s_ac, 4, g2)
                        upto(dve, s_osp, 1, g2 - 1)
                        for hl in range(4):
                            ins = v.transpose(bd[32 * hl:32 * hl + 32, :, 32 * hl:32 * hl + 32], sc[32 * hl:32 * hl + 32, :, :])
                        ins.then_inc(s_bd, 1)
                    if C_:
                        c0 = 300 + (uc % 2) * UH * VW
                        cv = ps_e[0:S, c0:c0 + UH * VW].rearrange("p (h n) -> p h n", h=UH)
                        upto(dve, s_cp, UNITS, gc_, uc + 1)
                        v.reciprocal(rcx[:, uc % 2, :].unsqueeze(2), cv[:, :, DH2:VW]).then_inc(s_cr, 1)
                        upto(dve, s_cr, UNITS, gc_, uc + 1)
                        if uc == 0:
                            upto(dve, s_cTp, 1, gc_ - 2)
                        b, hf = uc // 2, uc % 2
                        v.tensor_tensor(cx[:, p if slot == 0 else 1 - p, b, hf * UH * DH2:(hf + 1) * UH * DH2].rearrange("p (h n) -> p h n", h=UH),
                                        cv[:, :, 0:DH2], rcx[:, uc % 2, :].unsqueeze(2).broadcast_to([S, UH, DH2]), ALU.mult)\
                            .then_inc(s_cx, 1)
                    if slot == 0 and A1:
                        upto(dve, s_hps, 1, g1)
                        norm_stats("a1", psh, s_a1c, g1)
                    if slot == 1 and A1:
                        upto(dve, s_gp, 1, g2)
                        norm_apply("a1", lambda b: xn[:, b, 0:D - 1], psh, D - 1, s_a1r, s_xn, g1)
                    if slot == 6:
                        if A1:
                            weight_sums(g1, 1)
                    if slot == 7:
                        if A2:
                            upto(dve, s_osp, 1, g2)
                            upto(dve, s_oxp, 4, g2 - 1)
                            for hl in (2, 3):
                                ins = v.tensor_copy(osb[32 * hl:32 * hl + 32, :, hl * DH:(hl + 1) * DH],
                                                    ps_a2[32 * hl:32 * hl + 32, 512:1024].rearrange("p (q n) -> p q n", q=Q))
                            ins.then_inc(s_osb, 1)
                        if on(i, 3):
                            norm_moments("f1", s_f1c, g3)
                        if F3:
                            upto(dve, s_gtp, 1, f3)
                            v.tensor_tensor(glb[:, :, :], ps_f[0:S, 0:GI * E].rearrange("p (b n) -> p b n", b=GI),
                                            bg_bc[:, :].unsqueeze(1).broadcast_to([S, GI, E]), ALU.add).then_inc(s_gt, 1)
            def weight_sums(g1, r):
                m = mx1[:, 2 * r * H:(2 * r + 2) * H]
                upto(dve, s_exp1, 2, g1, r + 1)
                v.tensor_reduce(m, w[:, 2 * r:2 * r + 2, :].rearrange("p b (h m) -> p (b h) m", m=M), AX, ALU.add).then_inc(s_ws, 1)
                upto(dve, s_ws, 2, g1, r + 1)
                v.reciprocal(m, m).then_inc(s_wc, 1)

            def self_max(dve, v, g1, r):
                lv = ps_a1[0:S, :].rearrange("p (a m) -> p a m", m=M)
                upto(dve, s_lg, 2, g1, r + 1)
                v.tensor_reduce(mx1[:, 2 * r * H:(2 * r + 2) * H], lv, AX, ALU.max).then_inc(s_mx1, 1)
                upto(dve, s_mx1, 2, g1, r + 1)
                upto(dve, s_gp, 1, g1 - 1)
                v.tensor_tensor(w[:, 2 * r:2 * r + 2, :].rearrange("p b (h m) -> p (b h) m", m=M), lv,
                                mx1[:, 2 * r * H:(2 * r + 2) * H].unsqueeze(2).broadcast_to([S, 2 * H, M]), ALU.subtract)\
                    .then_inc(s_sub1, 1)

            body(0, 0, 0)
            dve.wait_ge(s_pe0, TB + PE0["wlog"])
            step(v.tensor_tensor(w_log[:, :].rearrange("p (h m) -> p h m", h=H),
                                 ps_f[:, 0:H * M].rearrange("p (h m) -> p h m", h=H),
                                 itemp.unsqueeze(2).broadcast_to([D, H, M]), ALU.mult), "wlog")
            dve.wait_ge(s_pe0, TB + PE0["wstp"])
            step(v.tensor_copy(w_stp[:, :, :].rearrange("p h n -> p (h n)"), ps_a2[:, :]), "wstp")
            dve.wait_ge(s_pe0, TB + PE0["wout"])
            step(v.tensor_copy(wout_raw, ps_a3[:, :]), "wout")
            dve.wait_ge(s_ld[5], 9 * 16)
            step(v.tensor_scalar(neg_keep, ident[:, D - 1:D], -1.0, None, ALU.add), "negk")
            step(v.scalar_tensor_tensor(wq_aug[:, :], lastq, neg_keep, natq, ALU.mult, ALU.add), "wqa")
            step(v.tensor_scalar(wq_aug[:, :], wq_aug[:, :], float(DH2) ** -0.5, None, ALU.mult), "wqs")
            step(v.scalar_tensor_tensor(wk_aug[:, :], lastk, neg_keep, natk, ALU.mult, ALU.add), "wka")
            step(v.scalar_tensor_tensor(wv_aug[:, :], lastv, neg_keep, natv, ALU.mult, ALU.add), "wva")
            body(1, 0, 1)
            dve.wait_ge(s_pe0, TB + PE0["wvo"])
            step(v.tensor_copy(woutT[:, :, :].rearrange("p h n -> p (h n)"), ps_a3[:, :]), "wvo")
            bodies(dve, body, start=2)
            dve_tail(dve)



_INS = ['x', 'L0_tok_W', 'L0_tok_b', 'L0_tok_class_token', 'L0_tok_pos_embed',
        'L0_attn_Wx', 'L0_attn_bx', 'L0_attn_Wfx', 'L0_attn_bfx', 'L0_attn_Wslice', 'L0_attn_bslice',
        'L0_attn_Wq', 'L0_attn_Wk', 'L0_attn_Wv', 'L0_attn_Wout', 'L0_attn_bout', 'L0_attn_temperature',
        'L0_ffn_Wq', 'L0_ffn_bq', 'L0_ffn_Wk', 'L0_ffn_bk', 'L0_ffn_Wv', 'L0_ffn_bv', 'L0_ffn_Wo', 'L0_ffn_bo',
        'L0_ffn_g1', 'L0_ffn_beta1', 'L0_ffn_g2', 'L0_ffn_beta2', 'L0_ffn_Wg', 'L0_ffn_bg',
        'L0_ffn_W1', 'L0_ffn_b1', 'L0_ffn_W2', 'L0_ffn_b2']
_OUTS = [((64, 65, 128), 'float32')]


def kernel(**inputs):
    import numpy as _np
    import concourse.bacc as _bacc
    from concourse import mybir as _mybir
    from concourse.bass_utils import run_bass_kernel_spmd as _run

    nc = _bacc.Bacc("TRN2", target_bir_lowering=False, num_devices=1)
    arrays, args = {}, []
    for name in _INS:
        a = _np.ascontiguousarray(inputs[name])
        arrays[f"in_{name}"] = a
        args.append(nc.dram_tensor(f"in_{name}", a.shape, _mybir.dt.from_np(a.dtype), kind="ExternalInput").ap())
    for i, (shape, dtype) in enumerate(_OUTS):
        dt = _mybir.dt.from_np(_np.dtype(dtype))
        args.append(nc.dram_tensor(f"out_{i}", shape, dt, kind="ExternalOutput").ap())
    vit_tower_kernel(nc, *args)
    r = _run(nc, [arrays], core_ids=[0])
    return r.results[0]["out_0"]
```
